# Optimizing a Trainium2 kernel written in Bass

```python
import numpy as np
import jax
import jax.numpy as jnp

def _softmax(x, axis=-1):
    return jax.nn.softmax(x, axis=axis)

def _gelu(x):
    return jax.nn.gelu(x, approximate=True)

def _silu(x):
    return jax.nn.silu(x)

def _sigmoid(x):
    return jax.nn.sigmoid(x)

def _layernorm(x, axis=-1, eps=1e-05):
    m = jnp.mean(x, axis=axis, keepdims=True)
    v = jnp.var(x, axis=axis, keepdims=True)
    return (x - m) / jnp.sqrt(v + eps)

def _scatter_add(tgt, idx, src, axis=0):
    return tgt.at[idx].add(src)

def _segment_sum(src, seg, n):
    return jax.ops.segment_sum(src, seg, n)
kernel_name = 'mk_adj_ffn_d2_adj_r2_4d3652'

def setup_inputs(seed: int=0):
    np.random.seed(seed)
    _w = jnp.asarray

    def _rec_inputs():
        import jax
        import jax.numpy as jnp
        _gk = jax.random.key(seed)
        x = -9.29e-06 + 0.01 * jax.random.normal(jax.random.fold_in(_gk, 1), (8192, 128), jnp.float32)
        _w = (1.0 + jnp.arange(8192, dtype=jnp.float32)) ** (-0.5)
        _w = _w / _w.mean()
        _pij = jnp.clip(0.000488281 * _w[:, None] * _w[None, :], 0.0, 1.0)
        _a = jax.random.uniform(jax.random.fold_in(_gk, 2), (8192, 8192)) < _pij
        _af = _a.astype(jnp.float32)
        adj = _af
        return (x, adj)
    x, adj = _rec_inputs()

    def _L0_gnn_setup():
        import jax, jax.numpy as jnp
        import numpy as np
        N = 2048
        IN_C = 128
        OUT_C = 128
        H = 4
        D = OUT_C // H
        C_CURV = 1.0
        EPS = 1e-15
        MAX_TANH_ARG = 1.0 - 1e-05
        NEG_INF = -1e+30

        def logmap0(x, c):
            sqrt_c = jnp.sqrt(c)
            xn = jnp.maximum(jnp.linalg.norm(x, axis=-1, keepdims=True), EPS)
            arg = jnp.minimum(sqrt_c * xn, MAX_TANH_ARG)
            return jnp.arctanh(arg) * x / (sqrt_c * xn)

        def expmap0(v, c):
            sqrt_c = jnp.sqrt(c)
            vn = jnp.maximum(jnp.linalg.norm(v, axis=-1, keepdims=True), EPS)
            return jnp.tanh(sqrt_c * vn) * v / (sqrt_c * vn)
        key = jax.random.key(seed)
        k_x, k_adj, k_w, k_al, k_ar = jax.random.split(key, 5)
        x = 0.01 * jax.random.normal(k_x, (N, IN_C), dtype=jnp.float32)
        adj = (jax.random.uniform(k_adj, (N, N)) < 0.004).astype(jnp.float32)
        lim_w = float(np.sqrt(6.0 / (IN_C + OUT_C)))
        W = jax.random.uniform(k_w, (OUT_C, IN_C), minval=-lim_w, maxval=lim_w, dtype=jnp.float32)
        lim_a = float(np.sqrt(6.0 / (H + D)))
        a_l = jax.random.uniform(k_al, (H, D), minval=-lim_a, maxval=lim_a, dtype=jnp.float32)
        a_r = jax.random.uniform(k_ar, (H, D), minval=-lim_a, maxval=lim_a, dtype=jnp.float32)
        bias = jnp.zeros((OUT_C,), dtype=jnp.float32)
        return {'x': x, 'adj': adj, 'W': W, 'a_l': a_l, 'a_r': a_r, 'bias': bias}
    _L0_gnn_all = _L0_gnn_setup()
    _L0_gnn_in = {k: v for k, v in _L0_gnn_all.items() if k in ('W', 'a_l', 'a_r', 'bias')}
    del _L0_gnn_all

    def _L0_ffn_setup():
        import jax, jax.numpy as jnp
        import numpy as np
        D_MODEL = 128
        D_STATE = 64
        D_CONV = 4
        EXPAND = 2
        HEADDIM = 64
        D_INNER = EXPAND * D_MODEL
        NHEADS = D_INNER // HEADDIM
        CONV_DIM = D_INNER + 2 * D_STATE
        D_IN_PROJ = 2 * D_INNER + 2 * D_STATE + NHEADS
        CHUNK = 128
        EPS = 1e-05

        def segsum(a):
            T = a.shape[-1]
            cs = jnp.cumsum(a, axis=-1)
            ss = cs[..., :, None] - cs[..., None, :]
            mask = jnp.tril(jnp.ones((T, T), dtype=bool))
            return jnp.where(mask, ss, -jnp.inf)

        def mamba2_block(x, W_in, conv_w, conv_b, dt_bias, A_log, D, norm_w, W_out, W_lin, b_lin):
            Bsz, L, _ = x.shape
            zxbcdt = x @ W_in
            z, xBC, dt = jnp.split(zxbcdt, [D_INNER, D_INNER + CONV_DIM], axis=-1)
            xp = jnp.pad(xBC, ((0, 0), (D_CONV - 1, 0), (0, 0)))
            conv = conv_b + sum((xp[:, k:k + L, :] * conv_w[:, k] for k in range(D_CONV)))
            xBC = jax.nn.silu(conv)
            xh, Bmat, Cmat = jnp.split(xBC, [D_INNER, D_INNER + D_STATE], axis=-1)
            dt = jax.nn.softplus(dt + dt_bias)
            A = -jnp.exp(A_log)
            nc = L // CHUNK
            xh = xh.reshape(Bsz, nc, CHUNK, NHEADS, HEADDIM)
            Bc = Bmat.reshape(Bsz, nc, CHUNK, D_STATE)
            Cc = Cmat.reshape(Bsz, nc, CHUNK, D_STATE)
            dtc = dt.reshape(Bsz, nc, CHUNK, NHEADS)
            dA = jnp.einsum('bclh,h->bhcl', dtc, A)
            A_cum = jnp.cumsum(dA, axis=-1)
            Lmat = jnp.exp(segsum(dA))
            xdt = xh * dtc[..., None]
            Y_diag = jnp.einsum('bcln,bcsn,bhcls,bcshp->bclhp', Cc, Bc, Lmat, xdt)
            decay_states = jnp.exp(A_cum[..., -1:] - A_cum)
            states = jnp.einsum('bcln,bhcl,bclhp->bchpn', Bc, decay_states, xdt)
            chunk_decay = jnp.exp(A_cum[..., -1])

            def step(h, inp):
                s, d = inp
                return (h * d[..., None, None] + s, h)
            _, prevs = jax.lax.scan(step, jnp.zeros_like(states[:, 0]), (jnp.moveaxis(states, 1, 0), jnp.moveaxis(chunk_decay, 2, 0)))
            prevs = jnp.moveaxis(prevs, 0, 1)
            Y_off = jnp.einsum('bcln,bchpn,bhcl->bclhp', Cc, prevs, jnp.exp(A_cum))
            Y = (Y_diag + Y_off + xh * D[:, None]).reshape(Bsz, L, D_INNER)
            Y = Y * jax.nn.silu(z)
            Y = Y * jax.lax.rsqrt(jnp.mean(Y * Y, axis=-1, keepdims=True) + EPS) * norm_w
            out = Y @ W_out
            return out @ W_lin + b_lin
        key = jax.random.key(seed)
        ks = jax.random.split(key, 12)
        B, L = (8, 2048)

        def gauss(k, shape, scale):
            return jax.random.normal(k, shape, dtype=jnp.float32) * scale
        return {'x': gauss(ks[0], (B, L, D_MODEL), 1.0), 'W_in': gauss(ks[1], (D_MODEL, D_IN_PROJ), D_MODEL ** (-0.5)), 'conv_w': gauss(ks[2], (CONV_DIM, D_CONV), 0.3), 'conv_b': gauss(ks[3], (CONV_DIM,), 0.1), 'dt_bias': jax.random.uniform(ks[4], (NHEADS,), minval=-4.0, maxval=-1.0), 'A_log': jnp.log(jax.random.uniform(ks[5], (NHEADS,), minval=1.0, maxval=16.0)), 'D': jnp.ones((NHEADS,), jnp.float32), 'norm_w': jnp.ones((D_INNER,), jnp.float32), 'W_out': gauss(ks[6], (D_INNER, D_MODEL), D_INNER ** (-0.5)), 'W_lin': gauss(ks[7], (D_MODEL, D_MODEL), D_MODEL ** (-0.5)), 'b_lin': jnp.zeros((D_MODEL,), jnp.float32)}
    _L0_ffn_all = _L0_ffn_setup()
    _L0_ffn_in = {k: v for k, v in _L0_ffn_all.items() if k in ('W_in', 'conv_w', 'conv_b', 'dt_bias', 'A_log', 'D', 'norm_w', 'W_out', 'W_lin', 'b_lin')}
    del _L0_ffn_all

    def _L1_gnn_setup():
        import jax, jax.numpy as jnp
        import numpy as np
        N = 5000
        F = 128
        key = jax.random.key(seed)
        k1, k2 = jax.random.split(key)
        x = jax.random.normal(k1, (N, F), dtype=jnp.float32)
        A = jax.random.uniform(k2, (N, N), dtype=jnp.float32)
        W = jnp.ones((F,), dtype=jnp.float32)
        return {'input': x, 'A': A, 'W': W}
    _L1_gnn_all = _L1_gnn_setup()
    _L1_gnn_in = {k: v for k, v in _L1_gnn_all.items() if k in ('W',)}
    del _L1_gnn_all

    def _L1_ffn_setup():
        import jax, jax.numpy as jnp
        import numpy as np
        N_EXPERTS = 8
        TOP_K = 2
        key = jax.random.key(seed)
        ks = jax.random.split(key, 5)
        B, T, C, E, H = (8, 1024, 128, 8, 341)
        scale = 1.0 / np.sqrt(C)
        return {'x': jax.random.normal(ks[0], (B, T, C), dtype=jnp.float32), 'router_w': jax.random.normal(ks[1], (E, C), dtype=jnp.float32) * scale, 'w1': jax.random.normal(ks[2], (E, H, C), dtype=jnp.float32) * scale, 'w2': jax.random.normal(ks[3], (E, C, H), dtype=jnp.float32) * (1.0 / np.sqrt(H)), 'w3': jax.random.normal(ks[4], (E, H, C), dtype=jnp.float32) * scale}
    _L1_ffn_all = _L1_ffn_setup()
    _L1_ffn_in = {k: v for k, v in _L1_ffn_all.items() if k in ('router_w', 'w1', 'w2', 'w3')}
    del _L1_ffn_all
    return {'x': x, 'adj': adj, 'L0_gnn_W': _L0_gnn_in['W'], 'L0_gnn_a_l': _L0_gnn_in['a_l'], 'L0_gnn_a_r': _L0_gnn_in['a_r'], 'L0_gnn_bias': _L0_gnn_in['bias'], 'L0_ffn_W_in': _L0_ffn_in['W_in'], 'L0_ffn_conv_w': _L0_ffn_in['conv_w'], 'L0_ffn_conv_b': _L0_ffn_in['conv_b'], 'L0_ffn_dt_bias': _L0_ffn_in['dt_bias'], 'L0_ffn_A_log': _L0_ffn_in['A_log'], 'L0_ffn_D': _L0_ffn_in['D'], 'L0_ffn_norm_w': _L0_ffn_in['norm_w'], 'L0_ffn_W_out': _L0_ffn_in['W_out'], 'L0_ffn_W_lin': _L0_ffn_in['W_lin'], 'L0_ffn_b_lin': _L0_ffn_in['b_lin'], 'L1_gnn_W': _L1_gnn_in['W'], 'L1_ffn_router_w': _L1_ffn_in['router_w'], 'L1_ffn_w1': _L1_ffn_in['w1'], 'L1_ffn_w2': _L1_ffn_in['w2'], 'L1_ffn_w3': _L1_ffn_in['w3']}

def reference(x, adj, L0_gnn_W, L0_gnn_a_l, L0_gnn_a_r, L0_gnn_bias, L0_ffn_W_in, L0_ffn_conv_w, L0_ffn_conv_b, L0_ffn_dt_bias, L0_ffn_A_log, L0_ffn_D, L0_ffn_norm_w, L0_ffn_W_out, L0_ffn_W_lin, L0_ffn_b_lin, L1_gnn_W, L1_ffn_router_w, L1_ffn_w1, L1_ffn_w2, L1_ffn_w3):
    import jax
    import jax.numpy as jnp

    def _L0_gnn_ref(x, adj, W, a_l, a_r, bias):
        import jax, jax.numpy as jnp
        import numpy as np
        N = 2048
        IN_C = 128
        OUT_C = 128
        H = 4
        D = OUT_C // H
        C_CURV = 1.0
        EPS = 1e-15
        MAX_TANH_ARG = 1.0 - 1e-05
        NEG_INF = -1e+30

        def logmap0(x, c):
            sqrt_c = jnp.sqrt(c)
            xn = jnp.maximum(jnp.linalg.norm(x, axis=-1, keepdims=True), EPS)
            arg = jnp.minimum(sqrt_c * xn, MAX_TANH_ARG)
            return jnp.arctanh(arg) * x / (sqrt_c * xn)

        def expmap0(v, c):
            sqrt_c = jnp.sqrt(c)
            vn = jnp.maximum(jnp.linalg.norm(v, axis=-1, keepdims=True), EPS)
            return jnp.tanh(sqrt_c * vn) * v / (sqrt_c * vn)
        n = x.shape[0]
        x_tan = logmap0(x, C_CURV)
        h = (x_tan @ W.T).reshape(n, H, D)
        e_l = jnp.einsum('nhd,hd->nh', h, a_l)
        e_r = jnp.einsum('nhd,hd->nh', h, a_r)
        logits = e_l[:, None, :] + e_r[None, :, :]
        logits = jax.nn.leaky_relu(logits, negative_slope=0.2)
        adj_hat = adj + jnp.eye(n, dtype=adj.dtype)
        mask = (adj_hat > 0)[:, :, None]
        logits = jnp.where(mask, logits, NEG_INF)
        attn = jax.nn.softmax(logits, axis=1)
        out = jnp.einsum('ijh,jhd->ihd', attn, h).reshape(n, -1)
        out = out + bias
        out = jax.nn.silu(out)
        return expmap0(out, C_CURV)

    def _L0_ffn_ref(x, W_in, conv_w, conv_b, dt_bias, A_log, D, norm_w, W_out, W_lin, b_lin):
        import jax, jax.numpy as jnp
        import numpy as np
        D_MODEL = 128
        D_STATE = 64
        D_CONV = 4
        EXPAND = 2
        HEADDIM = 64
        D_INNER = EXPAND * D_MODEL
        NHEADS = D_INNER // HEADDIM
        CONV_DIM = D_INNER + 2 * D_STATE
        D_IN_PROJ = 2 * D_INNER + 2 * D_STATE + NHEADS
        CHUNK = 128
        EPS = 1e-05

        def segsum(a):
            T = a.shape[-1]
            cs = jnp.cumsum(a, axis=-1)
            ss = cs[..., :, None] - cs[..., None, :]
            mask = jnp.tril(jnp.ones((T, T), dtype=bool))
            return jnp.where(mask, ss, -jnp.inf)

        def mamba2_block(x, W_in, conv_w, conv_b, dt_bias, A_log, D, norm_w, W_out, W_lin, b_lin):
            Bsz, L, _ = x.shape
            zxbcdt = x @ W_in
            z, xBC, dt = jnp.split(zxbcdt, [D_INNER, D_INNER + CONV_DIM], axis=-1)
            xp = jnp.pad(xBC, ((0, 0), (D_CONV - 1, 0), (0, 0)))
            conv = conv_b + sum((xp[:, k:k + L, :] * conv_w[:, k] for k in range(D_CONV)))
            xBC = jax.nn.silu(conv)
            xh, Bmat, Cmat = jnp.split(xBC, [D_INNER, D_INNER + D_STATE], axis=-1)
            dt = jax.nn.softplus(dt + dt_bias)
            A = -jnp.exp(A_log)
            nc = L // CHUNK
            xh = xh.reshape(Bsz, nc, CHUNK, NHEADS, HEADDIM)
            Bc = Bmat.reshape(Bsz, nc, CHUNK, D_STATE)
            Cc = Cmat.reshape(Bsz, nc, CHUNK, D_STATE)
            dtc = dt.reshape(Bsz, nc, CHUNK, NHEADS)
            dA = jnp.einsum('bclh,h->bhcl', dtc, A)
            A_cum = jnp.cumsum(dA, axis=-1)
            Lmat = jnp.exp(segsum(dA))
            xdt = xh * dtc[..., None]
            Y_diag = jnp.einsum('bcln,bcsn,bhcls,bcshp->bclhp', Cc, Bc, Lmat, xdt)
            decay_states = jnp.exp(A_cum[..., -1:] - A_cum)
            states = jnp.einsum('bcln,bhcl,bclhp->bchpn', Bc, decay_states, xdt)
            chunk_decay = jnp.exp(A_cum[..., -1])

            def step(h, inp):
                s, d = inp
                return (h * d[..., None, None] + s, h)
            _, prevs = jax.lax.scan(step, jnp.zeros_like(states[:, 0]), (jnp.moveaxis(states, 1, 0), jnp.moveaxis(chunk_decay, 2, 0)))
            prevs = jnp.moveaxis(prevs, 0, 1)
            Y_off = jnp.einsum('bcln,bchpn,bhcl->bclhp', Cc, prevs, jnp.exp(A_cum))
            Y = (Y_diag + Y_off + xh * D[:, None]).reshape(Bsz, L, D_INNER)
            Y = Y * jax.nn.silu(z)
            Y = Y * jax.lax.rsqrt(jnp.mean(Y * Y, axis=-1, keepdims=True) + EPS) * norm_w
            out = Y @ W_out
            return out @ W_lin + b_lin
        return mamba2_block(x, W_in, conv_w, conv_b, dt_bias, A_log, D, norm_w, W_out, W_lin, b_lin)

    def _L1_gnn_ref(input, A, W):
        import jax, jax.numpy as jnp
        import numpy as np
        N = 5000
        F = 128
        hidden = input * W
        return A @ hidden

    def _L1_ffn_ref(x, router_w, w1, w2, w3):
        import jax, jax.numpy as jnp
        import numpy as np
        N_EXPERTS = 8
        TOP_K = 2
        B, T, C = x.shape
        flat = x.reshape(-1, C)
        logits = flat @ router_w.T
        probs = jax.nn.softmax(logits, axis=-1)
        topk_probs, topk_idx = jax.lax.top_k(probs, TOP_K)
        topk_probs = topk_probs / (jnp.sum(topk_probs, axis=-1, keepdims=True) + 1e-09)
        onehot = jax.nn.one_hot(topk_idx, N_EXPERTS, dtype=flat.dtype)
        gates = jnp.einsum('nk,nke->ne', topk_probs, onehot)
        h1 = jnp.einsum('nc,ehc->neh', flat, w1)
        h3 = jnp.einsum('nc,ehc->neh', flat, w3)
        h = jax.nn.silu(h1) * h3
        y = jnp.einsum('neh,ech->nec', h, w2)
        out = jnp.einsum('ne,nec->nc', gates, y)
        return out.reshape(B, T, C)
    x = x + _L0_gnn_ref(_layernorm(x, axis=-1), adj, L0_gnn_W, L0_gnn_a_l, L0_gnn_a_r, L0_gnn_bias)
    x = x + _L0_ffn_ref(_layernorm(x, axis=-1)[None], L0_ffn_W_in, L0_ffn_conv_w, L0_ffn_conv_b, L0_ffn_dt_bias, L0_ffn_A_log, L0_ffn_D, L0_ffn_norm_w, L0_ffn_W_out, L0_ffn_W_lin, L0_ffn_b_lin)[0]
    x = x + _L1_gnn_ref(_layernorm(x, axis=-1), adj, L1_gnn_W)
    x = x + _L1_ffn_ref(_layernorm(x, axis=-1)[None], L1_ffn_router_w, L1_ffn_w1, L1_ffn_w2, L1_ffn_w3)[0]
    return x

_drawn_inputs = setup_inputs


def setup_inputs(seed=0):
    import zlib

    import numpy as np

    out = dict(_drawn_inputs(seed))
    spreads = {'L0_gnn_bias': (0.0, 0.1),
     'L0_ffn_D': (1.0, 0.2),
     'L0_ffn_norm_w': (1.0, 0.2),
     'L0_ffn_b_lin': (0.0, 0.1),
     'L1_gnn_W': (1.0, 0.2)}
    factors = {'L0_ffn_A_log': 4.401}
    for name, (base, spread) in spreads.items():
        noise = np.random.default_rng([zlib.crc32(name.encode()), seed]).standard_normal(out[name].shape)
        drawn = base * np.exp(spread * noise) if base else spread * noise
        out[name] = jnp.asarray(drawn.astype(out[name].dtype))
    for name, factor in factors.items():
        out[name] = (out[name] * factor).astype(out[name].dtype)
    return out
```

```python
import concourse.bass as bass
from concourse import mybir
from contextlib import ExitStack

FP32 = mybir.dt.float32
BF16 = mybir.dt.bfloat16
UINT32 = mybir.dt.uint32
ALU = mybir.AluOpType
ACT = mybir.ActivationFunctionType
AX = mybir.AxisListType

P = 128
C = 128
TB = 4
BLK = P * TB
H = 4
D = C // H
DV = D + 1
LN_EPS = 1e-5


class Scope:

    def __init__(self, nc, ctx, name):
        self.nc, self.ctx, self.name = nc, ctx, name

    def sb(self, name, shape, dt=FP32):
        return self.ctx.enter_context(self.nc.sbuf_tensor(f"{self.name}_{name}", shape, dt))

    def ps(self, name, shape, dt=FP32):
        return self.ctx.enter_context(self.nc.psum_tensor(f"{self.name}_ps_{name}", shape, dt))

    def sem(self, name):
        return self.ctx.enter_context(self.nc.semaphore(f"{self.name}_{name}"))


class Chain:

    def __init__(self, engine, sem, count=0):
        self.engine, self.sem, self.count, self.ops = engine, sem, count, 0

    def __call__(self, op):
        self.ops += 1
        self.count = self.count + 1
        op.then_inc(self.sem, 1)
        self.engine.wait_ge(self.sem, self.count)


def row_statistics(nc, link, stats, mean, var, tmp):
    half = C // 2
    link(nc.vector.tensor_tensor(mean, stats[:, :, 1], stats[:, :, 4], ALU.add))
    link(nc.vector.tensor_scalar(mean, mean, 0.5, None, ALU.mult))
    link(nc.vector.tensor_tensor(tmp, stats[:, :, 1], stats[:, :, 4], ALU.subtract))
    link(nc.vector.tensor_tensor(tmp, tmp, tmp, ALU.mult))
    link(nc.vector.tensor_scalar(tmp, tmp, 0.25, None, ALU.mult))
    link(nc.vector.tensor_tensor(var, stats[:, :, 2], stats[:, :, 5], ALU.add))
    link(nc.vector.tensor_scalar(var, var, 1.0 / C, None, ALU.mult))
    link(nc.vector.tensor_tensor(var, var, tmp, ALU.add))


def attention_layer(nc, x, adj, W, W_T, a_l, a_r, bias, left_t, x1):
    N = x.shape[0]
    NT, NB = N // P, N // BLK
    assert NB & (NB - 1) == 0
    CH = BLK
    JC = CH // P
    x_tiles = x.rearrange("(t p) c -> p t c", p=P)

    keep = ExitStack()
    with keep:
        k = Scope(nc, keep, "gat")
        values = k.sb("values", [P, NT, 2, H, 3, DV], BF16)
        threshold = k.sb("threshold", [P, NT, H])
        scale01 = k.sb("scale01", [P, NT, 2, H])
        ident = k.sb("ident", [P, 2, P])
        fold = k.sb("fold", [3 * DV, DV])
        bias_row = k.sb("bias_row", [P, C])

        with ExitStack() as ctx:
            s = Scope(nc, ctx, "prep")
            xin = s.sb("xin", [P, NT, C])
            hid = s.sb("hid", [P, NT, C])
            xn = s.sb("xn", [P, 2, TB, C])
            xt = s.sb("xt", [C, 2, BLK])
            w_nat = s.sb("w_nat", [C, C])
            w_t = s.sb("w_t", [C, C])
            a_blk = s.sb("a_blk", [C, 2 * H])
            wa = s.sb("wa", [C, 2 * H])
            logit = s.sb("logit", [P, NT, 2, H])
            lt = s.sb("lt", [H, 2, BLK])
            stats = s.sb("stats", [P, NT, 6])
            mean = s.sb("mean", [P, NT])
            var = s.sb("var", [P, NT])
            tmp = s.sb("tmp", [P, NT])
            root = s.sb("root", [P, 2, NT])
            rstd = s.sb("rstd", [P, NT])
            norm = s.sb("norm", [P, NT])
            arg = s.sb("arg", [P, 2, NT])
            lns = s.sb("lns", [P, 2, NT])
            fac = s.sb("fac", [P, NT])
            rm = s.sb("rm", [P, H])
            rmt = s.sb("rmt", [H, 1])
            rdiag = s.sb("rdiag", [H, H])
            rmax = s.sb("rmax", [P, H])
            ones = s.sb("ones", [H, P])
            q = s.sb("q", [P, NT, H])
            wexp = s.sb("wexp", [P, NT, 2, H])
            val = s.sb("val", [P, 2, TB, H, DV])
            res = s.sb("res", [P, 2, TB, H, DV])
            ps_t = s.ps("t", [P, 2, BLK])
            ps_h = s.ps("h", [P, 2, BLK])
            ps_e = s.ps("e", [P, 2, BLK])
            ps_l = s.ps("l", [P, 2, BLK])
            x_in = s.sem("x_in")
            w_in = s.sem("w_in")
            consts = s.sem("consts")
            chain_dve = s.sem("chain_dve")
            stats_done = s.sem("stats_done")
            rooted = s.sem("rooted")
            var_ready = s.sem("var_ready")
            arg_ready = s.sem("arg_ready")
            ln_ready = s.sem("ln_ready")
            wa_ps = s.sem("wa_ps")
            wa_ready = s.sem("wa_ready")
            xn_ready = s.sem("xn_ready")
            t_ps = s.sem("t_ps")
            xt_ready = s.sem("xt_ready")
            proj_ps = s.sem("proj_ps")
            hid_ready = s.sem("hid_ready")
            logit_ready = s.sem("logit_ready")
            lt_out = [s.sem(f"lt_out{u}") for u in range(2)]
            rm_ready = s.sem("rm_ready")
            rm_ps = s.sem("rm_ps")
            rm_diag = s.sem("rm_diag")
            rm_all = s.sem("rm_all")
            q_ready = s.sem("q_ready")
            exp_done = s.sem("exp_done")

            with nc.Block() as block:
                @block.sync
                def _(sp):
                    sp.wait_ge(consts, 2)
                    for h in range(H):
                        rows = slice(h * D, (h + 1) * D)
                        sp.dma_start(a_blk[rows, h:h + 1], a_l[h, :].unsqueeze(1)).then_inc(w_in, 16)
                        sp.dma_start(a_blk[rows, H + h:H + h + 1], a_r[h, :].unsqueeze(1)).then_inc(w_in, 16)
                    with sp.Fori(0, NB // 2) as pair:
                        for u in range(2):
                            sp.wait_ge(logit_ready, pair * 2 + (u + 1))
                            sp.dma_start(left_t[:, bass.ds((pair * 2 + u) * BLK, BLK)],
                                         lt[:, u, :]).then_inc(lt_out[u], 16)
                    for u in range(2):
                        sp.wait_ge(lt_out[u], 16 * (NB // 2))

                @block.gpsimd
                def _(pool):
                    link = Chain(pool, consts)
                    link(nc.gpsimd.memset(ident[:, :, :], 0.0))
                    link(nc.gpsimd.memset(a_blk[:, :], 0.0))
                    link(nc.gpsimd.affine_select(out=ident[:, 0, :], in_=ident[:, 0, :], compare_op=ALU.not_equal,
                                                 fill=1.0, base=0, pattern=[[-1, P]], channel_multiplier=1))
                    link(nc.gpsimd.memset(ones[:, :], 1.0))
                    link(nc.gpsimd.memset(fold[:, :], 0.0))
                    for part in range(3):
                        link(nc.gpsimd.affine_select(out=fold[:, :], in_=fold[:, :], compare_op=ALU.not_equal,
                                                     fill=1.0, base=-DV * part, pattern=[[-1, DV]],
                                                     channel_multiplier=1))

                @block.scalar
                def _(act):
                    for b in range(4):
                        tiles = slice(b * NT // 4, (b + 1) * NT // 4)
                        act.dma_start(xin[:, tiles, :], x_tiles[:, tiles, :]).then_inc(x_in, 16)
                    act.dma_start(w_nat[:, :], W).then_inc(w_in, 16)
                    act.dma_start(w_t[:, :], W_T).then_inc(w_in, 16)
                    act.dma_start(bias_row[:, :], bias.partition_broadcast(P)).then_inc(w_in, 16)
                    act.wait_ge(var_ready, 1)
                    nc.scalar.activation(root[:, 0, :], tmp[:, :], ACT.Sqrt).then_inc(rooted, 1)
                    nc.scalar.activation(root[:, 1, :], var[:, :], ACT.Sqrt, scale=float(C)).then_inc(rooted, 1)
                    act.wait_ge(arg_ready, 1)
                    nc.scalar.activation(lns[:, :, :], arg[:, :, :], ACT.Ln).then_inc(ln_ready, 1)
                    with act.Fori(0, NB // 2) as pair:
                        for u in range(2):
                            act.wait_ge(t_ps, pair * 2 + (u + 1))
                            nc.scalar.activation(xt[:, u, :], ps_t[:, u, :], ACT.Copy).then_inc(xt_ready, 1)
                            act.wait_ge(proj_ps, pair * 2 + (u + 1))
                            nc.scalar.activation(hid[:, bass.ds((pair * 2 + u) * TB, TB), :],
                                                 ps_h[:, u, :].rearrange("p (t c) -> p t c", c=C),
                                                 ACT.Copy).then_inc(hid_ready, 1)
                    act.wait_ge(q_ready, 1)
                    nc.scalar.activation(wexp[:, :, 0, :], q[:, :, :], ACT.Exp).then_inc(exp_done, 1)
                    nc.scalar.activation(wexp[:, :, 1, :], q[:, :, :], ACT.Exp, scale=0.2).then_inc(exp_done, 1)
                    act.wait_ge(q_ready, 2)
                    nc.scalar.activation(scale01[:, :, :, :], scale01[:, :, :, :], ACT.Exp).then_inc(exp_done, 1)

                @block.vector
                def _(dve):
                    link = Chain(dve, chain_dve)
                    dve.wait_ge(x_in, 16 * 4)
                    with dve.Fori(0, NT) as t:
                        nc.vector.bn_stats(stats[:, t, :], xin[:, t, :]).then_inc(stats_done, 1)
                    dve.wait_ge(stats_done, NT)
                    row_statistics(nc, link, stats, mean[:, :], var[:, :], tmp[:, :])
                    nc.vector.tensor_scalar(tmp[:, :], var[:, :], LN_EPS, None, ALU.add).then_inc(var_ready, 1)
                    dve.wait_ge(rooted, 1)
                    link(nc.vector.reciprocal(rstd[:, :], root[:, 0, :]))
                    dve.wait_ge(rooted, 2)
                    link(nc.vector.tensor_tensor(norm[:, :], root[:, 1, :], rstd[:, :], ALU.mult))
                    link(nc.vector.tensor_scalar(norm[:, :], norm[:, :], 1e-15, None, ALU.max))
                    link(nc.vector.tensor_scalar(fac[:, :], norm[:, :], 1.0 - 1e-5, None, ALU.min))
                    link(nc.vector.tensor_scalar(arg[:, 0, :], fac[:, :], 1.0, None, ALU.add))
                    nc.vector.tensor_scalar(arg[:, 1, :], fac[:, :], -1.0, 1.0, ALU.mult, ALU.add).then_inc(arg_ready, 1)
                    dve.wait_ge(ln_ready, 1)
                    link(nc.vector.tensor_tensor(fac[:, :], lns[:, 0, :], lns[:, 1, :], ALU.subtract))
                    link(nc.vector.tensor_scalar(fac[:, :], fac[:, :], 0.5, None, ALU.mult))
                    link(nc.vector.reciprocal(norm[:, :], norm[:, :]))
                    link(nc.vector.tensor_tensor(fac[:, :], fac[:, :], norm[:, :], ALU.mult))
                    link(nc.vector.tensor_tensor(fac[:, :], fac[:, :], rstd[:, :], ALU.mult))
                    dve.wait_ge(wa_ps, 1)
                    nc.vector.tensor_copy(wa[:, :], ps_e[:, 0, 0:2 * H]).then_inc(wa_ready, 1)
                    with dve.Fori(0, NB // 2) as pair:
                        for u in range(2):
                            b = pair * 2 + u
                            for i in range(TB):
                                op = nc.vector.tensor_scalar(xn[:, u, i, :], xin[:, b * TB + i, :],
                                                             mean[:, bass.ds(b * TB + i, 1)],
                                                             fac[:, bass.ds(b * TB + i, 1)],
                                                             ALU.subtract, ALU.mult)
                            op.then_inc(xn_ready, 1)
                            dve.wait_ge(proj_ps, b + 1)
                            nc.vector.tensor_scalar(logit[:, bass.ds(b * TB, TB), :, :],
                                                    ps_e[:, u, 0:TB * 2 * H]
                                                    .rearrange("p (t s h) -> p t s h", t=TB, s=2), 1.0, None, ALU.mult)
                            dve.wait_ge(lt_out[u], pair * 16)
                            nc.vector.tensor_copy(lt[:, u, :], ps_l[0:H, u, :]).then_inc(logit_ready, 1)
                    dve.wait_ge(logit_ready, NB)
                    nc.vector.tensor_reduce(rm[:, :], logit[:, :, 1, :].rearrange("p t h -> p h t"),
                                            AX.X, ALU.max).then_inc(rm_ready, 1)
                    dve.wait_ge(rm_ps, 1)
                    link(nc.vector.tensor_reduce(rmt[:, :], ps_t[0:H, 0, 0:P], AX.X, ALU.max))
                    nc.vector.tensor_scalar(rdiag[:, :], ident[0:H, 0, 0:H], rmt[:, 0:1], None,
                                            ALU.mult).then_inc(rm_diag, 1)
                    dve.wait_ge(rm_ps, 2)
                    link(nc.vector.tensor_copy(rmax[:, :], ps_e[:, 0, 0:H]))
                    rb = rmax[:, :].unsqueeze(1).to_broadcast([P, NT, H])
                    nc.vector.tensor_tensor(q[:, :, :], logit[:, :, 1, :], rb, ALU.subtract).then_inc(q_ready, 1)
                    link(nc.vector.tensor_scalar(threshold[:, :, :], logit[:, :, 1, :], -1.0, None, ALU.mult))
                    link(nc.vector.tensor_tensor(logit[:, :, 0, :], logit[:, :, 0, :], rb, ALU.add))
                    link(nc.vector.tensor_scalar(scale01[:, :, 0, :], logit[:, :, 0, :], 0.8, 0.0, ALU.mult, ALU.min))
                    nc.vector.tensor_scalar(scale01[:, :, 1, :], logit[:, :, 0, :], -0.8, 0.0, ALU.mult,
                                            ALU.min).then_inc(q_ready, 1)
                    dve.wait_ge(exp_done, 2)
                    dve.wait_ge(hid_ready, NB)
                    per_block = 2 * 6
                    first = link.count
                    with dve.Fori(0, NB) as b:
                        step = Chain(dve, chain_dve, b * per_block + first)
                        t0 = b * TB
                        for g in range(2):
                            w = wexp[:, bass.ds(t0, TB), g, :].unsqueeze(3)
                            hv = hid[:, bass.ds(t0, TB), :].rearrange("p t (h d) -> p t h d", h=H)
                            v, r = val[:, g, :, :, :], res[:, g, :, :, :]
                            part = [values[:, bass.ds(t0, TB), g, :, i, :] for i in range(3)]
                            step(nc.vector.tensor_tensor(v[:, :, :, 0:D], hv, w.to_broadcast([P, TB, H, D]), ALU.mult))
                            step(nc.vector.tensor_scalar(v[:, :, :, D:DV], w, 1.0, None, ALU.mult))
                            step(nc.vector.tensor_scalar(part[0], v, 1.0, None, ALU.mult))
                            step(nc.vector.tensor_tensor(r, v, part[0], ALU.subtract))
                            step(nc.vector.tensor_scalar(part[1], r, 1.0, None, ALU.mult))
                            step(nc.vector.tensor_tensor(part[2], r, part[1], ALU.subtract))

                @block.tensor
                def _(pe):
                    pe.wait_ge(consts, 8)
                    pe.wait_ge(w_in, 16 * 11)
                    nc.tensor.matmul(ps_e[:, 0, 0:2 * H], w_nat[:, :], a_blk[:, :], start=True,
                                     stop=True).then_inc(wa_ps, 1)
                    pe.wait_ge(wa_ready, 1)
                    with pe.Fori(0, NB // 2) as pair:
                        for u in range(2):
                            b = pair * 2 + u
                            pe.wait_ge(xn_ready, b + 1)
                            for i in range(TB):
                                op = nc.tensor.transpose(ps_t[:, u, i * P:(i + 1) * P], xn[:, u, i, :], ident[:, 0, :])
                            op.then_inc(t_ps, 1)
                            pe.wait_ge(xt_ready, b + 1)
                            pe.wait_ge(hid_ready, b)
                            pe.wait_ge(logit_ready, b)
                            for i in range(TB):
                                rows = xt[:, u, i * P:(i + 1) * P]
                                nc.tensor.matmul(ps_h[:, u, i * C:(i + 1) * C], rows, w_t[:, :], start=True, stop=True)
                                nc.tensor.matmul(ps_e[:, u, i * 2 * H:(i + 1) * 2 * H], rows, wa[:, :],
                                                 start=True, stop=True)
                            nc.tensor.matmul(ps_l[0:H, u, :], wa[:, 0:H], xt[:, u, :], start=True,
                                             stop=True).then_inc(proj_ps, 1)
                    pe.wait_ge(rm_ready, 1)
                    nc.tensor.transpose(ps_t[0:H, 0, 0:P], rm[:, :], ident[:, 0, :]).then_inc(rm_ps, 1)
                    pe.wait_ge(rm_diag, 1)
                    nc.tensor.matmul(ps_e[:, 0, 0:H], ones[:, :], rdiag[:, :], start=True, stop=True).then_inc(rm_ps, 1)

        attention_sweep(nc, N, x_tiles, adj, left_t, x1, values, threshold, scale01, ident, fold, bias_row)



def attention_sweep(nc, N, x_tiles, adj, left_t, x1, values, threshold, scale01, ident, fold, bias_row):
    NT, NB = N // P, N // BLK
    UJ = 2 * TB
    HG = 2
    x1_tiles = x1.rearrange("(t p) c -> p t c", p=P)
    adj_rows = adj.rearrange("(t p) c -> p t c", p=P)
    DVH = 3 * DV

    with ExitStack() as ctx:
        s = Scope(nc, ctx, "att")
        adjr = s.sb("adjr", [P, 2, TB, BLK])
        mask = s.sb("mask", [P, NT, BLK], BF16)
        left = s.sb("left", [P, H, BLK])
        sel = s.sb("sel", [P, 2, 2, HG, BLK], BF16)
        accs = s.sb("accs", [P, 2, BLK])
        num = s.sb("num", [P, TB, H, DV])
        half = s.sb("half", [P, TB // 2, HG, DV])
        zeros = s.sb("zeros", [1, BLK], BF16)
        small = s.sb("small", [P, 5, TB])
        rec = s.sb("rec", [P, TB, H])
        work = sel[:, :, :, :, :].rearrange("p s b h i -> p (s b h i)").bitcast(FP32)
        out_w = work[:, 0:TB * C]
        th_w = work[:, TB * C:2 * TB * C]
        xo = work[:, 2 * TB * C:3 * TB * C].rearrange("p (t c) -> p t c", t=TB)
        ps_acc = s.ps("acc", [P, 2 * HG, BLK])
        ps_t = s.ps("t", [P, 2, BLK])
        ps_d = s.ps("d", [P, 2, BLK])

        adj_in = [s.sem(f"adj_in{u}") for u in range(2)]
        adj_ready = s.sem("adj_ready")
        t_ps = s.sem("t_ps")
        mask_ready = s.sem("mask_ready")
        sel0_ready = s.sem("sel0_ready")
        sel1_ready = s.sem("sel1_ready")
        sel_free = s.sem("sel_free")
        accs_ready = s.sem("accs_ready")
        fold_ps = s.sem("fold_ps")
        num_ready = s.sem("num_ready")
        left_in = s.sem("left_in")
        x_in = s.sem("x_in")
        x_out = s.sem("x_out")
        out_ready = s.sem("out_ready")
        tanh_done = s.sem("tanh_done")
        silu_ready = s.sem("silu_ready")
        square_done = s.sem("square_done")
        norm_ready = s.sem("norm_ready")
        x1_ready = s.sem("x1_ready")
        chain_dve = s.sem("chain_dve")
        zeroed = s.sem("zeroed")
        SQ = 0
        NORM = 1
        TNORM = 2
        FACT = 3
        VN = 4

        with nc.Block() as block:
            @block.sync
            def _(sp):
                with sp.Fori(0, NB) as ib:
                    sp.wait_ge(sel0_ready, ib * 2 * NT)
                    for h in range(H):
                        sp.dma_start(left[:, h, :], left_t[h:h + 1, bass.ds(ib * BLK, BLK)].squeeze(0)
                                     .partition_broadcast(P)).then_inc(left_in, 16)
                    with sp.Fori(0, NT // UJ) as jp:
                        for u in range(2):
                            load = ib * (NT // TB) + (jp * 2 + u)
                            sp.wait_ge(t_ps, load * TB)
                            sp.dma_start(adjr[:, u, :, :],
                                         adj_rows[:, bass.ds(ib * TB, TB), bass.ds((jp * 2 + u) * BLK, BLK)]
                                         ).then_inc(adj_in[u], 16)

            @block.gpsimd
            def _(pool):
                pool.sem_inc(t_ps, TB)
                pool.sem_inc(mask_ready, 2)
                pool.sem_inc(sel_free, 2)
                nc.gpsimd.memset(zeros[:, :], 0.0).then_inc(zeroed, 1)

                def other_branch(u, jt, step):
                    pool.wait_ge(sel0_ready, step + 1)
                    nc.gpsimd.tensor_tensor(sel[:, u % 2, 1, :, :],
                                            mask[:, bass.ds(jt, 1), :].to_broadcast([P, HG, BLK]),
                                            sel[:, u % 2, 0, :, :], ALU.subtract).then_inc(sel1_ready, 1)

                with pool.Fori(0, NB) as ib:
                    with pool.Fori(0, NT // UJ) as jp:
                        for u in range(UJ):
                            if u % TB == 0:
                                away = ((ib * (NB - 1) + jp * 2 + u // TB) & (NB - 1)) + (NB - 1)
                                away = pool.snap(away >> (NB.bit_length() - 1)).with_bounds(min_val=0, max_val=1)
                                add = ident[:, bass.ds(away, 1), :].squeeze(1)
                                pool.wait_ge(adj_in[u // TB], ib * (NT // UJ * 16) + jp * 16 + 16)
                                for i in range(TB):
                                    diag = adjr[:, u // TB, i, i * P:(i + 1) * P]
                                    op = nc.gpsimd.tensor_tensor(diag, diag, add, ALU.add)
                                op.then_inc(adj_ready, 1)
                            jt = jp * UJ + u
                            other_branch(u, jt, ib * 2 * NT + jt)
                    with pool.Fori(0, NT // UJ) as jp:
                        for u in range(UJ):
                            jt = jp * UJ + u
                            other_branch(u, jt, ib * 2 * NT + NT + jt)

            @block.scalar
            def _(act):
                with act.Fori(0, NB) as ib:
                    for g in range(H // HG):
                        group = ib * 2 + g
                        act.wait_ge(sel_free, (group + 1) * NT + 2)
                        for a in range(2 * HG):
                            if a < 2:
                                act.wait_ge(fold_ps, group * 4)
                            else:
                                act.wait_ge(fold_ps, group * 4 + (a - 1))
                            nc.scalar.activation(accs[0:DVH, a % 2, :], ps_acc[0:DVH, a, :],
                                                 ACT.Copy).then_inc(accs_ready, 1)
                    act.dma_start(xo[:, :, :], x_tiles[:, bass.ds(ib * TB, TB), :]).then_inc(x_in, 16)
                    act.wait_ge(out_ready, ib + 1)
                    nc.scalar.activation(th_w, out_w, ACT.Tanh, scale=0.5).then_inc(tanh_done, 1)
                    act.wait_ge(silu_ready, ib + 1)
                    for i in range(TB):
                        nc.scalar.activation(th_w[:, i * C:(i + 1) * C], out_w[:, i * C:(i + 1) * C], ACT.Square,
                                             scale=0.5, accum_out=small[:, SQ, i:i + 1]).then_inc(square_done, 1)
                    act.wait_ge(square_done, ib * (TB + 3) + TB)
                    nc.scalar.activation(small[:, VN, :], small[:, SQ, :], ACT.Sqrt).then_inc(square_done, 1)
                    act.wait_ge(norm_ready, ib + 1)
                    nc.scalar.activation(small[:, TNORM, :], small[:, NORM, :], ACT.Tanh).then_inc(square_done, 2)
                    act.wait_ge(x1_ready, ib + 1)
                    act.dma_start(x1_tiles[:, bass.ds(ib * TB, TB), :], xo[:, :, :]).then_inc(x_out, 16)
                act.wait_ge(x_out, NB * 16)

            @block.vector
            def _(dve):
                per_block = 2 * 6 + 2 + 4

                def first_branch(u, g, jt, step):
                    dve.wait_ge(sel_free, step + 1)
                    for h in range(HG):
                        op = nc.vector.scalar_tensor_tensor(
                            out=sel[:, u % 2, 0, h, :], in0=left[:, g * HG + h, :],
                            scalar=threshold[:, jt, g * HG + h:g * HG + h + 1],
                            in1=mask[:, jt, :], op0=ALU.is_gt, op1=ALU.mult)
                    op.then_inc(sel0_ready, 1)

                def sum_branches(link, ib, g):
                    dve.wait_ge(fold_ps, (ib * 2 + g + 1) * 4)
                    for b in range(2):
                        folded = ps_d[:, b, 0:2 * 4 * DV].rearrange("p (i h g v) -> p g i h v", i=2, h=HG, g=2)
                        tiles = bass.ds(ib * TB + b * 2, 2)
                        heads = slice(g * HG, (g + 1) * HG)
                        out = num[:, b * 2:b * 2 + 2, heads, :]
                        link(nc.vector.tensor_tensor(half[:, :, :, :], folded[:, 0],
                                                     scale01[:, tiles, 0, heads].unsqueeze(3)
                                                     .to_broadcast([P, 2, HG, DV]), ALU.mult))
                        link(nc.vector.tensor_tensor(out, folded[:, 1],
                                                     scale01[:, tiles, 1, heads].unsqueeze(3)
                                                     .to_broadcast([P, 2, HG, DV]), ALU.mult))
                        link(nc.vector.tensor_tensor(out, out, half[:, :, :, :], ALU.add))
                    dve.sem_inc(num_ready, 1)

                with dve.Fori(0, NB) as ib:
                    link = Chain(dve, chain_dve, ib * per_block)
                    with dve.Fori(0, NT // UJ) as jp:
                        dve.wait_ge(left_in, (ib + 1) * (16 * H))
                        dve.wait_ge(sel1_ready, ib * 2 * NT)
                        dve.wait_ge(x_out, ib * 16)
                        for u in range(UJ):
                            jt = jp * UJ + u
                            dve.wait_ge(t_ps, ib * NT + jt + (TB + 1))
                            nc.vector.tensor_scalar(mask[:, jt, :], ps_t[:, u % 2, :], 0.0, None,
                                                    ALU.is_gt).then_inc(mask_ready, 1)
                            dve.wait_ge(mask_ready, ib * NT + jt + 3)
                            first_branch(u, 0, jt, ib * 2 * NT + jt)
                    sum_branches(link, ib, 0)
                    with dve.Fori(0, NT // UJ) as jp:
                        for u in range(UJ):
                            jt = jp * UJ + u
                            first_branch(u, 1, jt, ib * 2 * NT + NT + jt)
                    sum_branches(link, ib, 1)
                    link(nc.vector.reciprocal(rec[:, :, :], num[:, :, :, D]))
                    out4 = out_w.rearrange("p (t h d) -> p t h d", t=TB, h=H)
                    out3 = out_w.rearrange("p (t c) -> p t c", t=TB)
                    link(nc.vector.tensor_tensor(out4, num[:, :, :, 0:D],
                                                 rec[:, :, :].unsqueeze(3).to_broadcast([P, TB, H, D]), ALU.mult))
                    nc.vector.tensor_tensor(out3, out3, bias_row[:, :].unsqueeze(1).to_broadcast([P, TB, C]),
                                            ALU.add).then_inc(out_ready, 1)
                    dve.wait_ge(tanh_done, ib + 1)
                    nc.vector.scalar_tensor_tensor(out=out_w, in0=th_w, scalar=1.0, in1=out_w, op0=ALU.add,
                                                   op1=ALU.mult).then_inc(silu_ready, 1)
                    dve.wait_ge(square_done, ib * (TB + 3) + TB + 1)
                    nc.vector.tensor_scalar(small[:, NORM, :], small[:, VN, :], 1e-15, None,
                                            ALU.max).then_inc(norm_ready, 1)
                    dve.wait_ge(norm_ready, ib + 1)
                    link(nc.vector.reciprocal(small[:, FACT, :], small[:, NORM, :]))
                    dve.wait_ge(square_done, (ib + 1) * (TB + 3))
                    link(nc.vector.tensor_tensor(small[:, FACT, :], small[:, FACT, :], small[:, TNORM, :], ALU.mult))
                    link(nc.vector.tensor_scalar(small[:, FACT, :], small[:, FACT, :], 0.5, None, ALU.mult))
                    dve.wait_ge(x_in, (ib + 1) * 16)
                    for i in range(TB):
                        op = nc.vector.scalar_tensor_tensor(out=xo[:, i, :], in0=out_w[:, i * C:(i + 1) * C],
                                                            scalar=small[:, FACT, i:i + 1], in1=xo[:, i, :],
                                                            op0=ALU.mult, op1=ALU.add)
                    op.then_inc(x1_ready, 1)
                    link(nc.vector.tensor_copy(small[:, NORM, :], small[:, FACT, :]))

            @block.tensor
            def _(pe):
                pe.wait_ge(zeroed, 1)

                def transposes(ib, jp, u):
                    if u % TB == 0:
                        pe.wait_ge(adj_ready, ib * (NT // TB) + (jp * 2 + (u // TB + 1)))
                    pe.wait_ge(mask_ready, ib * NT + jp * UJ + (u + 1))
                    for i in range(TB):
                        op = nc.tensor.transpose(ps_t[:, u % 2, i * P:(i + 1) * P],
                                                 adjr[:, u // TB, i, (u % TB) * P:(u % TB + 1) * P], ident[:, 0, :])
                    op.then_inc(t_ps, 1)

                def products(g, u, jt, step):
                    for branch, ready in ((0, sel0_ready), (1, sel1_ready)):
                        pe.wait_ge(ready, step + 1)
                        for h in range(HG):
                            op = nc.tensor.matmul(
                                ps_acc[0:DVH, h * 2 + branch, :],
                                values[:, jt, branch, g * HG + h, :, :].rearrange("p s v -> p (s v)"),
                                sel[:, u % 2, branch, h, :], start=False, stop=False, skip_group_check=True)
                    op.then_inc(sel_free, 1)

                def clear(group):
                    pe.wait_ge(accs_ready, group * 4)
                    for a in range(2 * HG):
                        nc.tensor.matmul(ps_acc[:, a, :], zeros[:, 0:P], zeros[:, :], start=True, stop=True,
                                         skip_group_check=True)

                def fold_groups(group):
                    pe.wait_ge(num_ready, group)
                    for a in range(2 * HG):
                        pe.wait_ge(accs_ready, group * 4 + (a + 1))
                        for i in range(TB):
                            at = (i % 2) * 4 * DV + a * DV
                            op = nc.tensor.matmul(ps_d[:, i // 2, at:at + DV], accs[0:DVH, a % 2, i * P:(i + 1) * P],
                                                  fold[:, :], start=True, stop=True)
                        op.then_inc(fold_ps, 1)

                with pe.Fori(0, NB) as ib:
                    clear(ib * 2)
                    with pe.Fori(0, NT // UJ) as jp:
                        transposes(ib, jp, 0)
                        for u in range(UJ):
                            if u + 1 < UJ:
                                transposes(ib, jp, u + 1)
                            jt = jp * UJ + u
                            products(0, u, jt, ib * 2 * NT + jt)
                    fold_groups(ib * 2)
                    clear(ib * 2 + 1)
                    with pe.Fori(0, NT // UJ) as jp:
                        for u in range(UJ):
                            jt = jp * UJ + u
                            products(1, u, jt, ib * 2 * NT + NT + jt)
                    fold_groups(ib * 2 + 1)


HM = 4
PM = 64
DI = HM * PM
S = 64
TAPS = 4
SSM_EPS = 1e-5


def mamba_layer(nc, x1, w_zdt, w_xbc, conv_w, conv_b, dt_bias, a_log, d_skip, norm_w, w_out_t, w_lin, b_lin, x2):
    N = x1.shape[0]
    NT, NB = N // P, N // BLK
    x1_tiles = x1.rearrange("(t p) c -> p t c", p=P)
    x2_tiles = x2.rearrange("(t p) c -> p t c", p=P)

    keep = ExitStack()
    with keep:
        k = Scope(nc, keep, "ssm")
        xr = k.sb("xr", [P, NT, C])
        ut = k.sb("ut", [C, N])
        wz = k.sb("wz", [C, DI + HM])
        wx = k.sb("wx", [C, DI + 2 * S])
        wc = k.sb("wc", [P, 2, C])
        cw = k.sb("cw", [P, 3, TAPS])
        cb = k.sb("cb", [P, 3])
        dskip = k.sb("dskip", [P, HM])
        ident = k.sb("ident", [P, P])
        upto = k.sb("upto", [P, P])
        after = k.sb("after", [P, P])
        dt = k.sb("dt", [P, NT, HM])
        da = k.sb("da", [P, NT, HM])
        decay = k.sb("decay", [P, 3, NT, HM])

        with ExitStack() as ctx:
            s = Scope(nc, ctx, "ssmprep")
            xn = s.sb("xn", [P, 2, TB, C])
            stats = s.sb("stats", [P, NT, 6])
            mean = s.sb("mean", [P, NT])
            var = s.sb("var", [P, NT])
            tmp = s.sb("tmp", [P, NT])
            root = s.sb("root", [P, NT])
            rstd = s.sb("rstd", [P, NT])
            ones = s.sb("ones", [P, P])
            brow = s.sb("brow", [P, C])
            dtb = s.sb("dtb", [P, HM])
            al = s.sb("al", [P, HM])
            wot = s.sb("wot", [C, DI])
            wl = s.sb("wl", [C, C])
            nw = s.sb("nw", [P, 2])
            f = s.sb("f", [P, 6, NT, HM])
            ps_t = s.ps("t", [P, 2, BLK])
            ps_d = s.ps("d", [P, BLK])
            ps_w = s.ps("w", [P, BLK])
            ps_a = s.ps("a", [P, 3, BLK])
            x_in = s.sem("x_in")
            w_in = s.sem("w_in")
            consts = s.sem("consts")
            chain_dve = s.sem("chain_dve")
            stats_done = s.sem("stats_done")
            var_ready = s.sem("var_ready")
            rooted = s.sem("rooted")
            xn_ready = s.sem("xn_ready")
            t_ps = s.sem("t_ps")
            ut_ready = s.sem("ut_ready")
            dt_ps = s.sem("dt_ps")
            wc_ps = s.sem("wc_ps")
            abs_ready = s.sem("abs_ready")
            exps = s.sem("exps")
            one_more = s.sem("one_more")
            da_ready = s.sem("da_ready")
            sums_ps = s.sem("sums_ps")

            with nc.Block() as block:
                @block.sync
                def _(sp):
                    sp.dma_start(xr[:, :, :], x1_tiles).then_inc(x_in, 16)
                    sp.dma_start(wz[:, :], w_zdt).then_inc(w_in, 16)
                    sp.dma_start(wx[:, :], w_xbc).then_inc(w_in, 16)
                    sp.dma_start(cw[:, :, :], conv_w.rearrange("(g p) k -> p g k", p=P)).then_inc(w_in, 16)
                    sp.dma_start(cb[:, :], conv_b).then_inc(w_in, 16)
                    sp.dma_start(dskip[:, :], d_skip.partition_broadcast(P)).then_inc(w_in, 16)
                    sp.dma_start(brow[:, :], b_lin.partition_broadcast(P)).then_inc(w_in, 16)
                    sp.dma_start(dtb[:, :], dt_bias.partition_broadcast(P)).then_inc(w_in, 16)
                    sp.dma_start(al[:, :], a_log.partition_broadcast(P)).then_inc(w_in, 16)
                    sp.dma_start(wot[:, :], w_out_t).then_inc(w_in, 16)
                    sp.dma_start(wl[:, :], w_lin).then_inc(w_in, 16)
                    sp.dma_start(nw[:, :], norm_w).then_inc(w_in, 16)

                @block.gpsimd
                def _(pool):
                    link = Chain(pool, consts)
                    link(nc.gpsimd.memset(ident[:, :], 0.0))
                    link(nc.gpsimd.memset(ones[:, :], 1.0))
                    link(nc.gpsimd.affine_select(out=ident[:, :], in_=ident[:, :], compare_op=ALU.not_equal,
                                                 fill=1.0, base=0, pattern=[[-1, P]], channel_multiplier=1))
                    link(nc.gpsimd.affine_select(out=upto[:, :], in_=ones[:, :], compare_op=ALU.is_ge,
                                                 fill=0.0, base=0, pattern=[[1, P]], channel_multiplier=-1))
                    link(nc.gpsimd.affine_select(out=after[:, :], in_=ones[:, :], compare_op=ALU.is_gt,
                                                 fill=0.0, base=0, pattern=[[-1, P]], channel_multiplier=1))

                @block.scalar
                def _(act):
                    act.wait_ge(var_ready, 1)
                    nc.scalar.activation(root[:, :], tmp[:, :], ACT.Sqrt).then_inc(rooted, 1)
                    with act.Fori(0, NB // 2) as pair:
                        for u in range(2):
                            b = pair * 2 + u
                            act.wait_ge(t_ps, b + 1)
                            nc.scalar.activation(ut[:, bass.ds(b * BLK, BLK)], ps_t[:, u, :],
                                                 ACT.Copy).then_inc(ut_ready, 1)
                    act.wait_ge(w_in, 16 * 11)
                    nc.scalar.activation(al[:, :], al[:, :], ACT.Exp).then_inc(exps, 1)
                    act.wait_ge(abs_ready, 1)
                    nc.scalar.activation(f[:, 2, :, :], f[:, 1, :, :], ACT.Exp, scale=-1.0).then_inc(exps, 1)
                    act.wait_ge(one_more, 1)
                    nc.scalar.activation(f[:, 4, :, :], f[:, 3, :, :], ACT.Ln).then_inc(exps, 1)
                    act.wait_ge(sums_ps, 1)
                    for i in range(3):
                        nc.scalar.activation(decay[:, i, :, :], ps_a[:, i, 0:NT * HM]
                                             .rearrange("p (t h) -> p t h", h=HM), ACT.Exp).then_inc(exps, 1)

                @block.vector
                def _(dve):
                    link = Chain(dve, chain_dve)
                    dve.wait_ge(x_in, 16)
                    with dve.Fori(0, NT) as t:
                        nc.vector.bn_stats(stats[:, t, :], xr[:, t, :]).then_inc(stats_done, 1)
                    dve.wait_ge(stats_done, NT)
                    row_statistics(nc, link, stats, mean[:, :], var[:, :], tmp[:, :])
                    nc.vector.tensor_scalar(tmp[:, :], var[:, :], LN_EPS, None, ALU.add).then_inc(var_ready, 1)
                    dve.wait_ge(rooted, 1)
                    link(nc.vector.reciprocal(rstd[:, :], root[:, :]))
                    dve.wait_ge(w_in, 16 * 11)
                    with dve.Fori(0, NB // 2) as pair:
                        for u in range(2):
                            b = pair * 2 + u
                            dve.wait_ge(t_ps, b)
                            for i in range(TB):
                                op = nc.vector.tensor_scalar(xn[:, u, i, :], xr[:, b * TB + i, :],
                                                             mean[:, bass.ds(b * TB + i, 1)],
                                                             rstd[:, bass.ds(b * TB + i, 1)],
                                                             ALU.subtract, ALU.mult)
                            op.then_inc(xn_ready, 1)
                            dve.wait_ge(xn_ready, b + 1)
                            rows = xr[:, bass.ds(b * TB, TB), :]
                            nc.vector.tensor_tensor(rows, rows, brow[:, :].unsqueeze(1).to_broadcast([P, TB, C]), ALU.add)
                    for g in range(2):
                        dve.wait_ge(wc_ps, 2)
                        link(nc.vector.tensor_scalar(wc[:, g, :], ps_w[:, g * C:(g + 1) * C], nw[:, g:g + 1], None,
                                                     ALU.mult))
                    link(nc.vector.tensor_scalar(cw[:, :, :], cw[:, :, :], 0.5, None, ALU.mult))
                    link(nc.vector.tensor_scalar(cb[:, :], cb[:, :], 0.5, None, ALU.mult))
                    v, a, e, w, lw, z = (f[:, i, :, :] for i in range(6))
                    dve.wait_ge(dt_ps, NT)
                    link(nc.vector.tensor_tensor(v, ps_d[:, 0:NT * HM].rearrange("p (t h) -> p t h", h=HM),
                                                 dtb[:, :].unsqueeze(1).to_broadcast([P, NT, HM]), ALU.add))
                    link(nc.vector.tensor_scalar(a, v, -1.0, None, ALU.mult))
                    nc.vector.tensor_tensor(a, a, v, ALU.max).then_inc(abs_ready, 1)
                    dve.wait_ge(exps, 2)
                    nc.vector.tensor_scalar(w, e, 1.0, None, ALU.add).then_inc(one_more, 1)
                    dve.wait_ge(one_more, 1)
                    link(nc.vector.tensor_scalar(a, w, -1.0, None, ALU.add))
                    link(nc.vector.tensor_scalar(z, a, 0.0, None, ALU.is_equal))
                    link(nc.vector.tensor_tensor(a, a, z, ALU.add))
                    dve.wait_ge(exps, 3)
                    link(nc.vector.tensor_tensor(lw, lw, z, ALU.add))
                    link(nc.vector.reciprocal(a, a))
                    link(nc.vector.tensor_tensor(lw, lw, a, ALU.mult))
                    link(nc.vector.tensor_tensor(lw, lw, e, ALU.mult))
                    link(nc.vector.tensor_scalar(v, v, 0.0, None, ALU.max))
                    link(nc.vector.tensor_tensor(dt[:, :, :], v, lw, ALU.add))
                    link(nc.vector.tensor_scalar(al[:, :], al[:, :], -1.0, None, ALU.mult))
                    nc.vector.tensor_tensor(da[:, :, :], dt[:, :, :], al[:, :].unsqueeze(1).to_broadcast([P, NT, HM]),
                                            ALU.mult).then_inc(da_ready, 1)

                @block.tensor
                def _(pe):
                    pe.wait_ge(consts, 5)
                    pe.wait_ge(w_in, 16 * 11)
                    for g in range(2):
                        nc.tensor.matmul(ps_w[:, g * C:(g + 1) * C], wot[:, g * P:(g + 1) * P], wl[:, :],
                                         start=True, stop=True).then_inc(wc_ps, 1)
                    with pe.Fori(0, NB // 2) as pair:
                        for u in range(2):
                            b = pair * 2 + u
                            pe.wait_ge(xn_ready, b + 1)
                            pe.wait_ge(ut_ready, b)
                            for i in range(TB):
                                op = nc.tensor.transpose(ps_t[:, u, i * P:(i + 1) * P], xn[:, u, i, :], ident[:, :])
                            op.then_inc(t_ps, 1)
                    pe.wait_ge(ut_ready, NB)
                    for t in range(NT):
                        nc.tensor.matmul(ps_d[:, t * HM:(t + 1) * HM], ut[:, t * P:(t + 1) * P], wz[:, DI:DI + HM],
                                         start=True, stop=True).then_inc(dt_ps, 1)
                    pe.wait_ge(da_ready, 1)
                    flat = da[:, :, :].rearrange("p t h -> p (t h)")
                    for i, sums in enumerate((upto, after, ones)):
                        op = nc.tensor.matmul(ps_a[:, i, 0:NT * HM], sums[:, :], flat, start=True, stop=True)
                    op.then_inc(sums_ps, 1)

        with ExitStack() as ctx:
            s = Scope(nc, ctx, "scan")
            ub = s.sb("ub", [C, 2, BLK])
            raw = s.sb("raw", [P, 3, TAPS - 1 + BLK])
            cv = s.sb("cv", [P, 3, BLK])
            th = s.sb("th", [P, 3, BLK])
            xs = s.sb("xs", [P, 2, 2, BLK])
            bt = s.sb("bt", [S, 2, BLK])
            ct = s.sb("ct", [S, 2, BLK])
            dal = s.sb("dal", [P, 2, HM, P])
            ex = s.sb("ex", [P, 2, HM, P])
            gm = s.sb("gm", [P, 2, P])
            mx = s.sb("mx", [P, 2, HM, P])
            xrow = s.sb("xrow", [P, 2, DI + S])
            xdt = s.sb("xdt", [P, 2, DI])
            xdec = s.sb("xdec", [P, 2, DI])
            xd = s.sb("xd", [P, 2, DI])
            hs = s.sb("hs", [S, 2, DI])
            hd = s.sb("hd", [S, DI])
            zt = s.sb("zt", [P, 2, DI])
            zs = s.sb("zs", [P, 2, DI])
            y = s.sb("y", [P, 2, DI])
            yt = s.sb("yt", [P, 2, DI])
            yo = s.sb("yo", [P, NT, C])
            ss = s.sb("ss", [P, NT])
            junk = s.sb("junk", [P, DI])
            ps_e = s.ps("e", [P, BLK])
            ps_g = s.ps("g", [P, BLK])
            ps_x = s.ps("x", [P, BLK])
            ps_y = s.ps("y", [P, BLK])
            ps_s = s.ps("s", [P, BLK])
            ps_z = s.ps("z", [P, BLK])
            ps_r = s.ps("r", [P, 2, BLK])
            names = ("ub_ready raw_ps raw_ready conv_done tanh_done xs_ready seg_ps dal_ready exp_done g_ps x_ps "
                     "gm_ready mx_ready xrow_ready xdt_ready xdec_ready xd_ready yd_ps st_ps hd_ready hs_ready "
                     "z_ps zt_done zs_ready y_ready square_done yt_ps yt_ready out_ps yo_ready halo_done chain_dve "
                     "cleared rooted var_ready x_out").split()
            sem = {n: s.sem(n) for n in names}

            with nc.Block() as block:
                def chunks(b, fn):
                    for c in range(TB):
                        fn(c, b * TB + c)

                @block.gpsimd
                def _(pool):
                    nc.gpsimd.memset(raw[:, :, :], 0.0).then_inc(sem["cleared"], 1)
                    nc.gpsimd.memset(hs[:, :, :], 0.0).then_inc(sem["cleared"], 1)
                    with pool.Fori(0, NB // 2) as pair:
                        for u in range(2):
                            b = pair * 2 + u
                            pool.wait_ge(sem["z_ps"], b * TB)
                            nc.gpsimd.tensor_copy(ub[:, u, :], ut[:, bass.ds(b * BLK, BLK)]).then_inc(sem["ub_ready"], 1)
                            for c in range(TB):
                                q, p = b * TB + c, c % 2
                                pool.wait_ge(sem["seg_ps"], q)
                                nc.gpsimd.tensor_tensor(dal[:, p, :, :],
                                                        da[:, q, :].unsqueeze(2).to_broadcast([P, HM, P]),
                                                        after[:, :].unsqueeze(1).to_broadcast([P, HM, P]),
                                                        ALU.mult).then_inc(sem["dal_ready"], 1)

                                def per_head(v):
                                    return v.unsqueeze(2).to_broadcast([P, HM, PM])

                                def heads(v):
                                    return v.rearrange("p (h d) -> p h d", h=HM)

                                pool.wait_ge(sem["xrow_ready"], q + 1)
                                rows = heads(xrow[:, p, 0:DI])
                                pool.wait_ge(sem["st_ps"], q)
                                nc.gpsimd.tensor_tensor(heads(xdt[:, p, :]), rows, per_head(dt[:, q, :]),
                                                        ALU.mult).then_inc(sem["xdt_ready"], 1)
                                nc.gpsimd.tensor_tensor(heads(xd[:, p, :]), rows, per_head(dskip[:, :]),
                                                        ALU.mult).then_inc(sem["xd_ready"], 1)
                                pool.wait_ge(sem["xdt_ready"], q + 1)
                                nc.gpsimd.tensor_tensor(heads(xdec[:, p, :]), heads(xdt[:, p, :]),
                                                        per_head(decay[:, 1, q, :]),
                                                        ALU.mult).then_inc(sem["xdec_ready"], 1)
                                pool.wait_ge(sem["hs_ready"], q)
                                nc.gpsimd.tensor_tensor(heads(hd[:, :]), heads(hs[:, p, :]),
                                                        decay[0:S, 2, q, :].unsqueeze(2).to_broadcast([S, HM, PM]),
                                                        ALU.mult).then_inc(sem["hd_ready"], 1)

                @block.scalar
                def _(act):
                    act.wait_ge(sem["cleared"], 2)
                    with act.Fori(0, NB // 2) as pair:
                        for u in range(2):
                            b = pair * 2 + u
                            act.wait_ge(sem["halo_done"], b)
                            for g in range(3):
                                act.wait_ge(sem["raw_ps"], b * 3 + (g + 1))
                                nc.scalar.activation(raw[:, g, TAPS - 1:], ps_r[:, g % 2, :],
                                                     ACT.Copy).then_inc(sem["raw_ready"], 1)
                            for g in range(3):
                                act.wait_ge(sem["conv_done"], b * 3 + (g + 1))
                                nc.scalar.activation(th[:, g, :], cv[:, g, :], ACT.Tanh).then_inc(sem["tanh_done"], 1)
                            for c in range(TB):
                                q, p = b * TB + c, c % 2
                                act.wait_ge(sem["seg_ps"], q + 1)
                                act.wait_ge(sem["mx_ready"], q)
                                nc.scalar.activation(ex[:, p, :, :].rearrange("p h l -> p (h l)"), ps_e[:, :],
                                                     ACT.Exp).then_inc(sem["exp_done"], 1)
                                act.wait_ge(sem["x_ps"], q + 1)
                                nc.scalar.activation(xrow[:, p, :], ps_x[:, 0:DI + S],
                                                     ACT.Copy).then_inc(sem["xrow_ready"], 1)
                                act.wait_ge(sem["z_ps"], q + 1)
                                nc.scalar.activation(zt[:, p, :], ps_z[:, 0:DI], ACT.Tanh,
                                                     scale=0.5).then_inc(sem["zt_done"], 1)
                                act.wait_ge(sem["y_ready"], q + 1)
                                nc.scalar.activation(junk[:, :], y[:, p, :], ACT.Square,
                                                     accum_out=ss[:, bass.ds(q, 1)]).then_inc(sem["square_done"], 1)
                                act.wait_ge(sem["yt_ps"], q + 1)
                                nc.scalar.activation(yt[:, p, :], ps_z[:, DI:2 * DI], ACT.Copy).then_inc(sem["yt_ready"], 1)
                                act.wait_ge(sem["out_ps"], q + 1)
                                nc.scalar.activation(yo[:, q, :], ps_x[:, DI + S:DI + S + C], ACT.Copy).then_inc(sem["yo_ready"], 1)
                    act.wait_ge(sem["var_ready"], 1)
                    nc.scalar.activation(ss[:, :], ss[:, :], ACT.Sqrt).then_inc(sem["rooted"], 1)

                @block.vector
                def _(dve):
                    per_block = 3 * (TAPS - 1) + 1 + 3 * TB
                    dve.wait_ge(sem["cleared"], 2)

                    def heads(v):
                        return v.rearrange("p (h d) -> p h d", h=HM)

                    with dve.Fori(0, NB // 2) as pair:
                        for u in range(2):
                            b = pair * 2 + u
                            link = Chain(dve, sem["chain_dve"], b * per_block)
                            for g in range(3):
                                dve.wait_ge(sem["raw_ready"], b * 3 + (g + 1))
                                link(nc.vector.tensor_scalar(cv[:, g, :], raw[:, g, 0:BLK], cw[:, g, 0:1], cb[:, g:g + 1],
                                                             ALU.mult, ALU.add))
                                for j in range(1, TAPS):
                                    op = nc.vector.scalar_tensor_tensor(out=cv[:, g, :], in0=raw[:, g, j:j + BLK],
                                                                        scalar=cw[:, g, j:j + 1], in1=cv[:, g, :],
                                                                        op0=ALU.mult, op1=ALU.add)
                                    if j < TAPS - 1:
                                        link(op)
                                    else:
                                        op.then_inc(sem["conv_done"], 1)
                            link(nc.vector.tensor_copy(raw[:, :, 0:TAPS - 1], raw[:, :, BLK:BLK + TAPS - 1]))
                            dve.sem_inc(sem["halo_done"], 1)
                            dve.wait_ge(sem["yd_ps"], b * TB)
                            for g in range(3):
                                dve.wait_ge(sem["tanh_done"], b * 3 + (g + 1))
                                if g < 2:
                                    nc.vector.scalar_tensor_tensor(out=xs[:, u, g, :], in0=th[:, g, :], scalar=1.0,
                                                                   in1=cv[:, g, :], op0=ALU.add, op1=ALU.mult)
                                else:
                                    for i, to in enumerate((bt, ct)):
                                        rows = slice(i * S, (i + 1) * S)
                                        op = nc.vector.scalar_tensor_tensor(out=to[:, u, :], in0=th[rows, g, :], scalar=1.0,
                                                                            in1=cv[rows, g, :], op0=ALU.add, op1=ALU.mult)
                                    op.then_inc(sem["xs_ready"], 1)
                            for c in range(TB):
                                q, p = b * TB + c, c % 2
                                dve.wait_ge(sem["g_ps"], q + 1)
                                nc.vector.tensor_tensor(gm[:, p, :], ps_g[:, 0:P], upto[:, :],
                                                        ALU.mult).then_inc(sem["gm_ready"], 1)
                                dve.wait_ge(sem["gm_ready"], q + 1)
                                dve.wait_ge(sem["exp_done"], q + 1)
                                dve.wait_ge(sem["yd_ps"], q)
                                nc.vector.tensor_tensor(mx[:, p, :, :], ex[:, p, :, :],
                                                        gm[:, p, :].unsqueeze(1).to_broadcast([P, HM, P]),
                                                        ALU.mult).then_inc(sem["mx_ready"], 1)
                                dve.wait_ge(sem["st_ps"], q + 1)
                                dve.wait_ge(sem["hd_ready"], q + 1)
                                nc.vector.tensor_tensor(hs[:, 1 - p, :], hd[:, :], ps_s[0:S, 0:DI],
                                                        ALU.add).then_inc(sem["hs_ready"], 1)
                                dve.wait_ge(sem["zt_done"], q + 1)
                                nc.vector.scalar_tensor_tensor(out=zs[:, p, :], in0=zt[:, p, :], scalar=1.0,
                                                               in1=ps_z[:, 0:DI], op0=ALU.add,
                                                               op1=ALU.mult).then_inc(sem["zs_ready"], 1)
                                dve.wait_ge(sem["yd_ps"], q + 1)
                                dve.wait_ge(sem["yt_ps"], q)
                                yy = y[:, p, :]
                                link(nc.vector.tensor_tensor(heads(yy), heads(ps_y[:, DI:2 * DI]),
                                                             decay[:, 0, q, :].unsqueeze(2).to_broadcast([P, HM, PM]),
                                                             ALU.mult))
                                link(nc.vector.tensor_tensor(yy, yy, ps_y[:, 0:DI], ALU.add))
                                dve.wait_ge(sem["xd_ready"], q + 1)
                                link(nc.vector.tensor_tensor(yy, yy, xd[:, p, :], ALU.add))
                                dve.wait_ge(sem["zs_ready"], q + 1)
                                nc.vector.tensor_tensor(yy, yy, zs[:, p, :], ALU.mult).then_inc(sem["y_ready"], 1)
                    link = Chain(dve, sem["chain_dve"], NB * per_block)
                    dve.wait_ge(sem["square_done"], NT)
                    nc.vector.tensor_scalar(ss[:, :], ss[:, :], 0.25 / DI, SSM_EPS, ALU.mult,
                                            ALU.add).then_inc(sem["var_ready"], 1)
                    dve.wait_ge(sem["rooted"], 1)
                    link(nc.vector.reciprocal(ss[:, :], ss[:, :]))
                    link(nc.vector.tensor_scalar(ss[:, :], ss[:, :], 0.5, None, ALU.mult))
                    dve.wait_ge(sem["yo_ready"], NT)
                    with dve.Fori(0, NT) as t:
                        nc.vector.scalar_tensor_tensor(out=xr[:, t, :], in0=yo[:, t, :], scalar=ss[:, bass.ds(t, 1)],
                                                       in1=xr[:, t, :], op0=ALU.mult,
                                                       op1=ALU.add).then_inc(sem["x_out"], 1)

                @block.tensor
                def _(pe):
                    with pe.Fori(0, NB // 2) as pair:
                        for u in range(2):
                            b = pair * 2 + u
                            pe.wait_ge(sem["ub_ready"], b + 1)
                            for g in range(3):
                                pe.wait_ge(sem["raw_ready"], b * 3 + max(g - 1, 0))
                                nc.tensor.matmul(ps_r[:, g % 2, :], wx[:, g * P:(g + 1) * P], ub[:, u, :], start=True,
                                                 stop=True).then_inc(sem["raw_ps"], 1)
                            for c in range(TB):
                                q, p = b * TB + c, c % 2
                                cols = slice(c * P, (c + 1) * P)
                                pe.wait_ge(sem["zs_ready"], q)
                                nc.tensor.matmul(ps_z[:, 0:DI], ub[:, u, cols], wz[:, 0:DI], start=True,
                                                 stop=True).then_inc(sem["z_ps"], 1)
                                pe.wait_ge(sem["dal_ready"], q + 1)
                                pe.wait_ge(sem["exp_done"], q)
                                for h in range(HM):
                                    op = nc.tensor.matmul(ps_e[:, h * P:(h + 1) * P], dal[:, p, h, :], upto[:, :],
                                                          start=True, stop=True)
                                op.then_inc(sem["seg_ps"], 1)
                                if c == 0:
                                    pe.wait_ge(sem["xs_ready"], b + 1)
                                pe.wait_ge(sem["gm_ready"], q)
                                nc.tensor.matmul(ps_g[:, 0:P], bt[:, u, cols], ct[:, u, cols], start=True,
                                                 stop=True).then_inc(sem["g_ps"], 1)
                                pe.wait_ge(sem["yo_ready"], q)
                                for g in range(2):
                                    nc.tensor.transpose(ps_x[:, g * P:(g + 1) * P], xs[:, u, g, cols], ident[:, :])
                                nc.tensor.transpose(ps_x[:, DI:DI + S], bt[:, u, cols],
                                                    ident[0:S, 0:S]).then_inc(sem["x_ps"], 1)
                                pe.wait_ge(sem["y_ready"], q)
                                pe.wait_ge(sem["hs_ready"], q)
                                nc.tensor.matmul(ps_y[:, DI:2 * DI], ct[:, u, cols], hs[:, p, :], start=True,
                                                 stop=True)
                                pe.wait_ge(sem["xdec_ready"], q + 1)
                                nc.tensor.matmul(ps_s[0:S, 0:DI], xrow[:, p, DI:DI + S], xdec[:, p, :], start=True,
                                                 stop=True).then_inc(sem["st_ps"], 1)
                                pe.wait_ge(sem["mx_ready"], q + 1)
                                for h in range(HM):
                                    op = nc.tensor.matmul(ps_y[:, h * PM:(h + 1) * PM], mx[:, p, h, :],
                                                          xdt[:, p, h * PM:(h + 1) * PM], start=True, stop=True)
                                op.then_inc(sem["yd_ps"], 1)
                                pe.wait_ge(sem["y_ready"], q + 1)
                                for g in range(2):
                                    op = nc.tensor.transpose(ps_z[:, DI + g * P:DI + (g + 1) * P],
                                                             y[:, p, g * P:(g + 1) * P], ident[:, :])
                                op.then_inc(sem["yt_ps"], 1)
                                pe.wait_ge(sem["yt_ready"], q + 1)
                                for g in range(2):
                                    op = nc.tensor.matmul(ps_x[:, DI + S:DI + S + C], yt[:, p, g * P:(g + 1) * P], wc[:, g, :],
                                                          start=(g == 0), stop=(g == 1))
                                op.then_inc(sem["out_ps"], 1)

                @block.sync
                def _(sp):
                    sp.wait_ge(sem["x_out"], NT)
                    sp.dma_start(x2_tiles, xr[:, :, :]).then_inc(sem["x_out"], 16)
                    sp.wait_ge(sem["x_out"], NT + 16)


E = 8
TOP = 2
HID = 341
GATE_EPS = 1e-9
HID_TILES = [(h0, min(P, HID - h0)) for h0 in range(0, HID, P)]


def propagate_layer(nc, x2, adj, w_row, router_t, w1_t, w3_t, w2_t, out):
    N = x2.shape[0]
    NT, NB = N // P, N // BLK
    x2_tiles = x2.rearrange("(t p) c -> p t c", p=P)
    out_tiles = out.rearrange("(t p) c -> p t c", p=P)
    adj_rows = adj.rearrange("(t p) c -> p t c", p=P)

    keep = ExitStack()
    with keep:
        k = Scope(nc, keep, "gnn")
        xr = k.sb("xr", [P, NT, C])
        hid = k.sb("hid", [P, NT, C])
        ident = k.sb("ident", [P, P])
        eye8 = k.sb("eye8", [P, E])
        rt = k.sb("rt", [C, E])
        w1 = k.sb("w1", [C, E, HID])
        w3 = k.sb("w3", [C, E, HID])
        w2 = k.sb("w2", [P, len(HID_TILES), E, C])

        with ExitStack() as ctx:
            s = Scope(nc, ctx, "gnnprep")
            stats = s.sb("stats", [P, NT, 6])
            mean = s.sb("mean", [P, NT])
            var = s.sb("var", [P, NT])
            tmp = s.sb("tmp", [P, NT])
            root = s.sb("root", [P, NT])
            rstd = s.sb("rstd", [P, NT])
            wrow = s.sb("wrow", [P, C])
            count8 = s.sb("count8", [P, E], mybir.dt.int32)
            x_in = s.sem("x_in")
            w_in = s.sem("w_in")
            consts = s.sem("consts")
            chain_dve = s.sem("chain_dve")
            stats_done = s.sem("stats_done")
            var_ready = s.sem("var_ready")
            rooted = s.sem("rooted")

            with nc.Block() as block:
                @block.sync
                def _(sp):
                    sp.dma_start(xr[:, :, :], x2_tiles).then_inc(x_in, 16)
                    sp.dma_start(wrow[:, :], w_row.partition_broadcast(P)).then_inc(w_in, 16)
                    sp.dma_start(rt[:, :], router_t).then_inc(w_in, 16)
                    sp.dma_start(w1[:, :, :], w1_t).then_inc(w_in, 16)
                    sp.dma_start(w3[:, :, :], w3_t).then_inc(w_in, 16)
                    for i, (h0, hn) in enumerate(HID_TILES):
                        sp.dma_start(w2[0:hn, i, :, :], w2_t[h0:h0 + hn, :, :]).then_inc(w_in, 16)
                    sp.wait_ge(w_in, 16 * (4 + len(HID_TILES)))

                @block.gpsimd
                def _(pool):
                    link = Chain(pool, consts)
                    link(nc.gpsimd.memset(ident[:, :], 0.0))
                    link(nc.gpsimd.affine_select(out=ident[:, :], in_=ident[:, :], compare_op=ALU.not_equal,
                                                 fill=1.0, base=0, pattern=[[-1, P]], channel_multiplier=1))
                    link(nc.gpsimd.iota(count8[:, :], pattern=[[1, E]], base=0, channel_multiplier=0))
                    link(nc.gpsimd.tensor_copy(eye8[:, :], count8[:, :]))

                @block.scalar
                def _(act):
                    act.wait_ge(var_ready, 1)
                    nc.scalar.activation(root[:, :], tmp[:, :], ACT.Sqrt).then_inc(rooted, 1)

                @block.vector
                def _(dve):
                    link = Chain(dve, chain_dve)
                    dve.wait_ge(x_in, 16)
                    with dve.Fori(0, NT) as t:
                        nc.vector.bn_stats(stats[:, t, :], xr[:, t, :]).then_inc(stats_done, 1)
                    dve.wait_ge(stats_done, NT)
                    row_statistics(nc, link, stats, mean[:, :], var[:, :], tmp[:, :])
                    nc.vector.tensor_scalar(tmp[:, :], var[:, :], LN_EPS, None, ALU.add).then_inc(var_ready, 1)
                    dve.wait_ge(rooted, 1)
                    link(nc.vector.reciprocal(rstd[:, :], root[:, :]))
                    dve.wait_ge(w_in, 16 * (4 + len(HID_TILES)))
                    with dve.Fori(0, NB) as b:
                        step = Chain(dve, chain_dve, b * 2 + link.count)
                        for i in range(TB):
                            op = nc.vector.tensor_scalar(hid[:, b * TB + i, :], xr[:, b * TB + i, :],
                                                         mean[:, bass.ds(b * TB + i, 1)],
                                                         rstd[:, bass.ds(b * TB + i, 1)], ALU.subtract, ALU.mult)
                        step(op)
                        rows = hid[:, bass.ds(b * TB, TB), :]
                        step(nc.vector.tensor_tensor(rows, rows, wrow[:, :].unsqueeze(1).to_broadcast([P, TB, C]),
                                                     ALU.mult))

        with ExitStack() as ctx:
            s = Scope(nc, ctx, "sweep")
            adjr = s.sb("adjr", [P, 2, TB, BLK])
            adjt = s.sb("adjt", [P, 2, BLK])
            acct = s.sb("acct", [C, BLK])
            xo = s.sb("xo", [P, 2, TB, C])
            xn = s.sb("xn", [P, TB, C])
            xt = s.sb("xt", [C, BLK])
            stats = s.sb("stats", [P, TB, 6])
            mv = s.sb("mv", [P, TB, 2])
            ve = s.sb("ve", [P, TB])
            rstd = s.sb("rstd", [P, TB])
            lg = s.sb("lg", [P, TB, E])
            pr = s.sb("pr", [P, TB, E])
            hot = s.sb("hot", [P, TB, E])
            gate = s.sb("gate", [P, TB, E])
            m4 = s.sb("m4", [P, TB])
            top = s.sb("top", [P, TB, 8])
            topi = s.sb("topi", [P, TB, 8], UINT32)
            topf = s.sb("topf", [P, TB, 8])
            wk = s.sb("wk", [P, TB, TOP])
            th = s.sb("th", [P, 2, BLK])
            pa = s.sb("pa", [P, 2, BLK])
            hh = s.sb("hh", [P, 2, BLK])
            ps_acc = s.ps("acc", [P, BLK])
            ps_h = s.ps("h", [P, 4, BLK])
            ps_m = s.ps("m", [P, BLK])
            ps_y = s.ps("y", [P, 2, BLK])
            adj_in = [s.sem(f"adj_in{u}") for u in range(2)]
            names = ("t_ps mm_done acct_ready back_ps x3_ready ve_ready rooted xn_ready xt_ps xt_ready "
                     "router_ps lg_ready exp_done gate_ready pa_ready h_ps th_ready hh_ready y_ps y_used carried chain_dve").split()
            sem = {n: s.sem(n) for n in names}
            x_out = [s.sem(f"x_out{u}") for u in range(2)]
            adjt_ready = [s.sem(f"adjt_ready{u}") for u in range(2)]
            NU = E * len(HID_TILES)
            NCH = NT // TB

            with nc.Block() as block:
                @block.sync
                def _(sp):
                    with sp.Fori(0, NB // 2) as pair:
                        for v in range(2):
                            ib = pair * 2 + v
                            with sp.Fori(0, NCH // 2) as cp:
                                for u in range(2):
                                    sp.wait_ge(sem["mm_done"], ib * NT + (cp * 2 + u) * TB)
                                    sp.dma_start(adjr[:, u, :, :],
                                                 adj_rows[:, bass.ds(ib * TB, TB), bass.ds((cp * 2 + u) * BLK, BLK)]
                                                 ).then_inc(adj_in[u], 16)

                @block.gpsimd
                def _(pool):
                    pool.sem_inc(sem["mm_done"], TB)
                    with pool.Fori(0, NB // 2) as pair:
                        for v in range(2):
                            ib = pair * 2 + v
                            pool.wait_ge(sem["y_used"], (ib + 1) * E)
                            pool.dma_start(out_tiles[:, bass.ds(ib * TB, TB), :], xo[:, v, :, :]).then_inc(x_out[v], 16)
                    for v in range(2):
                        pool.wait_ge(x_out[v], 16 * (NB // 2))

                @block.scalar
                def _(act):
                    with act.Fori(0, NB // 2) as pair:
                        for v in range(2):
                            ib = pair * 2 + v
                            for j in range(1, NT, 2):
                                act.wait_ge(sem["t_ps"], ib * NT + (j + 1))
                                nc.scalar.activation(adjt[:, 1, :], ps_h[:, 1, :], ACT.Copy).then_inc(adjt_ready[1], 1)
                            act.wait_ge(sem["mm_done"], (ib + 1) * NT + TB)
                            nc.scalar.activation(acct[:, :], ps_acc[:, :], ACT.Copy).then_inc(sem["acct_ready"], 1)
                            act.wait_ge(sem["ve_ready"], ib + 1)
                            nc.scalar.activation(ve[:, :], ve[:, :], ACT.Sqrt).then_inc(sem["rooted"], 1)
                            act.wait_ge(sem["xt_ps"], ib + 1)
                            nc.scalar.activation(xt[:, :], ps_m[:, :], ACT.Copy).then_inc(sem["xt_ready"], 1)
                            act.wait_ge(sem["lg_ready"], ib + 1)
                            nc.scalar.activation(pr[:, :, :], lg[:, :, :], ACT.Exp).then_inc(sem["exp_done"], 1)
                            for n in range(NU):
                                h0, hn = HID_TILES[n % len(HID_TILES)]
                                act.wait_ge(sem["h_ps"], ib * NU + (n + 1))
                                nc.scalar.activation(th[0:hn, n % 2, :], ps_h[0:hn, 2 * (n % 2), :], ACT.Tanh,
                                                     scale=0.5).then_inc(sem["th_ready"], 1)

                @block.vector
                def _(dve):
                    per_block = 27

                    def carry():
                        dve.sem_inc(sem["carried"], 1)

                    with dve.Fori(0, NB // 2) as pair:
                        for v in range(2):
                            ib = pair * 2 + v
                            link = Chain(dve, sem["chain_dve"], ib * per_block)
                            for j in range(0, NT, 2):
                                dve.wait_ge(sem["t_ps"], ib * NT + (j + 1))
                                nc.vector.tensor_copy(adjt[:, 0, :], ps_h[:, 0, :]).then_inc(adjt_ready[0], 1)
                            x3 = xo[:, v, :, :]
                            dve.wait_ge(x_out[v], pair * 16)
                            dve.wait_ge(sem["back_ps"], ib + 1)
                            nc.vector.tensor_tensor(x3, xr[:, bass.ds(ib * TB, TB), :],
                                                    ps_m[:, :].rearrange("p (t c) -> p t c", t=TB),
                                                    ALU.add).then_inc(sem["x3_ready"], 1)
                            dve.wait_ge(sem["x3_ready"], ib + 1)
                            for i in range(TB):
                                op = nc.vector.bn_stats(stats[:, i, :], x3[:, i, :])
                            link(op)
                            carry()
                            for i in range(TB):
                                op = nc.vector.bn_aggr(mv[:, i, :], stats[:, i, :])
                            link(op)
                            nc.vector.tensor_scalar(ve[:, :], mv[:, :, 1], LN_EPS, None, ALU.add).then_inc(sem["ve_ready"], 1)
                            dve.wait_ge(sem["rooted"], ib + 1)
                            link(nc.vector.reciprocal(rstd[:, :], ve[:, :]))
                            for i in range(TB):
                                op = nc.vector.tensor_scalar(xn[:, i, :], x3[:, i, :], mv[:, i, 0:1], rstd[:, i:i + 1],
                                                             ALU.subtract, ALU.mult)
                            op.then_inc(sem["xn_ready"], 1)
                            dve.wait_ge(sem["router_ps"], ib + 1)
                            link(nc.vector.tensor_scalar(lg[:, :, :], ps_m[:, 0:TB * E].rearrange("p (t e) -> p t e", e=E),
                                                         1.0, None, ALU.mult))
                            link(nc.vector.tensor_reduce(m4[:, :], lg[:, :, :], AX.X, ALU.max))
                            nc.vector.tensor_tensor(lg[:, :, :], lg[:, :, :], m4[:, :].unsqueeze(2).to_broadcast([P, TB, E]),
                                                    ALU.subtract).then_inc(sem["lg_ready"], 1)
                            dve.wait_ge(sem["exp_done"], ib + 1)
                            link(nc.vector.tensor_reduce(m4[:, :], pr[:, :, :], AX.X, ALU.add))
                            link(nc.vector.reciprocal(m4[:, :], m4[:, :]))
                            link(nc.vector.tensor_tensor(pr[:, :, :], pr[:, :, :], m4[:, :].unsqueeze(2).to_broadcast([P, TB, E]),
                                                         ALU.mult))
                            for i in range(TB):
                                carry()
                                link(nc.vector.max(top[:, i, :], pr[:, i, :]))
                                carry()
                                link(nc.vector.max_index(topi[:, i, :], top[:, i, :], pr[:, i, :]))
                            link(nc.vector.tensor_copy(topf[:, :, :], topi[:, :, :]))
                            link(nc.vector.tensor_tensor(m4[:, :], top[:, :, 0], top[:, :, 1], ALU.add))
                            link(nc.vector.tensor_scalar(m4[:, :], m4[:, :], GATE_EPS, None, ALU.add))
                            link(nc.vector.reciprocal(m4[:, :], m4[:, :]))
                            link(nc.vector.tensor_scalar(m4[:, :], m4[:, :], 0.5, None, ALU.mult))
                            link(nc.vector.tensor_tensor(wk[:, :, :], top[:, :, 0:TOP],
                                                         m4[:, :].unsqueeze(2).to_broadcast([P, TB, TOP]), ALU.mult))
                            places = eye8[:, :].unsqueeze(1).to_broadcast([P, TB, E])
                            for r, to in enumerate((gate, hot)):
                                link(nc.vector.tensor_tensor(to[:, :, :], places,
                                                             topf[:, :, r:r + 1].to_broadcast([P, TB, E]), ALU.is_equal))
                                link(nc.vector.tensor_tensor(to[:, :, :], to[:, :, :],
                                                             wk[:, :, r:r + 1].to_broadcast([P, TB, E]), ALU.mult))
                            link(nc.vector.tensor_tensor(gate[:, :, :], gate[:, :, :], hot[:, :, :], ALU.add))

                            def add_expert(e):
                                dve.wait_ge(sem["y_ps"], ib * E + (e + 1))
                                if e > 0:
                                    dve.wait_ge(sem["y_used"], ib * E + e)
                                for i in range(TB):
                                    op = nc.vector.scalar_tensor_tensor(
                                        out=x3[:, i, :], in0=ps_y[:, e % 2, i * C:(i + 1) * C],
                                        scalar=gate[:, i, e:e + 1], in1=x3[:, i, :], op0=ALU.mult, op1=ALU.add)
                                op.then_inc(sem["y_used"], 1)

                            for n in range(NU):
                                h0, hn = HID_TILES[n % len(HID_TILES)]
                                dve.wait_ge(sem["th_ready"], ib * NU + (n + 1))
                                dve.wait_ge(sem["hh_ready"], ib * NU + n)
                                nc.vector.scalar_tensor_tensor(out=pa[0:hn, n % 2, :], in0=th[0:hn, n % 2, :], scalar=1.0,
                                                               in1=ps_h[0:hn, 2 * (n % 2), :], op0=ALU.add,
                                                               op1=ALU.mult).then_inc(sem["pa_ready"], 1)
                                dve.wait_ge(sem["pa_ready"], ib * NU + (n + 1))
                                nc.vector.tensor_tensor(hh[0:hn, n % 2, :], pa[0:hn, n % 2, :],
                                                        ps_h[0:hn, 2 * (n % 2) + 1, :], ALU.mult).then_inc(sem["hh_ready"], 1)
                                if n >= 4 and (n - 4) % 3 == 0:
                                    add_expert((n - 4) // 3)
                            add_expert(E - 1)
                            assert link.ops == per_block, link.ops

                @block.tensor
                def _(pe):
                    with pe.Fori(0, NB // 2) as pair:
                        for v in range(2):
                            ib = pair * 2 + v

                            def transposes(j):
                                u = (j // TB) % 2
                                if j % TB == 0:
                                    pe.wait_ge(adj_in[u], ib * (NCH // 2 * 16) + 16 * (j // (2 * TB) + 1))
                                if j >= 2:
                                    pe.wait_ge(adjt_ready[j % 2], ib * (NT // 2) + j // 2)
                                for i in range(TB):
                                    op = nc.tensor.transpose(ps_h[:, j % 2, i * P:(i + 1) * P],
                                                             adjr[:, u, i, (j % TB) * P:(j % TB + 1) * P], ident[:, :])
                                op.then_inc(sem["t_ps"], 1)

                            pe.wait_ge(sem["hh_ready"], ib * NU)
                            transposes(0)
                            for j in range(NT):
                                if j + 1 < NT:
                                    transposes(j + 1)
                                pe.wait_ge(adjt_ready[j % 2], ib * (NT // 2) + (j // 2 + 1))
                                nc.tensor.matmul(ps_acc[:, :], hid[:, j, :], adjt[:, j % 2, :], start=(j == 0),
                                                 stop=(j == NT - 1)).then_inc(sem["mm_done"], 1)
                            pe.wait_ge(sem["acct_ready"], ib + 1)
                            for i in range(TB):
                                op = nc.tensor.transpose(ps_m[:, i * C:(i + 1) * C], acct[:, i * P:(i + 1) * P], ident[:, :])
                            op.then_inc(sem["back_ps"], 1)
                            pe.wait_ge(sem["xn_ready"], ib + 1)
                            for i in range(TB):
                                op = nc.tensor.transpose(ps_m[:, i * P:(i + 1) * P], xn[:, i, :], ident[:, :])
                            op.then_inc(sem["xt_ps"], 1)
                            pe.wait_ge(sem["xt_ready"], ib + 1)
                            for i in range(TB):
                                op = nc.tensor.matmul(ps_m[:, i * E:(i + 1) * E], xt[:, i * P:(i + 1) * P], rt[:, :],
                                                      start=True, stop=True)
                            op.then_inc(sem["router_ps"], 1)

                            def hidden(n):
                                e, (h0, hn) = n // len(HID_TILES), HID_TILES[n % len(HID_TILES)]
                                if n >= 2:
                                    pe.wait_ge(sem["hh_ready"], ib * NU + (n - 1))
                                nc.tensor.matmul(ps_h[0:hn, 2 * (n % 2), :], w1[:, e, h0:h0 + hn], xt[:, :],
                                                 start=True, stop=True)
                                nc.tensor.matmul(ps_h[0:hn, 2 * (n % 2) + 1, :], w3[:, e, h0:h0 + hn], xt[:, :],
                                                 start=True, stop=True).then_inc(sem["h_ps"], 1)

                            hidden(0)
                            for n in range(NU):
                                if n + 1 < NU:
                                    hidden(n + 1)
                                e, t = n // len(HID_TILES), n % len(HID_TILES)
                                hn = HID_TILES[t][1]
                                if t == 0 and e >= 2:
                                    pe.wait_ge(sem["y_used"], ib * E + (e - 1))
                                pe.wait_ge(sem["hh_ready"], ib * NU + (n + 1))
                                for i in range(TB):
                                    op = nc.tensor.matmul(ps_y[:, e % 2, i * C:(i + 1) * C],
                                                          hh[0:hn, n % 2, i * P:(i + 1) * P], w2[0:hn, t, e, :],
                                                          start=(t == 0 and i == 0), stop=(t == len(HID_TILES) - 1),
                                                          skip_group_check=True)
                                if t == len(HID_TILES) - 1:
                                    op.then_inc(sem["y_ps"], 1)


def build(nc, ins, out):
    N = ins["x"].shape[0]
    left_t = nc.dram_tensor("left_t", (H, N), FP32).ap()
    x1 = nc.dram_tensor("x1", (N, C), FP32).ap()
    x2 = nc.dram_tensor("x2", (N, C), FP32).ap()
    attention_layer(nc, ins["x"], ins["adj"], ins["W"], ins["W_T"], ins["a_l"], ins["a_r"], ins["bias"], left_t, x1)
    mamba_layer(nc, x1, ins["w_zdt"], ins["w_xbc"], ins["conv_w"], ins["conv_b"], ins["dt_bias"], ins["a_log"],
                ins["d_skip"], ins["norm_w"], ins["w_out_t"], ins["w_lin"], ins["b_lin"], x2)
    propagate_layer(nc, x2, ins["adj"], ins["w_row"], ins["router_t"], ins["w1_t"], ins["w3_t"], ins["w2_t"], out)


def kernel(**inputs):
    import numpy as _np
    import concourse.bacc as _bacc
    from concourse import mybir as _mybir
    from concourse.bass_utils import run_bass_kernel_spmd as _run

    nc = _bacc.Bacc("TRN2", target_bir_lowering=False, num_devices=1)
    w_in = _np.asarray(inputs["L0_ffn_W_in"])
    inner, conv_dim = DI, DI + 2 * S
    laid = {
        "x": inputs["x"], "adj": inputs["adj"], "W": inputs["L0_gnn_W"], "W_T": _np.asarray(inputs["L0_gnn_W"]).T,
        "a_l": inputs["L0_gnn_a_l"], "a_r": inputs["L0_gnn_a_r"], "bias": inputs["L0_gnn_bias"],
        "w_zdt": _np.concatenate([w_in[:, :inner], w_in[:, inner + conv_dim:]], axis=1),
        "w_xbc": w_in[:, inner:inner + conv_dim],
        "conv_w": inputs["L0_ffn_conv_w"], "conv_b": _np.asarray(inputs["L0_ffn_conv_b"]).reshape(-1, P).T, "dt_bias": inputs["L0_ffn_dt_bias"],
        "a_log": inputs["L0_ffn_A_log"], "d_skip": inputs["L0_ffn_D"], "norm_w": _np.asarray(inputs["L0_ffn_norm_w"]).reshape(-1, P).T,
        "w_out_t": _np.asarray(inputs["L0_ffn_W_out"]).T, "w_lin": inputs["L0_ffn_W_lin"],
        "b_lin": inputs["L0_ffn_b_lin"], "w_row": inputs["L1_gnn_W"],
        "router_t": _np.asarray(inputs["L1_ffn_router_w"]).T,
        "w1_t": _np.asarray(inputs["L1_ffn_w1"]).transpose(2, 0, 1),
        "w3_t": _np.asarray(inputs["L1_ffn_w3"]).transpose(2, 0, 1),
        "w2_t": _np.asarray(inputs["L1_ffn_w2"]).transpose(2, 0, 1),
    }
    arrays, ins = {}, {}
    for name, value in laid.items():
        a = _np.ascontiguousarray(value)
        arrays[f"in_{name}_dram"] = a
        ins[name] = nc.dram_tensor(f"in_{name}_dram", a.shape, _mybir.dt.from_np(a.dtype), kind="ExternalInput").ap()
    out = nc.dram_tensor("out_0_dram", laid["x"].shape, FP32, kind="ExternalOutput").ap()
    build(nc, ins, out)
    r = _run(nc, [arrays], core_ids=[0])
    return r.results[0]["out_0_dram"]
```

```python
import concourse.bass as bass
from concourse import mybir
from contextlib import ExitStack

FP32 = mybir.dt.float32
BF16 = mybir.dt.bfloat16
UINT32 = mybir.dt.uint32
ALU = mybir.AluOpType
ACT = mybir.ActivationFunctionType
AX = mybir.AxisListType

P = 128
C = 128
TB = 4
BLK = P * TB
H = 4
D = C // H
DV = D + 1
LN_EPS = 1e-5


class Scope:

    def __init__(self, nc, ctx, name):
        self.nc, self.ctx, self.name = nc, ctx, name

    def sb(self, name, shape, dt=FP32):
        return self.ctx.enter_context(self.nc.sbuf_tensor(f"{self.name}_{name}", shape, dt))

    def ps(self, name, shape, dt=FP32):
        return self.ctx.enter_context(self.nc.psum_tensor(f"{self.name}_ps_{name}", shape, dt))

    def sem(self, name):
        return self.ctx.enter_context(self.nc.semaphore(f"{self.name}_{name}"))


class Chain:

    def __init__(self, engine, sem, count=0):
        self.engine, self.sem, self.count, self.ops = engine, sem, count, 0

    def __call__(self, op):
        self.ops += 1
        self.count = self.count + 1
        op.then_inc(self.sem, 1)
        self.engine.wait_ge(self.sem, self.count)


def row_statistics(nc, link, stats, mean, var, tmp):
    half = C // 2
    link(nc.vector.tensor_tensor(mean, stats[:, :, 1], stats[:, :, 4], ALU.add))
    link(nc.vector.tensor_scalar(mean, mean, 0.5, None, ALU.mult))
    link(nc.vector.tensor_tensor(tmp, stats[:, :, 1], stats[:, :, 4], ALU.subtract))
    link(nc.vector.tensor_tensor(tmp, tmp, tmp, ALU.mult))
    link(nc.vector.tensor_scalar(tmp, tmp, 0.25, None, ALU.mult))
    link(nc.vector.tensor_tensor(var, stats[:, :, 2], stats[:, :, 5], ALU.add))
    link(nc.vector.tensor_scalar(var, var, 1.0 / C, None, ALU.mult))
    link(nc.vector.tensor_tensor(var, var, tmp, ALU.add))


def attention_layer(nc, x, adj, W, W_T, a_l, a_r, left_t, values_d, sums_d):
    N = x.shape[0]
    NT, NB = N // P, N // BLK
    assert NB & (NB - 1) == 0
    CH = BLK
    JC = CH // P
    x_tiles = x.rearrange("(t p) c -> p t c", p=P)

    keep = ExitStack()
    with keep:
        k = Scope(nc, keep, "gat")
        right = k.sb("right", [P, NT, H])
        scale01 = k.sb("scale01", [P, NT, 2, H])
        ident = k.sb("ident", [P, 2, P])
        fold = k.sb("fold", [3 * DV, DV])

        with ExitStack() as ctx:
            s = Scope(nc, ctx, "prep")
            xin = s.sb("xin", [P, NT, C])
            hid = s.sb("hid", [P, NT, C])
            xn = s.sb("xn", [P, 2, TB, C])
            xt = s.sb("xt", [C, 2, BLK])
            w_nat = s.sb("w_nat", [C, C])
            w_t = s.sb("w_t", [C, C])
            a_blk = s.sb("a_blk", [C, 2 * H])
            wa = s.sb("wa", [C, 2 * H])
            logit = s.sb("logit", [P, NT, 2, H])
            lt = s.sb("lt", [H, 2, BLK])
            stats = s.sb("stats", [P, NT, 6])
            mean = s.sb("mean", [P, NT])
            var = s.sb("var", [P, NT])
            tmp = s.sb("tmp", [P, NT])
            root = s.sb("root", [P, 2, NT])
            rstd = s.sb("rstd", [P, NT])
            norm = s.sb("norm", [P, NT])
            arg = s.sb("arg", [P, 2, NT])
            lns = s.sb("lns", [P, 2, NT])
            fac = s.sb("fac", [P, NT])
            rm = s.sb("rm", [P, H])
            rmt = s.sb("rmt", [H, 1])
            rdiag = s.sb("rdiag", [H, H])
            rmax = s.sb("rmax", [P, H])
            ones = s.sb("ones", [H, P])
            q = s.sb("q", [P, NT, H])
            wexp = s.sb("wexp", [P, NT, 2, H])
            val = s.sb("val", [P, 2, H, TB, DV])
            res = s.sb("res", [P, 2, H, TB, DV])
            parts = s.sb("parts", [P, 2, H, TB, 2, 3, DV], BF16)
            ps_t = s.ps("t", [P, 2, BLK])
            ps_h = s.ps("h", [P, 2, BLK])
            ps_e = s.ps("e", [P, 2, BLK])
            ps_l = s.ps("l", [P, 2, BLK])
            x_in = s.sem("x_in")
            w_in = s.sem("w_in")
            consts = s.sem("consts")
            chain_dve = s.sem("chain_dve")
            stats_done = s.sem("stats_done")
            rooted = s.sem("rooted")
            var_ready = s.sem("var_ready")
            arg_ready = s.sem("arg_ready")
            ln_ready = s.sem("ln_ready")
            wa_ps = s.sem("wa_ps")
            wa_ready = s.sem("wa_ready")
            xn_ready = s.sem("xn_ready")
            t_ps = s.sem("t_ps")
            xt_ready = s.sem("xt_ready")
            proj_ps = s.sem("proj_ps")
            hid_ready = s.sem("hid_ready")
            logit_ready = s.sem("logit_ready")
            lt_out = [s.sem(f"lt_out{u}") for u in range(2)]
            rm_ready = s.sem("rm_ready")
            rm_ps = s.sem("rm_ps")
            rm_diag = s.sem("rm_diag")
            rm_all = s.sem("rm_all")
            q_ready = s.sem("q_ready")
            exp_done = s.sem("exp_done")
            parts_ready = s.sem("parts_ready")
            parts_out = [s.sem(f"parts_out{u}") for u in range(2)]

            with nc.Block() as block:
                @block.sync
                def _(sp):
                    sp.wait_ge(consts, 2)
                    for h in range(H):
                        rows = slice(h * D, (h + 1) * D)
                        sp.dma_start(a_blk[rows, h:h + 1], a_l[h, :].unsqueeze(1)).then_inc(w_in, 16)
                        sp.dma_start(a_blk[rows, H + h:H + h + 1], a_r[h, :].unsqueeze(1)).then_inc(w_in, 16)
                    with sp.Fori(0, NB // 2) as pair:
                        for u in range(2):
                            sp.wait_ge(logit_ready, pair * 2 + (u + 1))
                            sp.dma_start(left_t[:, bass.ds((pair * 2 + u) * BLK, BLK)],
                                         lt[:, u, :]).then_inc(lt_out[u], 16)
                    for u in range(2):
                        sp.wait_ge(lt_out[u], 16 * (NB // 2))
                    with sp.Fori(0, NB // 2) as pair:
                        for u in range(2):
                            sp.wait_ge(parts_ready, pair * 2 + (u + 1))
                            sp.dma_start(values_d[:, :, bass.ds((pair * 2 + u) * TB, TB), :]
                                         .rearrange("h p t x -> p h (t x)"),
                                         parts[:, u, :, :, :, :, :].rearrange("p h t g s v -> p h (t g s v)")
                                         ).then_inc(parts_out[u], 16)
                    for u in range(2):
                        sp.wait_ge(parts_out[u], 16 * (NB // 2))

                @block.gpsimd
                def _(pool):
                    link = Chain(pool, consts)
                    link(nc.gpsimd.memset(ident[:, :, :], 0.0))
                    link(nc.gpsimd.memset(a_blk[:, :], 0.0))
                    link(nc.gpsimd.affine_select(out=ident[:, 0, :], in_=ident[:, 0, :], compare_op=ALU.not_equal,
                                                 fill=1.0, base=0, pattern=[[-1, P]], channel_multiplier=1))
                    link(nc.gpsimd.memset(ones[:, :], 1.0))
                    link(nc.gpsimd.memset(fold[:, :], 0.0))
                    for part in range(3):
                        link(nc.gpsimd.affine_select(out=fold[:, :], in_=fold[:, :], compare_op=ALU.not_equal,
                                                     fill=1.0, base=-DV * part, pattern=[[-1, DV]],
                                                     channel_multiplier=1))

                @block.scalar
                def _(act):
                    for b in range(4):
                        tiles = slice(b * NT // 4, (b + 1) * NT // 4)
                        act.dma_start(xin[:, tiles, :], x_tiles[:, tiles, :]).then_inc(x_in, 16)
                    act.dma_start(w_nat[:, :], W).then_inc(w_in, 16)
                    act.dma_start(w_t[:, :], W_T).then_inc(w_in, 16)
                    act.wait_ge(var_ready, 1)
                    nc.scalar.activation(root[:, 0, :], tmp[:, :], ACT.Sqrt).then_inc(rooted, 1)
                    nc.scalar.activation(root[:, 1, :], var[:, :], ACT.Sqrt, scale=float(C)).then_inc(rooted, 1)
                    act.wait_ge(arg_ready, 1)
                    nc.scalar.activation(lns[:, :, :], arg[:, :, :], ACT.Ln).then_inc(ln_ready, 1)
                    with act.Fori(0, NB // 2) as pair:
                        for u in range(2):
                            act.wait_ge(t_ps, pair * 2 + (u + 1))
                            nc.scalar.activation(xt[:, u, :], ps_t[:, u, :], ACT.Copy).then_inc(xt_ready, 1)
                            act.wait_ge(proj_ps, pair * 2 + (u + 1))
                            nc.scalar.activation(hid[:, bass.ds((pair * 2 + u) * TB, TB), :],
                                                 ps_h[:, u, :].rearrange("p (t c) -> p t c", c=C),
                                                 ACT.Copy).then_inc(hid_ready, 1)
                    act.wait_ge(q_ready, 1)
                    nc.scalar.activation(wexp[:, :, 0, :], q[:, :, :], ACT.Exp).then_inc(exp_done, 1)
                    nc.scalar.activation(wexp[:, :, 1, :], q[:, :, :], ACT.Exp, scale=0.2).then_inc(exp_done, 1)
                    act.wait_ge(q_ready, 2)
                    nc.scalar.activation(scale01[:, :, :, :], scale01[:, :, :, :], ACT.Exp).then_inc(exp_done, 1)

                @block.vector
                def _(dve):
                    link = Chain(dve, chain_dve)
                    dve.wait_ge(x_in, 16 * 4)
                    with dve.Fori(0, NT) as t:
                        nc.vector.bn_stats(stats[:, t, :], xin[:, t, :]).then_inc(stats_done, 1)
                    dve.wait_ge(stats_done, NT)
                    row_statistics(nc, link, stats, mean[:, :], var[:, :], tmp[:, :])
                    nc.vector.tensor_scalar(tmp[:, :], var[:, :], LN_EPS, None, ALU.add).then_inc(var_ready, 1)
                    dve.wait_ge(rooted, 1)
                    link(nc.vector.reciprocal(rstd[:, :], root[:, 0, :]))
                    dve.wait_ge(rooted, 2)
                    link(nc.vector.tensor_tensor(norm[:, :], root[:, 1, :], rstd[:, :], ALU.mult))
                    link(nc.vector.tensor_scalar(norm[:, :], norm[:, :], 1e-15, None, ALU.max))
                    link(nc.vector.tensor_scalar(fac[:, :], norm[:, :], 1.0 - 1e-5, None, ALU.min))
                    link(nc.vector.tensor_scalar(arg[:, 0, :], fac[:, :], 1.0, None, ALU.add))
                    nc.vector.tensor_scalar(arg[:, 1, :], fac[:, :], -1.0, 1.0, ALU.mult, ALU.add).then_inc(arg_ready, 1)
                    dve.wait_ge(ln_ready, 1)
                    link(nc.vector.tensor_tensor(fac[:, :], lns[:, 0, :], lns[:, 1, :], ALU.subtract))
                    link(nc.vector.tensor_scalar(fac[:, :], fac[:, :], 0.5, None, ALU.mult))
                    link(nc.vector.reciprocal(norm[:, :], norm[:, :]))
                    link(nc.vector.tensor_tensor(fac[:, :], fac[:, :], norm[:, :], ALU.mult))
                    link(nc.vector.tensor_tensor(fac[:, :], fac[:, :], rstd[:, :], ALU.mult))
                    dve.wait_ge(wa_ps, 1)
                    nc.vector.tensor_copy(wa[:, :], ps_e[:, 0, 0:2 * H]).then_inc(wa_ready, 1)
                    with dve.Fori(0, NB // 2) as pair:
                        for u in range(2):
                            b = pair * 2 + u
                            for i in range(TB):
                                op = nc.vector.tensor_scalar(xn[:, u, i, :], xin[:, b * TB + i, :],
                                                             mean[:, bass.ds(b * TB + i, 1)],
                                                             fac[:, bass.ds(b * TB + i, 1)],
                                                             ALU.subtract, ALU.mult)
                            op.then_inc(xn_ready, 1)
                            dve.wait_ge(proj_ps, b + 1)
                            nc.vector.tensor_scalar(logit[:, bass.ds(b * TB, TB), :, :],
                                                    ps_e[:, u, 0:TB * 2 * H]
                                                    .rearrange("p (t s h) -> p t s h", t=TB, s=2), 1.0, None, ALU.mult)
                            dve.wait_ge(lt_out[u], pair * 16)
                            nc.vector.tensor_copy(lt[:, u, :], ps_l[0:H, u, :]).then_inc(logit_ready, 1)
                    dve.wait_ge(logit_ready, NB)
                    nc.vector.tensor_reduce(rm[:, :], logit[:, :, 1, :].rearrange("p t h -> p h t"),
                                            AX.X, ALU.max).then_inc(rm_ready, 1)
                    dve.wait_ge(rm_ps, 1)
                    link(nc.vector.tensor_reduce(rmt[:, :], ps_t[0:H, 0, 0:P], AX.X, ALU.max))
                    nc.vector.tensor_scalar(rdiag[:, :], ident[0:H, 0, 0:H], rmt[:, 0:1], None,
                                            ALU.mult).then_inc(rm_diag, 1)
                    dve.wait_ge(rm_ps, 2)
                    link(nc.vector.tensor_copy(rmax[:, :], ps_e[:, 0, 0:H]))
                    rb = rmax[:, :].unsqueeze(1).to_broadcast([P, NT, H])
                    nc.vector.tensor_tensor(q[:, :, :], logit[:, :, 1, :], rb, ALU.subtract).then_inc(q_ready, 1)
                    link(nc.vector.tensor_copy(right[:, :, :], logit[:, :, 1, :]))
                    link(nc.vector.tensor_tensor(logit[:, :, 0, :], logit[:, :, 0, :], rb, ALU.add))
                    link(nc.vector.tensor_scalar(scale01[:, :, 0, :], logit[:, :, 0, :], 0.8, 0.0, ALU.mult, ALU.min))
                    nc.vector.tensor_scalar(scale01[:, :, 1, :], logit[:, :, 0, :], -0.8, 0.0, ALU.mult,
                                            ALU.min).then_inc(q_ready, 1)
                    dve.wait_ge(exp_done, 2)
                    dve.wait_ge(hid_ready, NB)
                    per_block = 2 * 6
                    first = link.count
                    with dve.Fori(0, NB // 2) as pair:
                        for u in range(2):
                            step = Chain(dve, chain_dve, (pair * 2 + u) * per_block + first)
                            t0 = (pair * 2 + u) * TB
                            for g in range(2):
                                w = wexp[:, bass.ds(t0, TB), g, :].rearrange("p t h -> p h t").unsqueeze(3)
                                hv = hid[:, bass.ds(t0, TB), :].rearrange("p t (h d) -> p h t d", h=H)
                                v, r = val[:, g, :, :, :], res[:, g, :, :, :]
                                part = [parts[:, u, :, :, g, i, :] for i in range(3)]
                                step(nc.vector.tensor_tensor(v[:, :, :, 0:D], hv, w.to_broadcast([P, H, TB, D]), ALU.mult))
                                step(nc.vector.tensor_scalar(v[:, :, :, D:DV], w, 1.0, None, ALU.mult))
                                dve.wait_ge(parts_out[u], pair * 16)
                                step(nc.vector.tensor_scalar(part[0], v, 1.0, None, ALU.mult))
                                step(nc.vector.tensor_tensor(r, v, part[0], ALU.subtract))
                                step(nc.vector.tensor_scalar(part[1], r, 1.0, None, ALU.mult))
                                step(nc.vector.tensor_tensor(part[2], r, part[1], ALU.subtract))
                            assert step.ops == per_block
                            dve.sem_inc(parts_ready, 1)

                @block.tensor
                def _(pe):
                    pe.wait_ge(consts, 8)
                    pe.wait_ge(w_in, 16 * 10)
                    nc.tensor.matmul(ps_e[:, 0, 0:2 * H], w_nat[:, :], a_blk[:, :], start=True,
                                     stop=True).then_inc(wa_ps, 1)
                    pe.wait_ge(wa_ready, 1)
                    with pe.Fori(0, NB // 2) as pair:
                        for u in range(2):
                            b = pair * 2 + u
                            pe.wait_ge(xn_ready, b + 1)
                            for i in range(TB):
                                op = nc.tensor.transpose(ps_t[:, u, i * P:(i + 1) * P], xn[:, u, i, :], ident[:, 0, :])
                            op.then_inc(t_ps, 1)
                            pe.wait_ge(xt_ready, b + 1)
                            pe.wait_ge(hid_ready, b)
                            pe.wait_ge(logit_ready, b)
                            for i in range(TB):
                                rows = xt[:, u, i * P:(i + 1) * P]
                                nc.tensor.matmul(ps_h[:, u, i * C:(i + 1) * C], rows, w_t[:, :], start=True, stop=True)
                                nc.tensor.matmul(ps_e[:, u, i * 2 * H:(i + 1) * 2 * H], rows, wa[:, :],
                                                 start=True, stop=True)
                            nc.tensor.matmul(ps_l[0:H, u, :], wa[:, 0:H], xt[:, u, :], start=True,
                                             stop=True).then_inc(proj_ps, 1)
                    pe.wait_ge(rm_ready, 1)
                    nc.tensor.transpose(ps_t[0:H, 0, 0:P], rm[:, :], ident[:, 0, :]).then_inc(rm_ps, 1)
                    pe.wait_ge(rm_diag, 1)
                    nc.tensor.matmul(ps_e[:, 0, 0:H], ones[:, :], rdiag[:, :], start=True, stop=True).then_inc(rm_ps, 1)

        attention_sweep(nc, N, adj, left_t, values_d, sums_d, right, scale01, ident, fold)



def attention_sweep(nc, N, adj, left_t, values_d, sums_d, right, scale01, ident, fold):
    NT = N // P
    WT = 8
    WB = WT * P
    NW = N // WB
    HALF = BLK
    ST = 2
    BT = 16
    NBODY = NT // BT
    LT = 2
    R = 4
    ONE = 0x38
    DVH = 3 * DV
    VW = 2 * DVH
    assert NT % BT == 0 and NW & (NW - 1) == 0
    U8, I8, F8 = mybir.dt.uint8, mybir.dt.int8, mybir.dt.float8e4
    adj_rows = adj.rearrange("(t p) c -> p t c", p=P)

    with ExitStack() as ctx:
        s = Scope(nc, ctx, "att")
        adjr = s.sb("adjr", [P, 2, WT, LT * P])
        rows_mask = s.sb("rows_mask", [P, 2, WT, LT * P], BF16)
        ident16 = s.sb("ident16", [P, P], BF16)
        mask = s.sb("mask", [P, 2 * NT, WB], U8)
        left = s.sb("left", [P, 2, WB])
        vals = s.sb("vals", [P, 2, BT // 2, 2, DVH], BF16)
        side = s.sb("side", [P, R, ST, WB], I8)
        sel = s.sb("sel", [P, R, 2, ST, WB], U8)
        neg_right = s.sb("neg_right", [P, NBODY, H])
        accs = s.sb("accs", [P, 4, HALF])
        num = s.sb("num", [P, WT, H, DV])
        half = s.sb("half", [P, WT // 2, DV])
        ps_acc = s.ps("acc", [P, 4, HALF])
        ps_t = s.ps("t", [P, 2, WB], BF16)
        ps_f = s.ps("f", [P, 2, HALF])

        adj_in = [s.sem(f"adj_in{u}") for u in range(2)]
        adj_ready = s.sem("adj_ready")
        diag_done = s.sem("diag_done")
        ident_ready = s.sem("ident_ready")
        t_ps = s.sem("t_ps")
        mask_ready = s.sem("mask_ready")
        left_in = [s.sem(f"left_in{u}") for u in range(2)]
        vals_in = [s.sem(f"vals_in{u}") for u in range(2)]
        side_act = s.sem("side_act")
        side_dve = s.sem("side_dve")
        sel1_ready = s.sem("sel1_ready")
        sel0_ready = s.sem("sel0_ready")
        sel_free = s.sem("sel_free")
        acc_act = s.sem("acc_act")
        acc_dve = s.sem("acc_dve")
        fold_ps = s.sem("fold_ps")
        num_ready = s.sem("num_ready")
        num_out = s.sem("num_out")
        num_free = s.sem("num_free")
        chain_dve = s.sem("chain_dve")
        carried_pe = s.sem("carried_pe")
        carried_pool = s.sem("carried_pool")
        A0, T0, M0, L0, F0 = 2, 4, 2, 4, 6
        STEPS = BT // ST
        PER_PASS = NBODY * STEPS
        GROUPS = NT // 4
        LOG_NW = NW.bit_length() - 1
        DVE_STEP, DVE_TILE = 3, 1
        CHAINED = 6

        def blocks(engine, head_pass, end):
            def block(ib, produce):
                for h in range(H):
                    head_pass(ib, h, 0, produce)
                    if NBODY > 1:
                        with engine.Fori(1, NBODY) as jb:
                            head_pass(ib, h, jb, produce)
                end(ib)

            if NW > 1:
                with engine.Fori(0, NW - 1) as ib:
                    block(ib, True)
            block(NW - 1, False)

        def starts(jb):
            return isinstance(jb, int) and jb == 0

        def body_number(ib, h, jb):
            return ib * (H * NBODY) + jb + h * NBODY

        with nc.Block() as block:
            @block.sync
            def _(sp):
                def load_adj(ib, group, u):
                    sp.wait_ge(adj_ready, ib * (GROUPS * 2) + group * 2 + (A0 - 1 + u))
                    sp.dma_start(adjr[:, u, :, :],
                                 adj_rows[:, bass.ds(ib * WT, WT), bass.ds((group * 2 + u) * (LT * P), LT * P)]
                                 ).then_inc(adj_in[u], 16)

                def load_left(ib, h):
                    row = left_t[h:h + 1, bass.ds(ib * WB, WB)].squeeze(0)
                    sp.dma_start(left[:, h % 2, :], row.partition_broadcast(P)).then_inc(left_in[h % 2], 16)

                def head_pass(ib, h, jb, produce):
                    number = body_number(ib, h, jb)
                    for u in range(2):
                        if produce:
                            load_adj(ib + 1, jb + h * NBODY, u)
                        sp.wait_ge(sel_free, number * STEPS + (F0 - STEPS // 2 * (1 - u)))
                        sp.dma_start(vals[:, u, :, :, :].rearrange("p t g x -> p (t g x)"),
                                     values_d[h, :, bass.ds(jb * BT + u * (BT // 2), BT // 2), :]
                                     .rearrange("p t x -> p (t x)")).then_inc(vals_in[u], 16)
                    if starts(jb) and (h < H - 1 or produce):
                        load_left(ib if h < H - 1 else ib + 1, (h + 1) % H)

                load_left(0, 0)
                with sp.Fori(0, GROUPS) as group:
                    for u in range(2):
                        load_adj(0, group, u)
                blocks(sp, head_pass, lambda ib: None)

            @block.gpsimd
            def _(pool):
                pool.sem_inc(num_free, 1)

                pool.sem_inc(adj_ready, A0)

                def mask_rows(ib, group):
                    away = ((group >> 1) + ib * (NW - 1)) & (NW - 1)
                    away = pool.snap((away + (NW - 1)) >> LOG_NW)
                    odd = pool.snap((group & 1) * 4)
                    if not isinstance(away, int):
                        away = away.with_bounds(min_val=0, max_val=1)
                    add = ident[:, bass.ds(away, 1), :].squeeze(1)
                    for u in range(2):
                        pool.wait_ge(adj_in[u], ib * (GROUPS * 16) + group * 16 + 16)
                        pool.sem_inc(carried_pool, 1)
                        for m in range(LT):
                            diag = adjr[:, u, bass.ds(odd + (2 * u + m), 1), m * P:(m + 1) * P].squeeze(1)
                            nc.gpsimd.tensor_tensor(diag, diag, add, ALU.add).then_inc(diag_done, 1)
                        pool.wait_ge(diag_done, ib * (GROUPS * 4) + group * 4 + (u + 1) * LT)
                        pool.wait_ge(t_ps, ib * (GROUPS * 4) + group * 4 + (T0 - 2 + 2 * u))
                        pool.sem_inc(carried_pool, 1)
                        nc.gpsimd.tensor_scalar(rows_mask[:, u, :, :], adjr[:, u, :, :], 0.0, None,
                                                ALU.is_gt).then_inc(adj_ready, 1)

                def head_pass(ib, h, jb, produce):
                    if produce:
                        mask_rows(ib + 1, jb + h * NBODY)

                def end(ib):
                    pool.wait_ge(num_ready, ib * H + (H + 1))
                    pool.dma_start(sums_d[bass.ds(ib * WT, WT), :, :].rearrange("t p x -> p t x"),
                                   num[:, :, :, :].rearrange("p t h v -> p t (h v)")).then_inc(num_out, 16)
                    pool.wait_ge(num_out, ib * 16 + 16)
                    pool.sem_inc(num_free, 1)

                with pool.Fori(0, GROUPS) as group:
                    mask_rows(0, group)
                blocks(pool, head_pass, end)
                pool.wait_ge(num_out, 16 * NW)

            @block.scalar
            def _(act):
                act.sem_inc(sel1_ready, L0)
                act.sem_inc(fold_ps, 1)

                def copy_sums(ib, h):
                    act.wait_ge(sel_free, ib * (H * PER_PASS) + ((h + 1) * PER_PASS + F0))
                    act.wait_ge(fold_ps, ib * H + (h + 1))
                    for a in range(2):
                        nc.scalar.activation(accs[0:DVH, a, :], ps_acc[0:DVH, a, :], ACT.Copy).then_inc(acc_act, 1)

                def head_pass(ib, h, jb, produce):
                    number = body_number(ib, h, jb)
                    for k in range(STEPS):
                        act.wait_ge(sel1_ready, number * STEPS + (k + L0 - R + 1))
                        if starts(jb) and k == 0:
                            act.wait_ge(left_in[h % 2], ib * 32 + (h // 2 + 1) * 16)
                        for j in range(ST):
                            if (k, j) != (DVE_STEP, DVE_TILE):
                                op = nc.scalar.activation(side[:, k % R, j, :], left[:, h % 2, :], ACT.Sign,
                                                          bias=right[:, jb * BT + (k * ST + j), h:h + 1])
                        op.then_inc(side_act, 1)
                        if starts(jb) and h > 0 and k == 1:
                            copy_sums(ib, h - 1)

                blocks(act, head_pass, lambda ib: copy_sums(ib, H - 1))

            @block.vector
            def _(dve):
                dve.sem_inc(num_ready, 1)
                dve.sem_inc(mask_ready, M0)
                nc.vector.tensor_scalar(neg_right[:, :, :], right[:, DVE_STEP * ST + DVE_TILE::BT, :], -1.0, None,
                                        ALU.mult).then_inc(side_dve, 1)
                dve.wait_ge(side_dve, 1)
                nc.vector.tensor_copy(ident16[:, :], ident[:, 0, :]).then_inc(ident_ready, 1)
                mask32 = mask[:, :, :].bitcast(UINT32)
                side32 = side[:, :, :, :].bitcast(UINT32)
                sel32 = sel[:, :, :, :, :].bitcast(UINT32)

                def make_mask(ib, group, i):
                    tile = ib * (GROUPS * 4) + group * 4 + i
                    dve.wait_ge(t_ps, tile + (T0 + 1))
                    row = (ib & 1) * NT + group * 4 + i
                    nc.vector.tensor_scalar(mask[:, bass.ds(row, 1), :].squeeze(1), ps_t[:, i % 2, :], float(ONE), None,
                                            ALU.mult).then_inc(mask_ready, 1)

                def copy_sums(ib, h):
                    dve.wait_ge(sel_free, ib * (H * PER_PASS) + ((h + 1) * PER_PASS + F0))
                    dve.wait_ge(fold_ps, ib * H + (h + 1))
                    for a in range(2, 4):
                        nc.vector.tensor_copy(accs[0:DVH, a, :], ps_acc[0:DVH, a, :]).then_inc(acc_dve, 1)

                def sum_branches(ib, h):
                    link = Chain(dve, chain_dve, ib * (H * CHAINED) + h * CHAINED)
                    dve.wait_ge(fold_ps, ib * H + (h + 2))
                    if h == 0:
                        dve.wait_ge(num_free, ib + 1)
                    for b in range(2):
                        folded = ps_f[:, b, 0:4 * 2 * DV].rearrange("p (i g v) -> p g i v", i=4, g=2)
                        tiles = bass.ds(ib * WT + b * 4, 4)
                        out = num[:, b * 4:b * 4 + 4, h, :]
                        row = [scale01[:, tiles, g, h:h + 1].to_broadcast([P, 4, DV]) for g in range(2)]
                        link(nc.vector.tensor_tensor(half[:, :, :], folded[:, 0], row[0], ALU.mult))
                        link(nc.vector.tensor_tensor(out, folded[:, 1], row[1], ALU.mult))
                        link(nc.vector.tensor_tensor(out, out, half[:, :, :], ALU.add))
                    assert link.ops == CHAINED
                    dve.sem_inc(num_ready, 1)

                def head_pass(ib, h, jb, produce):
                    number = body_number(ib, h, jb)
                    for k in range(STEPS):
                        step = number * STEPS + k
                        if k == DVE_STEP:
                            nc.vector.tensor_scalar(side[:, k % R, DVE_TILE, :].bitcast(U8), left[:, h % 2, :],
                                                    neg_right[:, jb, h:h + 1], 255.0,
                                                    ALU.is_lt, ALU.mult).then_inc(side_dve, 1)
                            dve.wait_ge(side_dve, number + 2)
                        dve.wait_ge(side_act, step + 1)
                        dve.wait_ge(sel_free, step + (F0 - R + 1))
                        rows = mask32[:, bass.ds((ib & 1) * NT + jb * BT + k * ST, ST), :]
                        nc.vector.tensor_tensor(sel32[:, k % R, 1, :, :], side32[:, k % R, :, :], rows,
                                                ALU.bitwise_and).then_inc(sel1_ready, 1)
                        dve.wait_ge(sel1_ready, step + (L0 + 1))
                        nc.vector.tensor_tensor(sel32[:, k % R, 0, :, :], sel32[:, k % R, 1, :, :], rows,
                                                ALU.bitwise_xor).then_inc(sel0_ready, 1)
                        if starts(jb) and h > 0:
                            if k == 0:
                                copy_sums(ib, h - 1)
                            if k == 3:
                                sum_branches(ib, h - 1)
                        if produce and k in (2, 4, 6):
                            make_mask(ib + 1, jb + h * NBODY, k // 2 - 1)
                    if produce:
                        make_mask(ib + 1, jb + h * NBODY, 3)

                def end(ib):
                    copy_sums(ib, H - 1)
                    sum_branches(ib, H - 1)

                with dve.Fori(0, GROUPS) as group:
                    for i in range(4):
                        make_mask(0, group, i)
                dve.wait_ge(mask_ready, NT + M0)
                blocks(dve, head_pass, end)

            @block.tensor
            def _(pe):
                pe.sem_inc(sel_free, F0)
                pe.sem_inc(t_ps, T0)
                pe.sem_inc(acc_act, 1)
                pe.sem_inc(acc_dve, 1)

                def transposes(ib, group, i):
                    if i % LT == 0:
                        pe.wait_ge(adj_ready, ib * (GROUPS * 2) + group * 2 + (i // LT + A0 + 1))
                    pe.wait_ge(mask_ready, ib * (GROUPS * 4) + group * 4 + (i + M0 - 1))
                    for t in range(WT):
                        op = nc.tensor.transpose(ps_t[:, i % 2, t * P:(t + 1) * P],
                                                 rows_mask[:, i // LT, t, (i % LT) * P:(i % LT + 1) * P],
                                                 ident16[:, :])
                    op.then_inc(t_ps, 1)

                def fold_sums(ib, h):
                    pe.wait_ge(num_ready, ib * H + (h + 1))
                    for copied in (acc_act, acc_dve):
                        pe.wait_ge(copied, ib * (H * 2) + ((h + 1) * 2 + 1))
                    for t in range(WT):
                        for g in range(2):
                            at = (t % 4) * 2 * DV + g * DV
                            op = nc.tensor.matmul(ps_f[:, t // 4, at:at + DV],
                                                  accs[0:DVH, g * 2 + t // 4, (t % 4) * P:(t % 4 + 1) * P],
                                                  fold[:, :], start=True, stop=True)
                    op.then_inc(fold_ps, 1)

                def head_pass(ib, h, jb, produce):
                    number = body_number(ib, h, jb)
                    if starts(jb):
                        for copied in (acc_act, acc_dve):
                            pe.wait_ge(copied, ib * (H * 2) + (h * 2 + 1))
                    for k in range(STEPS):
                        step = number * STEPS + k
                        if produce and k % 2 == 0:
                            transposes(ib + 1, jb + h * NBODY, k // 2)
                        if k % (STEPS // 2) == 0:
                            pe.wait_ge(vals_in[k // (STEPS // 2)], number * 16 + 16)
                        for g, ready in ((1, step + (L0 + 1)), (0, step + 1)):
                            pe.wait_ge((sel0_ready, sel1_ready)[g], ready)
                            pe.sem_inc(carried_pe, 1)
                            for j in range(ST):
                                for a in range(2):
                                    op = nc.tensor.matmul(
                                        ps_acc[0:DVH, g * 2 + a, :],
                                        vals[:, k // (STEPS // 2), (k * ST + j) % (BT // 2), g, :],
                                        sel[:, k % R, g, j, a * HALF:(a + 1) * HALF].bitcast(F8),
                                        start=(starts(jb) and k == 0 and j == 0), stop=False, skip_group_check=True)
                        op.then_inc(sel_free, 1)
                        if starts(jb) and h > 0 and k == 1:
                            fold_sums(ib, h - 1)

                pe.wait_ge(ident_ready, 1)
                with pe.Fori(0, GROUPS) as group:
                    for i in range(4):
                        transposes(0, group, i)
                blocks(pe, head_pass, lambda ib: fold_sums(ib, H - 1))


HM = 4
PM = 64
DI = HM * PM
S = 64
TAPS = 4
SSM_EPS = 1e-5


def mamba_layer(nc, x, sums_d, bias, w_zdt, w_xbc, conv_w, conv_b, dt_bias, a_log, d_skip, norm_w, w_out_t, w_lin, b_lin, x2):
    N = x.shape[0]
    NT, NB = N // P, N // BLK
    x_tiles = x.rearrange("(t p) c -> p t c", p=P)
    x2_tiles = x2.rearrange("(t p) c -> p t c", p=P)

    keep = ExitStack()
    with keep:
        k = Scope(nc, keep, "ssm")
        xr = k.sb("xr", [P, NT, C])
        ut = k.sb("ut", [C, N])
        wz = k.sb("wz", [C, DI + HM])
        wx = k.sb("wx", [C, DI + 2 * S])
        wc = k.sb("wc", [P, 2, C])
        cw = k.sb("cw", [P, 3, TAPS])
        cb = k.sb("cb", [P, 3])
        dskip = k.sb("dskip", [P, HM])
        ident = k.sb("ident", [P, P])
        upto = k.sb("upto", [P, P])
        after = k.sb("after", [P, P])
        dt = k.sb("dt", [P, NT, HM])
        da = k.sb("da", [P, NT, HM])
        decay = k.sb("decay", [P, 3, NT, HM])

        with ExitStack() as ctx:
            s = Scope(nc, ctx, "ssmprep")
            Q = 4
            TQ = NT // Q
            sums = s.sb("sums", [P, 2, TQ, H, DV])
            rec = s.sb("rec", [P, NT, H])
            att = s.sb("att", [P, 2, TQ, C])
            tanh = s.sb("tanh", [P, TQ, C])
            sq = s.sb("sq", [P, NT])
            vn = s.sb("vn", [P, NT])
            tn = s.sb("tn", [P, NT])
            arow = s.sb("arow", [P, C])
            sums_in = [s.sem(f"sums_in{u}") for u in range(2)]
            out_ready = s.sem("out_ready")
            tanh_done = s.sem("tanh_done")
            silu_ready = s.sem("silu_ready")
            square_done = s.sem("square_done")
            norm_ready = s.sem("norm_ready")
            normed = s.sem("normed")
            sums_used = s.sem("sums_used")
            xn = s.sb("xn", [P, 2, TB, C])
            stats = s.sb("stats", [P, NT, 6])
            mean = s.sb("mean", [P, NT])
            var = s.sb("var", [P, NT])
            tmp = s.sb("tmp", [P, NT])
            root = s.sb("root", [P, NT])
            rstd = s.sb("rstd", [P, NT])
            ones = s.sb("ones", [P, P])
            brow = s.sb("brow", [P, C])
            dtb = s.sb("dtb", [P, HM])
            al = s.sb("al", [P, HM])
            wot = s.sb("wot", [C, DI])
            wl = s.sb("wl", [C, C])
            nw = s.sb("nw", [P, 2])
            f = s.sb("f", [P, 6, NT, HM])
            ps_t = s.ps("t", [P, 2, BLK])
            ps_d = s.ps("d", [P, BLK])
            ps_w = s.ps("w", [P, BLK])
            ps_a = s.ps("a", [P, 3, BLK])
            x_in = s.sem("x_in")
            w_in = s.sem("w_in")
            consts = s.sem("consts")
            chain_dve = s.sem("chain_dve")
            stats_done = s.sem("stats_done")
            var_ready = s.sem("var_ready")
            rooted = s.sem("rooted")
            xn_ready = s.sem("xn_ready")
            t_ps = s.sem("t_ps")
            ut_ready = s.sem("ut_ready")
            dt_ps = s.sem("dt_ps")
            wc_ps = s.sem("wc_ps")
            abs_ready = s.sem("abs_ready")
            exps = s.sem("exps")
            one_more = s.sem("one_more")
            da_ready = s.sem("da_ready")
            sums_ps = s.sem("sums_ps")

            with nc.Block() as block:
                @block.sync
                def _(sp):
                    for qt in range(Q):
                        if qt >= 2:
                            sp.wait_ge(sums_used, qt - 1)
                        tiles = slice(qt * TQ, (qt + 1) * TQ)
                        sp.dma_start(sums[:, qt % 2, :, :, :].rearrange("p t h v -> p t (h v)"),
                                     sums_d[tiles, :, :].rearrange("t p x -> p t x")).then_inc(sums_in[qt % 2], 16)
                        if qt == 0:
                            sp.dma_start(xr[:, :, :], x_tiles).then_inc(x_in, 16)
                            sp.dma_start(arow[:, :], bias.partition_broadcast(P)).then_inc(x_in, 16)
                    sp.dma_start(wz[:, :], w_zdt).then_inc(w_in, 16)
                    sp.dma_start(wx[:, :], w_xbc).then_inc(w_in, 16)
                    sp.dma_start(cw[:, :, :], conv_w.rearrange("(g p) k -> p g k", p=P)).then_inc(w_in, 16)
                    sp.dma_start(cb[:, :], conv_b).then_inc(w_in, 16)
                    sp.dma_start(dskip[:, :], d_skip.partition_broadcast(P)).then_inc(w_in, 16)
                    sp.dma_start(brow[:, :], b_lin.partition_broadcast(P)).then_inc(w_in, 16)
                    sp.dma_start(dtb[:, :], dt_bias.partition_broadcast(P)).then_inc(w_in, 16)
                    sp.dma_start(al[:, :], a_log.partition_broadcast(P)).then_inc(w_in, 16)
                    sp.dma_start(wot[:, :], w_out_t).then_inc(w_in, 16)
                    sp.dma_start(wl[:, :], w_lin).then_inc(w_in, 16)
                    sp.dma_start(nw[:, :], norm_w).then_inc(w_in, 16)

                @block.gpsimd
                def _(pool):
                    link = Chain(pool, consts)
                    link(nc.gpsimd.memset(ident[:, :], 0.0))
                    link(nc.gpsimd.memset(ones[:, :], 1.0))
                    link(nc.gpsimd.affine_select(out=ident[:, :], in_=ident[:, :], compare_op=ALU.not_equal,
                                                 fill=1.0, base=0, pattern=[[-1, P]], channel_multiplier=1))
                    link(nc.gpsimd.affine_select(out=upto[:, :], in_=ones[:, :], compare_op=ALU.is_ge,
                                                 fill=0.0, base=0, pattern=[[1, P]], channel_multiplier=-1))
                    link(nc.gpsimd.affine_select(out=after[:, :], in_=ones[:, :], compare_op=ALU.is_gt,
                                                 fill=0.0, base=0, pattern=[[-1, P]], channel_multiplier=1))

                @block.scalar
                def _(act):
                    for qt in range(Q):
                        act.wait_ge(out_ready, qt + 1)
                        nc.scalar.activation(tanh[:, :, :], att[:, qt % 2, :, :], ACT.Tanh, scale=0.5).then_inc(tanh_done, 1)
                        act.wait_ge(silu_ready, qt + 1)
                        for i in range(TQ):
                            nc.scalar.activation(tanh[:, i, :], att[:, qt % 2, i, :], ACT.Square, scale=0.5,
                                                 accum_out=sq[:, qt * TQ + i:qt * TQ + i + 1]).then_inc(square_done, 1)
                        act.wait_ge(square_done, (qt + 1) * TQ + qt * 2)
                        nc.scalar.activation(vn[:, qt * TQ:(qt + 1) * TQ], sq[:, qt * TQ:(qt + 1) * TQ],
                                             ACT.Sqrt).then_inc(square_done, 1)
                        act.wait_ge(norm_ready, qt + 1)
                        nc.scalar.activation(tn[:, qt * TQ:(qt + 1) * TQ], vn[:, qt * TQ:(qt + 1) * TQ],
                                             ACT.Tanh).then_inc(square_done, 1)
                    act.wait_ge(var_ready, 1)
                    nc.scalar.activation(root[:, :], tmp[:, :], ACT.Sqrt).then_inc(rooted, 1)
                    with act.Fori(0, NB // 2) as pair:
                        for u in range(2):
                            b = pair * 2 + u
                            act.wait_ge(t_ps, b + 1)
                            nc.scalar.activation(ut[:, bass.ds(b * BLK, BLK)], ps_t[:, u, :],
                                                 ACT.Copy).then_inc(ut_ready, 1)
                    act.wait_ge(w_in, 16 * 11)
                    nc.scalar.activation(al[:, :], al[:, :], ACT.Exp).then_inc(exps, 1)
                    act.wait_ge(abs_ready, 1)
                    nc.scalar.activation(f[:, 2, :, :], f[:, 1, :, :], ACT.Exp, scale=-1.0).then_inc(exps, 1)
                    act.wait_ge(one_more, 1)
                    nc.scalar.activation(f[:, 4, :, :], f[:, 3, :, :], ACT.Ln).then_inc(exps, 1)
                    act.wait_ge(sums_ps, 1)
                    for i in range(3):
                        nc.scalar.activation(decay[:, i, :, :], ps_a[:, i, 0:NT * HM]
                                             .rearrange("p (t h) -> p t h", h=HM), ACT.Exp).then_inc(exps, 1)

                @block.vector
                def _(dve):
                    link = Chain(dve, chain_dve)
                    dve.wait_ge(x_in, 32)
                    for qt in range(Q):
                        tiles = slice(qt * TQ, (qt + 1) * TQ)
                        num, out = sums[:, qt % 2, :, :, :], att[:, qt % 2, :, :]
                        dve.wait_ge(sums_in[qt % 2], 16 * (qt // 2 + 1))
                        link(nc.vector.reciprocal(rec[:, tiles, :], num[:, :, :, D]))
                        link(nc.vector.tensor_tensor(out.rearrange("p t (h d) -> p t h d", h=H), num[:, :, :, 0:D],
                                                     rec[:, tiles, :].unsqueeze(3).to_broadcast([P, TQ, H, D]), ALU.mult))
                        dve.sem_inc(sums_used, 1)
                        nc.vector.tensor_tensor(out, out, arow[:, :].unsqueeze(1).to_broadcast([P, TQ, C]),
                                                ALU.add).then_inc(out_ready, 1)
                        dve.wait_ge(tanh_done, qt + 1)
                        nc.vector.scalar_tensor_tensor(out=out, in0=tanh[:, :, :], scalar=1.0, in1=out, op0=ALU.add,
                                                       op1=ALU.mult).then_inc(silu_ready, 1)
                        dve.wait_ge(square_done, (qt + 1) * TQ + qt * 2 + 1)
                        nc.vector.tensor_scalar(vn[:, tiles], vn[:, tiles], 1e-15, None, ALU.max).then_inc(norm_ready, 1)
                        dve.wait_ge(norm_ready, qt + 1)
                        link(nc.vector.reciprocal(rstd[:, tiles], vn[:, tiles]))
                        dve.wait_ge(square_done, (qt + 1) * TQ + qt * 2 + 2)
                        link(nc.vector.tensor_tensor(rstd[:, tiles], rstd[:, tiles], tn[:, tiles], ALU.mult))
                        link(nc.vector.tensor_scalar(rstd[:, tiles], rstd[:, tiles], 0.5, None, ALU.mult))
                        for i in range(TQ):
                            t = qt * TQ + i
                            op = nc.vector.scalar_tensor_tensor(out=xr[:, t, :], in0=out[:, i, :], scalar=rstd[:, t:t + 1],
                                                                in1=xr[:, t, :], op0=ALU.mult, op1=ALU.add)
                        link(op)
                    with dve.Fori(0, NT) as t:
                        nc.vector.bn_stats(stats[:, t, :], xr[:, t, :]).then_inc(stats_done, 1)
                    dve.wait_ge(stats_done, NT)
                    row_statistics(nc, link, stats, mean[:, :], var[:, :], tmp[:, :])
                    nc.vector.tensor_scalar(tmp[:, :], var[:, :], LN_EPS, None, ALU.add).then_inc(var_ready, 1)
                    dve.wait_ge(rooted, 1)
                    link(nc.vector.reciprocal(rstd[:, :], root[:, :]))
                    dve.wait_ge(w_in, 16 * 11)
                    with dve.Fori(0, NB // 2) as pair:
                        for u in range(2):
                            b = pair * 2 + u
                            dve.wait_ge(t_ps, b)
                            for i in range(TB):
                                op = nc.vector.tensor_scalar(xn[:, u, i, :], xr[:, b * TB + i, :],
                                                             mean[:, bass.ds(b * TB + i, 1)],
                                                             rstd[:, bass.ds(b * TB + i, 1)],
                                                             ALU.subtract, ALU.mult)
                            op.then_inc(xn_ready, 1)
                            dve.wait_ge(xn_ready, b + 1)
                            rows = xr[:, bass.ds(b * TB, TB), :]
                            nc.vector.tensor_tensor(rows, rows, brow[:, :].unsqueeze(1).to_broadcast([P, TB, C]), ALU.add)
                    for g in range(2):
                        dve.wait_ge(wc_ps, 2)
                        link(nc.vector.tensor_scalar(wc[:, g, :], ps_w[:, g * C:(g + 1) * C], nw[:, g:g + 1], None,
                                                     ALU.mult))
                    link(nc.vector.tensor_scalar(cw[:, :, :], cw[:, :, :], 0.5, None, ALU.mult))
                    link(nc.vector.tensor_scalar(cb[:, :], cb[:, :], 0.5, None, ALU.mult))
                    v, a, e, w, lw, z = (f[:, i, :, :] for i in range(6))
                    dve.wait_ge(dt_ps, NT)
                    link(nc.vector.tensor_tensor(v, ps_d[:, 0:NT * HM].rearrange("p (t h) -> p t h", h=HM),
                                                 dtb[:, :].unsqueeze(1).to_broadcast([P, NT, HM]), ALU.add))
                    link(nc.vector.tensor_scalar(a, v, -1.0, None, ALU.mult))
                    nc.vector.tensor_tensor(a, a, v, ALU.max).then_inc(abs_ready, 1)
                    dve.wait_ge(exps, 2)
                    nc.vector.tensor_scalar(w, e, 1.0, None, ALU.add).then_inc(one_more, 1)
                    dve.wait_ge(one_more, 1)
                    link(nc.vector.tensor_scalar(a, w, -1.0, None, ALU.add))
                    link(nc.vector.tensor_scalar(z, a, 0.0, None, ALU.is_equal))
                    link(nc.vector.tensor_tensor(a, a, z, ALU.add))
                    dve.wait_ge(exps, 3)
                    link(nc.vector.tensor_tensor(lw, lw, z, ALU.add))
                    link(nc.vector.reciprocal(a, a))
                    link(nc.vector.tensor_tensor(lw, lw, a, ALU.mult))
                    link(nc.vector.tensor_tensor(lw, lw, e, ALU.mult))
                    link(nc.vector.tensor_scalar(v, v, 0.0, None, ALU.max))
                    link(nc.vector.tensor_tensor(dt[:, :, :], v, lw, ALU.add))
                    link(nc.vector.tensor_scalar(al[:, :], al[:, :], -1.0, None, ALU.mult))
                    nc.vector.tensor_tensor(da[:, :, :], dt[:, :, :], al[:, :].unsqueeze(1).to_broadcast([P, NT, HM]),
                                            ALU.mult).then_inc(da_ready, 1)

                @block.tensor
                def _(pe):
                    pe.wait_ge(consts, 5)
                    pe.wait_ge(w_in, 16 * 11)
                    for g in range(2):
                        nc.tensor.matmul(ps_w[:, g * C:(g + 1) * C], wot[:, g * P:(g + 1) * P], wl[:, :],
                                         start=True, stop=True).then_inc(wc_ps, 1)
                    with pe.Fori(0, NB // 2) as pair:
                        for u in range(2):
                            b = pair * 2 + u
                            pe.wait_ge(xn_ready, b + 1)
                            pe.wait_ge(ut_ready, b)
                            for i in range(TB):
                                op = nc.tensor.transpose(ps_t[:, u, i * P:(i + 1) * P], xn[:, u, i, :], ident[:, :])
                            op.then_inc(t_ps, 1)
                    pe.wait_ge(ut_ready, NB)
                    for t in range(NT):
                        nc.tensor.matmul(ps_d[:, t * HM:(t + 1) * HM], ut[:, t * P:(t + 1) * P], wz[:, DI:DI + HM],
                                         start=True, stop=True).then_inc(dt_ps, 1)
                    pe.wait_ge(da_ready, 1)
                    flat = da[:, :, :].rearrange("p t h -> p (t h)")
                    for i, sums in enumerate((upto, after, ones)):
                        op = nc.tensor.matmul(ps_a[:, i, 0:NT * HM], sums[:, :], flat, start=True, stop=True)
                    op.then_inc(sums_ps, 1)

        with ExitStack() as ctx:
            s = Scope(nc, ctx, "scan")
            ub = s.sb("ub", [C, 2, BLK])
            raw = s.sb("raw", [P, 3, TAPS - 1 + BLK])
            cv = s.sb("cv", [P, 3, BLK])
            th = s.sb("th", [P, 3, BLK])
            xs = s.sb("xs", [P, 2, 2, BLK])
            bt = s.sb("bt", [S, 2, BLK])
            ct = s.sb("ct", [S, 2, BLK])
            dal = s.sb("dal", [P, 2, HM, P])
            ex = s.sb("ex", [P, 2, HM, P])
            gm = s.sb("gm", [P, 2, P])
            mx = s.sb("mx", [P, 2, HM, P])
            xrow = s.sb("xrow", [P, 2, DI + S])
            xdt = s.sb("xdt", [P, 2, DI])
            xdec = s.sb("xdec", [P, 2, DI])
            xd = s.sb("xd", [P, 2, DI])
            hs = s.sb("hs", [S, 2, DI])
            hd = s.sb("hd", [S, DI])
            zt = s.sb("zt", [P, 2, DI])
            zs = s.sb("zs", [P, 2, DI])
            y = s.sb("y", [P, 2, DI])
            yt = s.sb("yt", [P, 2, DI])
            yo = s.sb("yo", [P, NT, C])
            ss = s.sb("ss", [P, NT])
            junk = s.sb("junk", [P, DI])
            ps_e = s.ps("e", [P, BLK])
            ps_g = s.ps("g", [P, BLK])
            ps_x = s.ps("x", [P, BLK])
            ps_y = s.ps("y", [P, BLK])
            ps_s = s.ps("s", [P, BLK])
            ps_z = s.ps("z", [P, BLK])
            ps_r = s.ps("r", [P, 2, BLK])
            names = ("ub_ready raw_ps raw_ready conv_done tanh_done xs_ready seg_ps dal_ready exp_done g_ps x_ps "
                     "gm_ready mx_ready xrow_ready xdt_ready xdec_ready xd_ready yd_ps st_ps hd_ready hs_ready "
                     "z_ps zt_done zs_ready y_ready square_done yt_ps yt_ready out_ps yo_ready halo_done chain_dve "
                     "cleared rooted var_ready x_out").split()
            sem = {n: s.sem(n) for n in names}

            with nc.Block() as block:
                def chunks(b, fn):
                    for c in range(TB):
                        fn(c, b * TB + c)

                @block.gpsimd
                def _(pool):
                    nc.gpsimd.memset(raw[:, :, :], 0.0).then_inc(sem["cleared"], 1)
                    nc.gpsimd.memset(hs[:, :, :], 0.0).then_inc(sem["cleared"], 1)
                    with pool.Fori(0, NB // 2) as pair:
                        for u in range(2):
                            b = pair * 2 + u
                            pool.wait_ge(sem["z_ps"], b * TB)
                            nc.gpsimd.tensor_copy(ub[:, u, :], ut[:, bass.ds(b * BLK, BLK)]).then_inc(sem["ub_ready"], 1)
                            for c in range(TB):
                                q, p = b * TB + c, c % 2
                                pool.wait_ge(sem["seg_ps"], q)
                                nc.gpsimd.tensor_tensor(dal[:, p, :, :],
                                                        da[:, q, :].unsqueeze(2).to_broadcast([P, HM, P]),
                                                        after[:, :].unsqueeze(1).to_broadcast([P, HM, P]),
                                                        ALU.mult).then_inc(sem["dal_ready"], 1)

                                def per_head(v):
                                    return v.unsqueeze(2).to_broadcast([P, HM, PM])

                                def heads(v):
                                    return v.rearrange("p (h d) -> p h d", h=HM)

                                pool.wait_ge(sem["xrow_ready"], q + 1)
                                rows = heads(xrow[:, p, 0:DI])
                                pool.wait_ge(sem["st_ps"], q)
                                nc.gpsimd.tensor_tensor(heads(xdt[:, p, :]), rows, per_head(dt[:, q, :]),
                                                        ALU.mult).then_inc(sem["xdt_ready"], 1)
                                nc.gpsimd.tensor_tensor(heads(xd[:, p, :]), rows, per_head(dskip[:, :]),
                                                        ALU.mult).then_inc(sem["xd_ready"], 1)
                                pool.wait_ge(sem["xdt_ready"], q + 1)
                                nc.gpsimd.tensor_tensor(heads(xdec[:, p, :]), heads(xdt[:, p, :]),
                                                        per_head(decay[:, 1, q, :]),
                                                        ALU.mult).then_inc(sem["xdec_ready"], 1)
                                pool.wait_ge(sem["hs_ready"], q)
                                nc.gpsimd.tensor_tensor(heads(hd[:, :]), heads(hs[:, p, :]),
                                                        decay[0:S, 2, q, :].unsqueeze(2).to_broadcast([S, HM, PM]),
                                                        ALU.mult).then_inc(sem["hd_ready"], 1)

                @block.scalar
                def _(act):
                    act.wait_ge(sem["cleared"], 2)
                    with act.Fori(0, NB // 2) as pair:
                        for u in range(2):
                            b = pair * 2 + u
                            act.wait_ge(sem["halo_done"], b)
                            for g in range(3):
                                act.wait_ge(sem["raw_ps"], b * 3 + (g + 1))
                                nc.scalar.activation(raw[:, g, TAPS - 1:], ps_r[:, g % 2, :],
                                                     ACT.Copy).then_inc(sem["raw_ready"], 1)
                            for g in range(3):
                                act.wait_ge(sem["conv_done"], b * 3 + (g + 1))
                                nc.scalar.activation(th[:, g, :], cv[:, g, :], ACT.Tanh).then_inc(sem["tanh_done"], 1)
                            for c in range(TB):
                                q, p = b * TB + c, c % 2
                                act.wait_ge(sem["seg_ps"], q + 1)
                                act.wait_ge(sem["mx_ready"], q)
                                nc.scalar.activation(ex[:, p, :, :].rearrange("p h l -> p (h l)"), ps_e[:, :],
                                                     ACT.Exp).then_inc(sem["exp_done"], 1)
                                act.wait_ge(sem["x_ps"], q + 1)
                                nc.scalar.activation(xrow[:, p, :], ps_x[:, 0:DI + S],
                                                     ACT.Copy).then_inc(sem["xrow_ready"], 1)
                                act.wait_ge(sem["z_ps"], q + 1)
                                nc.scalar.activation(zt[:, p, :], ps_z[:, 0:DI], ACT.Tanh,
                                                     scale=0.5).then_inc(sem["zt_done"], 1)
                                act.wait_ge(sem["y_ready"], q + 1)
                                nc.scalar.activation(junk[:, :], y[:, p, :], ACT.Square,
                                                     accum_out=ss[:, bass.ds(q, 1)]).then_inc(sem["square_done"], 1)
                                act.wait_ge(sem["yt_ps"], q + 1)
                                nc.scalar.activation(yt[:, p, :], ps_z[:, DI:2 * DI], ACT.Copy).then_inc(sem["yt_ready"], 1)
                                act.wait_ge(sem["out_ps"], q + 1)
                                nc.scalar.activation(yo[:, q, :], ps_x[:, DI + S:DI + S + C], ACT.Copy).then_inc(sem["yo_ready"], 1)
                    act.wait_ge(sem["var_ready"], 1)
                    nc.scalar.activation(ss[:, :], ss[:, :], ACT.Sqrt).then_inc(sem["rooted"], 1)

                @block.vector
                def _(dve):
                    per_block = 3 * (TAPS - 1) + 1 + 3 * TB
                    dve.wait_ge(sem["cleared"], 2)

                    def heads(v):
                        return v.rearrange("p (h d) -> p h d", h=HM)

                    with dve.Fori(0, NB // 2) as pair:
                        for u in range(2):
                            b = pair * 2 + u
                            link = Chain(dve, sem["chain_dve"], b * per_block)
                            for g in range(3):
                                dve.wait_ge(sem["raw_ready"], b * 3 + (g + 1))
                                link(nc.vector.tensor_scalar(cv[:, g, :], raw[:, g, 0:BLK], cw[:, g, 0:1], cb[:, g:g + 1],
                                                             ALU.mult, ALU.add))
                                for j in range(1, TAPS):
                                    op = nc.vector.scalar_tensor_tensor(out=cv[:, g, :], in0=raw[:, g, j:j + BLK],
                                                                        scalar=cw[:, g, j:j + 1], in1=cv[:, g, :],
                                                                        op0=ALU.mult, op1=ALU.add)
                                    if j < TAPS - 1:
                                        link(op)
                                    else:
                                        op.then_inc(sem["conv_done"], 1)
                            link(nc.vector.tensor_copy(raw[:, :, 0:TAPS - 1], raw[:, :, BLK:BLK + TAPS - 1]))
                            dve.sem_inc(sem["halo_done"], 1)
                            dve.wait_ge(sem["yd_ps"], b * TB)
                            for g in range(3):
                                dve.wait_ge(sem["tanh_done"], b * 3 + (g + 1))
                                if g < 2:
                                    nc.vector.scalar_tensor_tensor(out=xs[:, u, g, :], in0=th[:, g, :], scalar=1.0,
                                                                   in1=cv[:, g, :], op0=ALU.add, op1=ALU.mult)
                                else:
                                    for i, to in enumerate((bt, ct)):
                                        rows = slice(i * S, (i + 1) * S)
                                        op = nc.vector.scalar_tensor_tensor(out=to[:, u, :], in0=th[rows, g, :], scalar=1.0,
                                                                            in1=cv[rows, g, :], op0=ALU.add, op1=ALU.mult)
                                    op.then_inc(sem["xs_ready"], 1)
                            for c in range(TB):
                                q, p = b * TB + c, c % 2
                                dve.wait_ge(sem["g_ps"], q + 1)
                                nc.vector.tensor_tensor(gm[:, p, :], ps_g[:, 0:P], upto[:, :],
                                                        ALU.mult).then_inc(sem["gm_ready"], 1)
                                dve.wait_ge(sem["gm_ready"], q + 1)
                                dve.wait_ge(sem["exp_done"], q + 1)
                                dve.wait_ge(sem["yd_ps"], q)
                                nc.vector.tensor_tensor(mx[:, p, :, :], ex[:, p, :, :],
                                                        gm[:, p, :].unsqueeze(1).to_broadcast([P, HM, P]),
                                                        ALU.mult).then_inc(sem["mx_ready"], 1)
                                dve.wait_ge(sem["st_ps"], q + 1)
                                dve.wait_ge(sem["hd_ready"], q + 1)
                                nc.vector.tensor_tensor(hs[:, 1 - p, :], hd[:, :], ps_s[0:S, 0:DI],
                                                        ALU.add).then_inc(sem["hs_ready"], 1)
                                dve.wait_ge(sem["zt_done"], q + 1)
                                nc.vector.scalar_tensor_tensor(out=zs[:, p, :], in0=zt[:, p, :], scalar=1.0,
                                                               in1=ps_z[:, 0:DI], op0=ALU.add,
                                                               op1=ALU.mult).then_inc(sem["zs_ready"], 1)
                                dve.wait_ge(sem["yd_ps"], q + 1)
                                dve.wait_ge(sem["yt_ps"], q)
                                yy = y[:, p, :]
                                link(nc.vector.tensor_tensor(heads(yy), heads(ps_y[:, DI:2 * DI]),
                                                             decay[:, 0, q, :].unsqueeze(2).to_broadcast([P, HM, PM]),
                                                             ALU.mult))
                                link(nc.vector.tensor_tensor(yy, yy, ps_y[:, 0:DI], ALU.add))
                                dve.wait_ge(sem["xd_ready"], q + 1)
                                link(nc.vector.tensor_tensor(yy, yy, xd[:, p, :], ALU.add))
                                dve.wait_ge(sem["zs_ready"], q + 1)
                                nc.vector.tensor_tensor(yy, yy, zs[:, p, :], ALU.mult).then_inc(sem["y_ready"], 1)
                    link = Chain(dve, sem["chain_dve"], NB * per_block)
                    dve.wait_ge(sem["square_done"], NT)
                    nc.vector.tensor_scalar(ss[:, :], ss[:, :], 0.25 / DI, SSM_EPS, ALU.mult,
                                            ALU.add).then_inc(sem["var_ready"], 1)
                    dve.wait_ge(sem["rooted"], 1)
                    link(nc.vector.reciprocal(ss[:, :], ss[:, :]))
                    link(nc.vector.tensor_scalar(ss[:, :], ss[:, :], 0.5, None, ALU.mult))
                    dve.wait_ge(sem["yo_ready"], NT)
                    with dve.Fori(0, NT) as t:
                        nc.vector.scalar_tensor_tensor(out=xr[:, t, :], in0=yo[:, t, :], scalar=ss[:, bass.ds(t, 1)],
                                                       in1=xr[:, t, :], op0=ALU.mult,
                                                       op1=ALU.add).then_inc(sem["x_out"], 1)

                @block.tensor
                def _(pe):
                    with pe.Fori(0, NB // 2) as pair:
                        for u in range(2):
                            b = pair * 2 + u
                            pe.wait_ge(sem["ub_ready"], b + 1)
                            for g in range(3):
                                pe.wait_ge(sem["raw_ready"], b * 3 + max(g - 1, 0))
                                nc.tensor.matmul(ps_r[:, g % 2, :], wx[:, g * P:(g + 1) * P], ub[:, u, :], start=True,
                                                 stop=True).then_inc(sem["raw_ps"], 1)
                            for c in range(TB):
                                q, p = b * TB + c, c % 2
                                cols = slice(c * P, (c + 1) * P)
                                pe.wait_ge(sem["zs_ready"], q)
                                nc.tensor.matmul(ps_z[:, 0:DI], ub[:, u, cols], wz[:, 0:DI], start=True,
                                                 stop=True).then_inc(sem["z_ps"], 1)
                                pe.wait_ge(sem["dal_ready"], q + 1)
                                pe.wait_ge(sem["exp_done"], q)
                                for h in range(HM):
                                    op = nc.tensor.matmul(ps_e[:, h * P:(h + 1) * P], dal[:, p, h, :], upto[:, :],
                                                          start=True, stop=True)
                                op.then_inc(sem["seg_ps"], 1)
                                if c == 0:
                                    pe.wait_ge(sem["xs_ready"], b + 1)
                                pe.wait_ge(sem["gm_ready"], q)
                                nc.tensor.matmul(ps_g[:, 0:P], bt[:, u, cols], ct[:, u, cols], start=True,
                                                 stop=True).then_inc(sem["g_ps"], 1)
                                pe.wait_ge(sem["yo_ready"], q)
                                for g in range(2):
                                    nc.tensor.transpose(ps_x[:, g * P:(g + 1) * P], xs[:, u, g, cols], ident[:, :])
                                nc.tensor.transpose(ps_x[:, DI:DI + S], bt[:, u, cols],
                                                    ident[0:S, 0:S]).then_inc(sem["x_ps"], 1)
                                pe.wait_ge(sem["y_ready"], q)
                                pe.wait_ge(sem["hs_ready"], q)
                                nc.tensor.matmul(ps_y[:, DI:2 * DI], ct[:, u, cols], hs[:, p, :], start=True,
                                                 stop=True)
                                pe.wait_ge(sem["xdec_ready"], q + 1)
                                nc.tensor.matmul(ps_s[0:S, 0:DI], xrow[:, p, DI:DI + S], xdec[:, p, :], start=True,
                                                 stop=True).then_inc(sem["st_ps"], 1)
                                pe.wait_ge(sem["mx_ready"], q + 1)
                                for h in range(HM):
                                    op = nc.tensor.matmul(ps_y[:, h * PM:(h + 1) * PM], mx[:, p, h, :],
                                                          xdt[:, p, h * PM:(h + 1) * PM], start=True, stop=True)
                                op.then_inc(sem["yd_ps"], 1)
                                pe.wait_ge(sem["y_ready"], q + 1)
                                for g in range(2):
                                    op = nc.tensor.transpose(ps_z[:, DI + g * P:DI + (g + 1) * P],
                                                             y[:, p, g * P:(g + 1) * P], ident[:, :])
                                op.then_inc(sem["yt_ps"], 1)
                                pe.wait_ge(sem["yt_ready"], q + 1)
                                for g in range(2):
                                    op = nc.tensor.matmul(ps_x[:, DI + S:DI + S + C], yt[:, p, g * P:(g + 1) * P], wc[:, g, :],
                                                          start=(g == 0), stop=(g == 1))
                                op.then_inc(sem["out_ps"], 1)

                @block.sync
                def _(sp):
                    sp.wait_ge(sem["x_out"], NT)
                    sp.dma_start(x2_tiles, xr[:, :, :]).then_inc(sem["x_out"], 16)
                    sp.wait_ge(sem["x_out"], NT + 16)


E = 8
TOP = 2
HID = 341
GATE_EPS = 1e-9
HID_TILES = [(h0, min(P, HID - h0)) for h0 in range(0, HID, P)]


def propagate_layer(nc, x2, adj, w_row, router_t, w1_t, w3_t, w2_t, out):
    N = x2.shape[0]
    NT, NB = N // P, N // BLK
    x2_tiles = x2.rearrange("(t p) c -> p t c", p=P)
    out_tiles = out.rearrange("(t p) c -> p t c", p=P)
    adj_rows = adj.rearrange("(t p) c -> p t c", p=P)

    keep = ExitStack()
    with keep:
        k = Scope(nc, keep, "gnn")
        xr = k.sb("xr", [P, NT, C])
        hid = k.sb("hid", [P, NT, C])
        ident = k.sb("ident", [P, P])
        eye8 = k.sb("eye8", [P, E])
        rt = k.sb("rt", [C, E])
        w1 = k.sb("w1", [C, E, HID])
        w3 = k.sb("w3", [C, E, HID])
        w2 = k.sb("w2", [P, len(HID_TILES), E, C])

        with ExitStack() as ctx:
            s = Scope(nc, ctx, "gnnprep")
            stats = s.sb("stats", [P, NT, 6])
            mean = s.sb("mean", [P, NT])
            var = s.sb("var", [P, NT])
            tmp = s.sb("tmp", [P, NT])
            root = s.sb("root", [P, NT])
            rstd = s.sb("rstd", [P, NT])
            wrow = s.sb("wrow", [P, C])
            count8 = s.sb("count8", [P, E], mybir.dt.int32)
            x_in = s.sem("x_in")
            w_in = s.sem("w_in")
            consts = s.sem("consts")
            chain_dve = s.sem("chain_dve")
            stats_done = s.sem("stats_done")
            var_ready = s.sem("var_ready")
            rooted = s.sem("rooted")

            with nc.Block() as block:
                @block.sync
                def _(sp):
                    sp.dma_start(xr[:, :, :], x2_tiles).then_inc(x_in, 16)
                    sp.dma_start(wrow[:, :], w_row.partition_broadcast(P)).then_inc(w_in, 16)
                    sp.dma_start(rt[:, :], router_t).then_inc(w_in, 16)
                    sp.dma_start(w1[:, :, :], w1_t).then_inc(w_in, 16)
                    sp.dma_start(w3[:, :, :], w3_t).then_inc(w_in, 16)
                    for i, (h0, hn) in enumerate(HID_TILES):
                        sp.dma_start(w2[0:hn, i, :, :], w2_t[h0:h0 + hn, :, :]).then_inc(w_in, 16)
                    sp.wait_ge(w_in, 16 * (4 + len(HID_TILES)))

                @block.gpsimd
                def _(pool):
                    link = Chain(pool, consts)
                    link(nc.gpsimd.memset(ident[:, :], 0.0))
                    link(nc.gpsimd.affine_select(out=ident[:, :], in_=ident[:, :], compare_op=ALU.not_equal,
                                                 fill=1.0, base=0, pattern=[[-1, P]], channel_multiplier=1))
                    link(nc.gpsimd.iota(count8[:, :], pattern=[[1, E]], base=0, channel_multiplier=0))
                    link(nc.gpsimd.tensor_copy(eye8[:, :], count8[:, :]))

                @block.scalar
                def _(act):
                    act.wait_ge(var_ready, 1)
                    nc.scalar.activation(root[:, :], tmp[:, :], ACT.Sqrt).then_inc(rooted, 1)

                @block.vector
                def _(dve):
                    link = Chain(dve, chain_dve)
                    dve.wait_ge(x_in, 16)
                    with dve.Fori(0, NT) as t:
                        nc.vector.bn_stats(stats[:, t, :], xr[:, t, :]).then_inc(stats_done, 1)
                    dve.wait_ge(stats_done, NT)
                    row_statistics(nc, link, stats, mean[:, :], var[:, :], tmp[:, :])
                    nc.vector.tensor_scalar(tmp[:, :], var[:, :], LN_EPS, None, ALU.add).then_inc(var_ready, 1)
                    dve.wait_ge(rooted, 1)
                    link(nc.vector.reciprocal(rstd[:, :], root[:, :]))
                    dve.wait_ge(w_in, 16 * (4 + len(HID_TILES)))
                    with dve.Fori(0, NB) as b:
                        step = Chain(dve, chain_dve, b * 2 + link.count)
                        for i in range(TB):
                            op = nc.vector.tensor_scalar(hid[:, b * TB + i, :], xr[:, b * TB + i, :],
                                                         mean[:, bass.ds(b * TB + i, 1)],
                                                         rstd[:, bass.ds(b * TB + i, 1)], ALU.subtract, ALU.mult)
                        step(op)
                        rows = hid[:, bass.ds(b * TB, TB), :]
                        step(nc.vector.tensor_tensor(rows, rows, wrow[:, :].unsqueeze(1).to_broadcast([P, TB, C]),
                                                     ALU.mult))

        with ExitStack() as ctx:
            s = Scope(nc, ctx, "sweep")
            AR = 4
            T0 = AR * TB
            adjr = s.sb("adjr", [P, AR, TB, BLK])
            adjt = s.sb("adjt", [P, 2, BLK])
            acct = s.sb("acct", [C, BLK])
            xo = s.sb("xo", [P, 2, TB, C])
            xn = s.sb("xn", [P, TB, C])
            xt = s.sb("xt", [C, BLK])
            stats = s.sb("stats", [P, TB, 6])
            mv = s.sb("mv", [P, TB, 2])
            ve = s.sb("ve", [P, TB])
            rstd = s.sb("rstd", [P, TB])
            lg = s.sb("lg", [P, TB, E])
            pr = s.sb("pr", [P, TB, E])
            hot = s.sb("hot", [P, TB, E])
            gate = s.sb("gate", [P, TB, E])
            m4 = s.sb("m4", [P, TB])
            top = s.sb("top", [P, TB, 8])
            topi = s.sb("topi", [P, TB, 8], UINT32)
            topf = s.sb("topf", [P, TB, 8])
            wk = s.sb("wk", [P, TB, TOP])
            th = s.sb("th", [P, 2, BLK])
            pa = s.sb("pa", [P, 2, BLK])
            hh = s.sb("hh", [P, 2, BLK])
            ps_acc = s.ps("acc", [P, BLK])
            ps_h = s.ps("h", [P, 4, BLK])
            ps_m = s.ps("m", [P, BLK])
            ps_y = s.ps("y", [P, 2, BLK])
            adj_in = [s.sem(f"adj_in{u}") for u in range(AR)]
            names = ("t_ps mm_done acct_ready back_ps x3_ready ve_ready rooted xn_ready xt_ps xt_ready "
                     "router_ps lg_ready exp_done gate_ready pa_ready h_ps th_ready hh_ready y_ps y_used carried chain_dve").split()
            sem = {n: s.sem(n) for n in names}
            x_out = [s.sem(f"x_out{u}") for u in range(2)]
            adjt_ready = [s.sem(f"adjt_ready{u}") for u in range(2)]
            NU = E * len(HID_TILES)
            NCH = NT // TB

            with nc.Block() as block:
                @block.sync
                def _(sp):
                    with sp.Fori(0, NB // 2) as pair:
                        for v in range(2):
                            ib = pair * 2 + v
                            with sp.Fori(0, NCH // AR) as cp:
                                for u in range(AR):
                                    sp.wait_ge(sem["t_ps"], ib * NT + (cp * AR + u + 1) * TB)
                                    sp.dma_start(adjr[:, u, :, :],
                                                 adj_rows[:, bass.ds(ib * TB, TB), bass.ds((cp * AR + u) * BLK, BLK)]
                                                 ).then_inc(adj_in[u], 16)

                @block.gpsimd
                def _(pool):
                    with pool.Fori(0, NB // 2) as pair:
                        for v in range(2):
                            ib = pair * 2 + v
                            pool.wait_ge(sem["y_used"], (ib + 1) * E)
                            pool.dma_start(out_tiles[:, bass.ds(ib * TB, TB), :], xo[:, v, :, :]).then_inc(x_out[v], 16)
                    for v in range(2):
                        pool.wait_ge(x_out[v], 16 * (NB // 2))

                @block.scalar
                def _(act):
                    with act.Fori(0, NB // 2) as pair:
                        for v in range(2):
                            ib = pair * 2 + v
                            for j in range(1, NT, 2):
                                act.wait_ge(sem["t_ps"], ib * NT + (j + 1 + T0))
                                nc.scalar.activation(adjt[:, 1, :], ps_h[:, 1, :], ACT.Copy).then_inc(adjt_ready[1], 1)
                            act.wait_ge(sem["mm_done"], (ib + 1) * NT)
                            nc.scalar.activation(acct[:, :], ps_acc[:, :], ACT.Copy).then_inc(sem["acct_ready"], 1)
                            act.wait_ge(sem["ve_ready"], ib + 1)
                            nc.scalar.activation(ve[:, :], ve[:, :], ACT.Sqrt).then_inc(sem["rooted"], 1)
                            act.wait_ge(sem["xt_ps"], ib + 1)
                            nc.scalar.activation(xt[:, :], ps_m[:, :], ACT.Copy).then_inc(sem["xt_ready"], 1)
                            act.wait_ge(sem["lg_ready"], ib + 1)
                            nc.scalar.activation(pr[:, :, :], lg[:, :, :], ACT.Exp).then_inc(sem["exp_done"], 1)
                            for n in range(NU):
                                h0, hn = HID_TILES[n % len(HID_TILES)]
                                act.wait_ge(sem["h_ps"], ib * NU + (n + 1))
                                nc.scalar.activation(th[0:hn, n % 2, :], ps_h[0:hn, 2 * (n % 2), :], ACT.Tanh,
                                                     scale=0.5).then_inc(sem["th_ready"], 1)

                @block.vector
                def _(dve):
                    per_block = 27

                    def carry():
                        dve.sem_inc(sem["carried"], 1)

                    with dve.Fori(0, NB // 2) as pair:
                        for v in range(2):
                            ib = pair * 2 + v
                            link = Chain(dve, sem["chain_dve"], ib * per_block)
                            for j in range(0, NT, 2):
                                dve.wait_ge(sem["t_ps"], ib * NT + (j + 1 + T0))
                                nc.vector.tensor_copy(adjt[:, 0, :], ps_h[:, 0, :]).then_inc(adjt_ready[0], 1)
                            x3 = xo[:, v, :, :]
                            dve.wait_ge(x_out[v], pair * 16)
                            dve.wait_ge(sem["back_ps"], ib + 1)
                            nc.vector.tensor_tensor(x3, xr[:, bass.ds(ib * TB, TB), :],
                                                    ps_m[:, :].rearrange("p (t c) -> p t c", t=TB),
                                                    ALU.add).then_inc(sem["x3_ready"], 1)
                            dve.wait_ge(sem["x3_ready"], ib + 1)
                            for i in range(TB):
                                op = nc.vector.bn_stats(stats[:, i, :], x3[:, i, :])
                            link(op)
                            carry()
                            for i in range(TB):
                                op = nc.vector.bn_aggr(mv[:, i, :], stats[:, i, :])
                            link(op)
                            nc.vector.tensor_scalar(ve[:, :], mv[:, :, 1], LN_EPS, None, ALU.add).then_inc(sem["ve_ready"], 1)
                            dve.wait_ge(sem["rooted"], ib + 1)
                            link(nc.vector.reciprocal(rstd[:, :], ve[:, :]))
                            for i in range(TB):
                                op = nc.vector.tensor_scalar(xn[:, i, :], x3[:, i, :], mv[:, i, 0:1], rstd[:, i:i + 1],
                                                             ALU.subtract, ALU.mult)
                            op.then_inc(sem["xn_ready"], 1)
                            dve.wait_ge(sem["router_ps"], ib + 1)
                            link(nc.vector.tensor_scalar(lg[:, :, :], ps_m[:, 0:TB * E].rearrange("p (t e) -> p t e", e=E),
                                                         1.0, None, ALU.mult))
                            link(nc.vector.tensor_reduce(m4[:, :], lg[:, :, :], AX.X, ALU.max))
                            nc.vector.tensor_tensor(lg[:, :, :], lg[:, :, :], m4[:, :].unsqueeze(2).to_broadcast([P, TB, E]),
                                                    ALU.subtract).then_inc(sem["lg_ready"], 1)
                            dve.wait_ge(sem["exp_done"], ib + 1)
                            link(nc.vector.tensor_reduce(m4[:, :], pr[:, :, :], AX.X, ALU.add))
                            link(nc.vector.reciprocal(m4[:, :], m4[:, :]))
                            link(nc.vector.tensor_tensor(pr[:, :, :], pr[:, :, :], m4[:, :].unsqueeze(2).to_broadcast([P, TB, E]),
                                                         ALU.mult))
                            for i in range(TB):
                                carry()
                                link(nc.vector.max(top[:, i, :], pr[:, i, :]))
                                carry()
                                link(nc.vector.max_index(topi[:, i, :], top[:, i, :], pr[:, i, :]))
                            link(nc.vector.tensor_copy(topf[:, :, :], topi[:, :, :]))
                            link(nc.vector.tensor_tensor(m4[:, :], top[:, :, 0], top[:, :, 1], ALU.add))
                            link(nc.vector.tensor_scalar(m4[:, :], m4[:, :], GATE_EPS, None, ALU.add))
                            link(nc.vector.reciprocal(m4[:, :], m4[:, :]))
                            link(nc.vector.tensor_scalar(m4[:, :], m4[:, :], 0.5, None, ALU.mult))
                            link(nc.vector.tensor_tensor(wk[:, :, :], top[:, :, 0:TOP],
                                                         m4[:, :].unsqueeze(2).to_broadcast([P, TB, TOP]), ALU.mult))
                            places = eye8[:, :].unsqueeze(1).to_broadcast([P, TB, E])
                            for r, to in enumerate((gate, hot)):
                                link(nc.vector.tensor_tensor(to[:, :, :], places,
                                                             topf[:, :, r:r + 1].to_broadcast([P, TB, E]), ALU.is_equal))
                                link(nc.vector.tensor_tensor(to[:, :, :], to[:, :, :],
                                                             wk[:, :, r:r + 1].to_broadcast([P, TB, E]), ALU.mult))
                            link(nc.vector.tensor_tensor(gate[:, :, :], gate[:, :, :], hot[:, :, :], ALU.add))

                            def add_expert(e):
                                dve.wait_ge(sem["y_ps"], ib * E + (e + 1))
                                if e > 0:
                                    dve.wait_ge(sem["y_used"], ib * E + e)
                                for i in range(TB):
                                    op = nc.vector.scalar_tensor_tensor(
                                        out=x3[:, i, :], in0=ps_y[:, e % 2, i * C:(i + 1) * C],
                                        scalar=gate[:, i, e:e + 1], in1=x3[:, i, :], op0=ALU.mult, op1=ALU.add)
                                op.then_inc(sem["y_used"], 1)

                            for n in range(NU):
                                h0, hn = HID_TILES[n % len(HID_TILES)]
                                dve.wait_ge(sem["th_ready"], ib * NU + (n + 1))
                                dve.wait_ge(sem["hh_ready"], ib * NU + n)
                                nc.vector.scalar_tensor_tensor(out=pa[0:hn, n % 2, :], in0=th[0:hn, n % 2, :], scalar=1.0,
                                                               in1=ps_h[0:hn, 2 * (n % 2), :], op0=ALU.add,
                                                               op1=ALU.mult).then_inc(sem["pa_ready"], 1)
                                dve.wait_ge(sem["pa_ready"], ib * NU + (n + 1))
                                nc.vector.tensor_tensor(hh[0:hn, n % 2, :], pa[0:hn, n % 2, :],
                                                        ps_h[0:hn, 2 * (n % 2) + 1, :], ALU.mult).then_inc(sem["hh_ready"], 1)
                                if n >= 4 and (n - 4) % 3 == 0:
                                    add_expert((n - 4) // 3)
                            add_expert(E - 1)
                            assert link.ops == per_block, link.ops

                @block.tensor
                def _(pe):
                    pe.sem_inc(sem["t_ps"], T0)
                    with pe.Fori(0, NB // 2) as pair:
                        for v in range(2):
                            ib = pair * 2 + v

                            def transposes(j):
                                u = (j // TB) % AR
                                if j % TB == 0:
                                    pe.wait_ge(adj_in[u], ib * (NCH // AR * 16) + 16 * (j // (AR * TB) + 1))
                                if j >= 2:
                                    pe.wait_ge(adjt_ready[j % 2], ib * (NT // 2) + j // 2)
                                for i in range(TB):
                                    op = nc.tensor.transpose(ps_h[:, j % 2, i * P:(i + 1) * P],
                                                             adjr[:, u, i, (j % TB) * P:(j % TB + 1) * P], ident[:, :])
                                op.then_inc(sem["t_ps"], 1)

                            pe.wait_ge(sem["hh_ready"], ib * NU)
                            transposes(0)
                            for j in range(NT):
                                if j + 1 < NT:
                                    transposes(j + 1)
                                pe.wait_ge(adjt_ready[j % 2], ib * (NT // 2) + (j // 2 + 1))
                                nc.tensor.matmul(ps_acc[:, :], hid[:, j, :], adjt[:, j % 2, :], start=(j == 0),
                                                 stop=(j == NT - 1)).then_inc(sem["mm_done"], 1)
                            pe.wait_ge(sem["acct_ready"], ib + 1)
                            for i in range(TB):
                                op = nc.tensor.transpose(ps_m[:, i * C:(i + 1) * C], acct[:, i * P:(i + 1) * P], ident[:, :])
                            op.then_inc(sem["back_ps"], 1)
                            pe.wait_ge(sem["xn_ready"], ib + 1)
                            for i in range(TB):
                                op = nc.tensor.transpose(ps_m[:, i * P:(i + 1) * P], xn[:, i, :], ident[:, :])
                            op.then_inc(sem["xt_ps"], 1)
                            pe.wait_ge(sem["xt_ready"], ib + 1)
                            for i in range(TB):
                                op = nc.tensor.matmul(ps_m[:, i * E:(i + 1) * E], xt[:, i * P:(i + 1) * P], rt[:, :],
                                                      start=True, stop=True)
                            op.then_inc(sem["router_ps"], 1)

                            def hidden(n):
                                e, (h0, hn) = n // len(HID_TILES), HID_TILES[n % len(HID_TILES)]
                                if n >= 2:
                                    pe.wait_ge(sem["hh_ready"], ib * NU + (n - 1))
                                nc.tensor.matmul(ps_h[0:hn, 2 * (n % 2), :], w1[:, e, h0:h0 + hn], xt[:, :],
                                                 start=True, stop=True)
                                nc.tensor.matmul(ps_h[0:hn, 2 * (n % 2) + 1, :], w3[:, e, h0:h0 + hn], xt[:, :],
                                                 start=True, stop=True).then_inc(sem["h_ps"], 1)

                            hidden(0)
                            for n in range(NU):
                                if n + 1 < NU:
                                    hidden(n + 1)
                                e, t = n // len(HID_TILES), n % len(HID_TILES)
                                hn = HID_TILES[t][1]
                                if t == 0 and e >= 2:
                                    pe.wait_ge(sem["y_used"], ib * E + (e - 1))
                                pe.wait_ge(sem["hh_ready"], ib * NU + (n + 1))
                                for i in range(TB):
                                    op = nc.tensor.matmul(ps_y[:, e % 2, i * C:(i + 1) * C],
                                                          hh[0:hn, n % 2, i * P:(i + 1) * P], w2[0:hn, t, e, :],
                                                          start=(t == 0 and i == 0), stop=(t == len(HID_TILES) - 1),
                                                          skip_group_check=True)
                                if t == len(HID_TILES) - 1:
                                    op.then_inc(sem["y_ps"], 1)


def build(nc, ins, out):
    N = ins["x"].shape[0]
    left_t = nc.dram_tensor("left_t", (H, N), FP32).ap()
    values_d = nc.dram_tensor("values_d", (H, P, N // P, 2 * 3 * DV), BF16).ap()
    sums_d = nc.dram_tensor("sums_d", (N // P, P, H * DV), FP32).ap()
    x2 = nc.dram_tensor("x2", (N, C), FP32).ap()
    attention_layer(nc, ins["x"], ins["adj"], ins["W"], ins["W_T"], ins["a_l"], ins["a_r"], left_t, values_d, sums_d)
    mamba_layer(nc, ins["x"], sums_d, ins["bias"], ins["w_zdt"], ins["w_xbc"], ins["conv_w"], ins["conv_b"], ins["dt_bias"], ins["a_log"],
                ins["d_skip"], ins["norm_w"], ins["w_out_t"], ins["w_lin"], ins["b_lin"], x2)
    propagate_layer(nc, x2, ins["adj"], ins["w_row"], ins["router_t"], ins["w1_t"], ins["w3_t"], ins["w2_t"], out)


def kernel(**inputs):
    import numpy as _np
    import concourse.bacc as _bacc
    from concourse import mybir as _mybir
    from concourse.bass_utils import run_bass_kernel_spmd as _run

    nc = _bacc.Bacc("TRN2", target_bir_lowering=False, num_devices=1)
    w_in = _np.asarray(inputs["L0_ffn_W_in"])
    inner, conv_dim = DI, DI + 2 * S
    laid = {
        "x": inputs["x"], "adj": inputs["adj"], "W": inputs["L0_gnn_W"], "W_T": _np.asarray(inputs["L0_gnn_W"]).T,
        "a_l": inputs["L0_gnn_a_l"], "a_r": inputs["L0_gnn_a_r"], "bias": inputs["L0_gnn_bias"],
        "w_zdt": _np.concatenate([w_in[:, :inner], w_in[:, inner + conv_dim:]], axis=1),
        "w_xbc": w_in[:, inner:inner + conv_dim],
        "conv_w": inputs["L0_ffn_conv_w"], "conv_b": _np.asarray(inputs["L0_ffn_conv_b"]).reshape(-1, P).T, "dt_bias": inputs["L0_ffn_dt_bias"],
        "a_log": inputs["L0_ffn_A_log"], "d_skip": inputs["L0_ffn_D"], "norm_w": _np.asarray(inputs["L0_ffn_norm_w"]).reshape(-1, P).T,
        "w_out_t": _np.asarray(inputs["L0_ffn_W_out"]).T, "w_lin": inputs["L0_ffn_W_lin"],
        "b_lin": inputs["L0_ffn_b_lin"], "w_row": inputs["L1_gnn_W"],
        "router_t": _np.asarray(inputs["L1_ffn_router_w"]).T,
        "w1_t": _np.asarray(inputs["L1_ffn_w1"]).transpose(2, 0, 1),
        "w3_t": _np.asarray(inputs["L1_ffn_w3"]).transpose(2, 0, 1),
        "w2_t": _np.asarray(inputs["L1_ffn_w2"]).transpose(2, 0, 1),
    }
    arrays, ins = {}, {}
    for name, value in laid.items():
        a = _np.ascontiguousarray(value)
        arrays[f"in_{name}_dram"] = a
        ins[name] = nc.dram_tensor(f"in_{name}_dram", a.shape, _mybir.dt.from_np(a.dtype), kind="ExternalInput").ap()
    out = nc.dram_tensor("out_0_dram", laid["x"].shape, FP32, kind="ExternalOutput").ap()
    build(nc, ins, out)
    r = _run(nc, [arrays], core_ids=[0])
    return r.results[0]["out_0_dram"]
```

```python
import concourse.bass as bass
from concourse import mybir
from contextlib import ExitStack

FP32 = mybir.dt.float32
BF16 = mybir.dt.bfloat16
UINT32 = mybir.dt.uint32
ALU = mybir.AluOpType
ACT = mybir.ActivationFunctionType
AX = mybir.AxisListType

P = 128
C = 128
TB = 4
BLK = P * TB
H = 4
D = C // H
DV = D + 1
LN_EPS = 1e-5


class Scope:

    def __init__(self, nc, ctx, name):
        self.nc, self.ctx, self.name = nc, ctx, name

    def sb(self, name, shape, dt=FP32):
        return self.ctx.enter_context(self.nc.sbuf_tensor(f"{self.name}_{name}", shape, dt))

    def ps(self, name, shape, dt=FP32):
        return self.ctx.enter_context(self.nc.psum_tensor(f"{self.name}_ps_{name}", shape, dt))

    def sem(self, name):
        return self.ctx.enter_context(self.nc.semaphore(f"{self.name}_{name}"))


UNROLL = 8


class Chain:

    def __init__(self, engine, sem, count=0):
        self.engine, self.sem, self.count, self.ops = engine, sem, count, 0

    def __call__(self, op):
        self.ops += 1
        self.count = self.count + 1
        op.then_inc(self.sem, 1)
        self.engine.wait_ge(self.sem, self.count)


def row_statistics(nc, link, stats, mean, var, tmp):
    half = C // 2
    link(nc.vector.tensor_tensor(mean, stats[:, :, 1], stats[:, :, 4], ALU.add))
    link(nc.vector.tensor_scalar(mean, mean, 0.5, None, ALU.mult))
    link(nc.vector.tensor_tensor(tmp, stats[:, :, 1], stats[:, :, 4], ALU.subtract))
    link(nc.vector.tensor_tensor(tmp, tmp, tmp, ALU.mult))
    link(nc.vector.tensor_scalar(tmp, tmp, 0.25, None, ALU.mult))
    link(nc.vector.tensor_tensor(var, stats[:, :, 2], stats[:, :, 5], ALU.add))
    link(nc.vector.tensor_scalar(var, var, 1.0 / C, None, ALU.mult))
    link(nc.vector.tensor_tensor(var, var, tmp, ALU.add))


def attention_layer(nc, x, adj, W, W_T, a_l, a_r, left_t, values_d, sums_d):
    N = x.shape[0]
    NT, NB = N // P, N // BLK
    assert NB & (NB - 1) == 0
    x_tiles = x.rearrange("(t p) c -> p t c", p=P)

    keep = ExitStack()
    with keep:
        k = Scope(nc, keep, "gat")
        right = k.sb("right", [P, NT, H])
        scale01 = k.sb("scale01", [P, NT, 2, H])
        ident = k.sb("ident", [P, 2, P])
        fold = k.sb("fold", [3 * DV, DV])

        with ExitStack() as ctx:
            s = Scope(nc, ctx, "prep")
            xin = s.sb("xin", [P, NT, C])
            hid = s.sb("hid", [P, NT, C])
            xn = s.sb("xn", [P, 2, TB, C])
            xt = s.sb("xt", [C, 2, BLK])
            w_nat = s.sb("w_nat", [C, C])
            w_t = s.sb("w_t", [C, C])
            a_blk = s.sb("a_blk", [C, 2 * H])
            wa = s.sb("wa", [C, 2 * H])
            logit = s.sb("logit", [P, NT, 2, H])
            lt = s.sb("lt", [H, 2, BLK])
            stats = s.sb("stats", [P, NT, 6])
            mean = s.sb("mean", [P, NT])
            var = s.sb("var", [P, NT])
            tmp = s.sb("tmp", [P, NT])
            root = s.sb("root", [P, 2, NT])
            rstd = s.sb("rstd", [P, NT])
            norm = s.sb("norm", [P, NT])
            arg = s.sb("arg", [P, 2, NT])
            lns = s.sb("lns", [P, 2, NT])
            fac = s.sb("fac", [P, NT])
            rm = s.sb("rm", [P, H])
            rmt = s.sb("rmt", [H, 1])
            rdiag = s.sb("rdiag", [H, H])
            rmax = s.sb("rmax", [P, H])
            ones = s.sb("ones", [H, P])
            q = s.sb("q", [P, NT, H])
            wexp = s.sb("wexp", [P, NT, 2, H])
            val = s.sb("val", [P, 2, H, TB, DV])
            res = s.sb("res", [P, 2, H, TB, DV])
            parts = s.sb("parts", [P, 2, H, TB, 2, 3, DV], BF16)
            ps_t = s.ps("t", [P, 2, BLK])
            ps_h = s.ps("h", [P, 2, BLK])
            ps_e = s.ps("e", [P, 2, BLK])
            ps_l = s.ps("l", [P, 2, BLK])
            x_in = s.sem("x_in")
            w_in = s.sem("w_in")
            consts = s.sem("consts")
            chain_dve = s.sem("chain_dve")
            stats_done = s.sem("stats_done")
            rooted = s.sem("rooted")
            var_ready = s.sem("var_ready")
            arg_ready = s.sem("arg_ready")
            ln_ready = s.sem("ln_ready")
            wa_ps = s.sem("wa_ps")
            wa_ready = s.sem("wa_ready")
            xn_ready = s.sem("xn_ready")
            t_ps = s.sem("t_ps")
            xt_ready = s.sem("xt_ready")
            proj_ps = s.sem("proj_ps")
            hid_ready = s.sem("hid_ready")
            logit_ready = s.sem("logit_ready")
            lt_free = s.sem("lt_free")
            parts_free = s.sem("parts_free")
            lt_out = [s.sem(f"lt_out{u}") for u in range(2)]
            rm_ready = s.sem("rm_ready")
            rm_ps = s.sem("rm_ps")
            rm_diag = s.sem("rm_diag")
            rm_all = s.sem("rm_all")
            q_ready = s.sem("q_ready")
            exp_done = s.sem("exp_done")
            parts_ready = s.sem("parts_ready")
            parts_out = [s.sem(f"parts_out{u}") for u in range(2)]

            with nc.Block() as block:
                @block.sync
                def _(sp):
                    sp.sem_inc(lt_free, 2)
                    sp.sem_inc(parts_free, 2)
                    sp.wait_ge(consts, 2)
                    for h in range(H):
                        rows = slice(h * D, (h + 1) * D)
                        sp.dma_start(a_blk[rows, h:h + 1], a_l[h, :].unsqueeze(1)).then_inc(w_in, 16)
                        sp.dma_start(a_blk[rows, H + h:H + h + 1], a_r[h, :].unsqueeze(1)).then_inc(w_in, 16)
                    with sp.Fori(0, NB // 2) as pair:
                        for u in range(2):
                            sp.wait_ge(logit_ready, pair * 2 + (u + 1 + 2))
                            sp.dma_start(left_t[:, bass.ds((pair * 2 + u) * BLK, BLK)],
                                         lt[:, u, :]).then_inc(lt_out[u], 16)
                            sp.wait_ge(lt_out[u], pair * 16 + 16)
                            sp.sem_inc(lt_free, 1)
                    with sp.Fori(0, NB // 2) as pair:
                        for u in range(2):
                            sp.wait_ge(parts_ready, pair * 2 + (u + 1))
                            sp.dma_start(values_d[:, :, bass.ds((pair * 2 + u) * TB, TB), :]
                                         .rearrange("h p t x -> p h (t x)"),
                                         parts[:, u, :, :, :, :, :].rearrange("p h t g s v -> p h (t g s v)")
                                         ).then_inc(parts_out[u], 16)
                            sp.wait_ge(parts_out[u], pair * 16 + 16)
                            sp.sem_inc(parts_free, 1)

                @block.gpsimd
                def _(pool):
                    link = Chain(pool, consts)
                    link(nc.gpsimd.memset(ident[:, :, :], 0.0))
                    link(nc.gpsimd.memset(a_blk[:, :], 0.0))
                    link(nc.gpsimd.affine_select(out=ident[:, 0, :], in_=ident[:, 0, :], compare_op=ALU.not_equal,
                                                 fill=1.0, base=0, pattern=[[-1, P]], channel_multiplier=1))
                    link(nc.gpsimd.memset(ones[:, :], 1.0))
                    link(nc.gpsimd.memset(fold[:, :], 0.0))
                    for part in range(3):
                        link(nc.gpsimd.affine_select(out=fold[:, :], in_=fold[:, :], compare_op=ALU.not_equal,
                                                     fill=1.0, base=-DV * part, pattern=[[-1, DV]],
                                                     channel_multiplier=1))

                @block.scalar
                def _(act):
                    for b in range(4):
                        tiles = slice(b * NT // 4, (b + 1) * NT // 4)
                        act.dma_start(xin[:, tiles, :], x_tiles[:, tiles, :]).then_inc(x_in, 16)
                    act.dma_start(w_nat[:, :], W).then_inc(w_in, 16)
                    act.dma_start(w_t[:, :], W_T).then_inc(w_in, 16)
                    act.sem_inc(hid_ready, 2)
                    act.wait_ge(var_ready, 1)
                    nc.scalar.activation(root[:, 0, :], tmp[:, :], ACT.Sqrt).then_inc(rooted, 1)
                    nc.scalar.activation(root[:, 1, :], var[:, :], ACT.Sqrt, scale=float(C)).then_inc(rooted, 1)
                    act.wait_ge(arg_ready, 1)
                    nc.scalar.activation(lns[:, :, :], arg[:, :, :], ACT.Ln).then_inc(ln_ready, 1)
                    with act.Fori(0, NB // 2) as pair:
                        for u in range(2):
                            act.wait_ge(t_ps, pair * 2 + (u + 1))
                            nc.scalar.activation(xt[:, u, :], ps_t[:, u, :], ACT.Copy).then_inc(xt_ready, 1)
                            act.wait_ge(proj_ps, pair * 2 + (u + 1))
                            nc.scalar.activation(hid[:, bass.ds((pair * 2 + u) * TB, TB), :],
                                                 ps_h[:, u, :].rearrange("p (t c) -> p t c", c=C),
                                                 ACT.Copy).then_inc(hid_ready, 1)
                    act.wait_ge(q_ready, 1)
                    nc.scalar.activation(wexp[:, :, 0, :], q[:, :, :], ACT.Exp).then_inc(exp_done, 1)
                    nc.scalar.activation(wexp[:, :, 1, :], q[:, :, :], ACT.Exp, scale=0.2).then_inc(exp_done, 1)
                    act.wait_ge(q_ready, 2)
                    nc.scalar.activation(scale01[:, :, :, :], scale01[:, :, :, :], ACT.Exp).then_inc(exp_done, 1)

                @block.vector
                def _(dve):
                    link = Chain(dve, chain_dve)
                    dve.sem_inc(logit_ready, 2)
                    dve.wait_ge(x_in, 16 * 4)
                    with dve.Fori(0, NT // UNROLL) as group:
                        for i in range(UNROLL):
                            nc.vector.bn_stats(stats[:, group * UNROLL + i, :],
                                               xin[:, group * UNROLL + i, :]).then_inc(stats_done, 1)
                    dve.wait_ge(stats_done, NT)
                    row_statistics(nc, link, stats, mean[:, :], var[:, :], tmp[:, :])
                    nc.vector.tensor_scalar(tmp[:, :], var[:, :], LN_EPS, None, ALU.add).then_inc(var_ready, 1)
                    dve.wait_ge(rooted, 1)
                    link(nc.vector.reciprocal(rstd[:, :], root[:, 0, :]))
                    dve.wait_ge(rooted, 2)
                    link(nc.vector.tensor_tensor(norm[:, :], root[:, 1, :], rstd[:, :], ALU.mult))
                    link(nc.vector.tensor_scalar(norm[:, :], norm[:, :], 1e-15, None, ALU.max))
                    link(nc.vector.tensor_scalar(fac[:, :], norm[:, :], 1.0 - 1e-5, None, ALU.min))
                    link(nc.vector.tensor_scalar(arg[:, 0, :], fac[:, :], 1.0, None, ALU.add))
                    nc.vector.tensor_scalar(arg[:, 1, :], fac[:, :], -1.0, 1.0, ALU.mult, ALU.add).then_inc(arg_ready, 1)
                    dve.wait_ge(ln_ready, 1)
                    link(nc.vector.tensor_tensor(fac[:, :], lns[:, 0, :], lns[:, 1, :], ALU.subtract))
                    link(nc.vector.tensor_scalar(fac[:, :], fac[:, :], 0.5, None, ALU.mult))
                    link(nc.vector.reciprocal(norm[:, :], norm[:, :]))
                    link(nc.vector.tensor_tensor(fac[:, :], fac[:, :], norm[:, :], ALU.mult))
                    link(nc.vector.tensor_tensor(fac[:, :], fac[:, :], rstd[:, :], ALU.mult))
                    dve.wait_ge(wa_ps, 1)
                    nc.vector.tensor_copy(wa[:, :], ps_e[:, 0, 0:2 * H]).then_inc(wa_ready, 1)

                    def scale_rows(b, u):
                        for i in range(TB):
                            op = nc.vector.tensor_scalar(xn[:, u, i, :], xin[:, b * TB + i, :],
                                                         mean[:, bass.ds(b * TB + i, 1)],
                                                         fac[:, bass.ds(b * TB + i, 1)],
                                                         ALU.subtract, ALU.mult)
                        op.then_inc(xn_ready, 1)

                    def logits(b, u):
                        dve.wait_ge(proj_ps, b + 1)
                        nc.vector.tensor_scalar(logit[:, bass.ds(b * TB, TB), :, :],
                                                ps_e[:, u, 0:TB * 2 * H]
                                                .rearrange("p (t s h) -> p t s h", t=TB, s=2), 1.0, None, ALU.mult)
                        dve.wait_ge(lt_free, b + 1)
                        nc.vector.tensor_copy(lt[:, u, :], ps_l[0:H, u, :]).then_inc(logit_ready, 1)

                    scale_rows(0, 0)
                    with dve.Fori(0, NB // 2 - 1) as pair:
                        for u in range(2):
                            scale_rows(pair * 2 + (u + 1), 1 - u)
                            logits(pair * 2 + u, u)
                    scale_rows(NB - 1, 1)
                    for u in range(2):
                        logits(NB - 2 + u, u)
                    dve.wait_ge(logit_ready, NB + 2)
                    nc.vector.tensor_reduce(rm[:, :], logit[:, :, 1, :].rearrange("p t h -> p h t"),
                                            AX.X, ALU.max).then_inc(rm_ready, 1)
                    dve.wait_ge(rm_ps, 1)
                    link(nc.vector.tensor_reduce(rmt[:, :], ps_t[0:H, 0, 0:P], AX.X, ALU.max))
                    nc.vector.tensor_scalar(rdiag[:, :], ident[0:H, 0, 0:H], rmt[:, 0:1], None,
                                            ALU.mult).then_inc(rm_diag, 1)
                    dve.wait_ge(rm_ps, 2)
                    link(nc.vector.tensor_copy(rmax[:, :], ps_e[:, 0, 0:H]))
                    rb = rmax[:, :].unsqueeze(1).to_broadcast([P, NT, H])
                    nc.vector.tensor_tensor(q[:, :, :], logit[:, :, 1, :], rb, ALU.subtract).then_inc(q_ready, 1)
                    link(nc.vector.tensor_copy(right[:, :, :], logit[:, :, 1, :]))
                    link(nc.vector.tensor_tensor(logit[:, :, 0, :], logit[:, :, 0, :], rb, ALU.add))
                    link(nc.vector.tensor_scalar(scale01[:, :, 0, :], logit[:, :, 0, :], 0.8, 0.0, ALU.mult, ALU.min))
                    nc.vector.tensor_scalar(scale01[:, :, 1, :], logit[:, :, 0, :], -0.8, 0.0, ALU.mult,
                                            ALU.min).then_inc(q_ready, 1)
                    dve.wait_ge(exp_done, 2)
                    dve.wait_ge(hid_ready, NB + 2)
                    per_block = 2 * 6
                    first = link.count
                    with dve.Fori(0, NB // 2) as pair:
                        for u in range(2):
                            b = pair * 2 + u
                            base = b * per_block + first

                            def hold(n):
                                dve.wait_ge(chain_dve, base + n)

                            w = [wexp[:, bass.ds(b * TB, TB), g, :].rearrange("p t h -> p h t").unsqueeze(3)
                                 for g in range(2)]
                            hv = hid[:, bass.ds(b * TB, TB), :].rearrange("p t (h d) -> p h t d", h=H)
                            part = [[parts[:, u, :, :, g, i, :] for i in range(3)] for g in range(2)]
                            for g in range(2):
                                nc.vector.tensor_tensor(val[:, g, :, :, 0:D], hv, w[g].to_broadcast([P, H, TB, D]),
                                                        ALU.mult).then_inc(chain_dve, 1)
                            for g in range(2):
                                nc.vector.tensor_scalar(val[:, g, :, :, D:DV], w[g], 1.0, None,
                                                        ALU.mult).then_inc(chain_dve, 1)
                            dve.wait_ge(parts_free, b + 1)
                            for g in range(2):
                                hold(3 + g)
                                nc.vector.tensor_scalar(part[g][0], val[:, g], 1.0, None,
                                                        ALU.mult).then_inc(chain_dve, 1)
                            for g in range(2):
                                hold(5 + g)
                                nc.vector.tensor_tensor(res[:, g], val[:, g], part[g][0],
                                                        ALU.subtract).then_inc(chain_dve, 1)
                            for g in range(2):
                                hold(7 + g)
                                nc.vector.tensor_scalar(part[g][1], res[:, g], 1.0, None,
                                                        ALU.mult).then_inc(chain_dve, 1)
                            for g in range(2):
                                hold(9 + g)
                                nc.vector.tensor_tensor(part[g][2], res[:, g], part[g][1],
                                                        ALU.subtract).then_inc(chain_dve, 1)
                            hold(per_block)
                            dve.sem_inc(parts_ready, 1)

                @block.tensor
                def _(pe):
                    pe.wait_ge(consts, 8)
                    pe.wait_ge(w_in, 16 * 10)
                    nc.tensor.matmul(ps_e[:, 0, 0:2 * H], w_nat[:, :], a_blk[:, :], start=True,
                                     stop=True).then_inc(wa_ps, 1)
                    pe.wait_ge(wa_ready, 1)
                    with pe.Fori(0, NB // 2) as pair:
                        for u in range(2):
                            b = pair * 2 + u
                            pe.wait_ge(xn_ready, b + 1)
                            for i in range(TB):
                                op = nc.tensor.transpose(ps_t[:, u, i * P:(i + 1) * P], xn[:, u, i, :], ident[:, 0, :])
                            op.then_inc(t_ps, 1)
                            pe.wait_ge(xt_ready, b + 1)
                            pe.wait_ge(hid_ready, b + 1)
                            pe.wait_ge(logit_ready, b + 1)
                            for i in range(TB):
                                rows = xt[:, u, i * P:(i + 1) * P]
                                nc.tensor.matmul(ps_h[:, u, i * C:(i + 1) * C], rows, w_t[:, :], start=True, stop=True)
                                nc.tensor.matmul(ps_e[:, u, i * 2 * H:(i + 1) * 2 * H], rows, wa[:, :],
                                                 start=True, stop=True)
                            nc.tensor.matmul(ps_l[0:H, u, :], wa[:, 0:H], xt[:, u, :], start=True,
                                             stop=True).then_inc(proj_ps, 1)
                    pe.wait_ge(rm_ready, 1)
                    nc.tensor.transpose(ps_t[0:H, 0, 0:P], rm[:, :], ident[:, 0, :]).then_inc(rm_ps, 1)
                    pe.wait_ge(rm_diag, 1)
                    nc.tensor.matmul(ps_e[:, 0, 0:H], ones[:, :], rdiag[:, :], start=True, stop=True).then_inc(rm_ps, 1)

        attention_sweep(nc, N, adj, left_t, values_d, sums_d, right, scale01, ident, fold)



def attention_sweep(nc, N, adj, left_t, values_d, sums_d, right, scale01, ident, fold):
    NT = N // P
    WT = 8
    WB = WT * P
    NW = N // WB
    HALF = BLK
    ST = 2
    BT = 16
    NBODY = NT // BT
    LT = 2
    R = 4
    ONE = 0x38
    DVH = 3 * DV
    assert NT % BT == 0 and NW & (NW - 1) == 0
    U8, I8, F8 = mybir.dt.uint8, mybir.dt.int8, mybir.dt.float8e4
    adj_rows = adj.rearrange("(t p) c -> p t c", p=P)

    with ExitStack() as ctx:
        s = Scope(nc, ctx, "att")
        adjr = s.sb("adjr", [P, 2, WT, LT * P])
        rows_mask = s.sb("rows_mask", [P, 2, WT, LT * P], BF16)
        ident16 = s.sb("ident16", [P, P], BF16)
        mask = s.sb("mask", [P, 2 * NT, WB], U8)
        left = s.sb("left", [P, 2, WB])
        vals = s.sb("vals", [P, 2, BT // 2, 2, DVH], BF16)
        side = s.sb("side", [P, R, ST, WB], I8)
        sel = s.sb("sel", [P, R, 2, ST, WB], U8)
        neg_right = s.sb("neg_right", [P, NBODY, H])
        accs = s.sb("accs", [P, 4, HALF])
        num = s.sb("num", [P, WT, H, DV])
        half = s.sb("half", [P, WT // 2, DV])
        ps_acc = s.ps("acc", [P, 4, HALF])
        ps_t = s.ps("t", [P, 2, WB], BF16)
        ps_f = s.ps("f", [P, 2, HALF])

        adj_in = [s.sem(f"adj_in{u}") for u in range(2)]
        adj_ready = s.sem("adj_ready")
        rows_dve = s.sem("rows_dve")
        diag_done = s.sem("diag_done")
        ident_ready = s.sem("ident_ready")
        t_ps = s.sem("t_ps")
        mask_ready = s.sem("mask_ready")
        left_in = [s.sem(f"left_in{u}") for u in range(2)]
        vals_in = [s.sem(f"vals_in{u}") for u in range(2)]
        side_act = s.sem("side_act")
        side_dve = s.sem("side_dve")
        sel1_ready = s.sem("sel1_ready")
        sel0_ready = s.sem("sel0_ready")
        sel_free = s.sem("sel_free")
        acc_act = s.sem("acc_act")
        acc_dve = s.sem("acc_dve")
        fold_ps = s.sem("fold_ps")
        num_ready = s.sem("num_ready")
        num_out = s.sem("num_out")
        num_free = s.sem("num_free")
        chain_dve = s.sem("chain_dve")
        carried_pe = s.sem("carried_pe")
        carried_pool = s.sem("carried_pool")
        A0, T0, M0, L0, F0 = 2, 4, 2, 4, 6
        STEPS = BT // ST
        PER_PASS = NBODY * STEPS
        GROUPS = NT // 4
        LOG_NW = NW.bit_length() - 1
        DVE_STEP, DVE_TILE = 3, 1
        CHAINED = 6

        def blocks(engine, head_pass, end):
            def block(ib, produce):
                for h in range(H):
                    head_pass(ib, h, 0, produce)
                    if NBODY > 1:
                        with engine.Fori(1, NBODY) as jb:
                            head_pass(ib, h, jb, produce)
                end(ib)

            if NW > 1:
                with engine.Fori(0, NW - 1) as ib:
                    block(ib, True)
            block(NW - 1, False)

        def starts(jb):
            return isinstance(jb, int) and jb == 0

        def body_number(ib, h, jb):
            return ib * (H * NBODY) + jb + h * NBODY

        with nc.Block() as block:
            @block.sync
            def _(sp):
                def load_adj(ib, group, u):
                    sp.wait_ge(adj_ready, ib * (GROUPS * 2) + group * 2 + (A0 - 1 + u))
                    sp.dma_start(adjr[:, u, :, :],
                                 adj_rows[:, bass.ds(ib * WT, WT), bass.ds((group * 2 + u) * (LT * P), LT * P)]
                                 ).then_inc(adj_in[u], 16)

                def load_left(ib, h):
                    row = left_t[h:h + 1, bass.ds(ib * WB, WB)].squeeze(0)
                    sp.dma_start(left[:, h % 2, :], row.partition_broadcast(P)).then_inc(left_in[h % 2], 16)

                def head_pass(ib, h, jb, produce):
                    number = body_number(ib, h, jb)
                    for u in range(2):
                        if produce:
                            load_adj(ib + 1, jb + h * NBODY, u)
                        sp.wait_ge(sel_free, number * STEPS + (F0 - STEPS // 2 * (1 - u)))
                        sp.dma_start(vals[:, u, :, :, :].rearrange("p t g x -> p (t g x)"),
                                     values_d[h, :, bass.ds(jb * BT + u * (BT // 2), BT // 2), :]
                                     .rearrange("p t x -> p (t x)")).then_inc(vals_in[u], 16)
                    if starts(jb) and (h < H - 1 or produce):
                        load_left(ib if h < H - 1 else ib + 1, (h + 1) % H)

                load_left(0, 0)
                with sp.Fori(0, GROUPS) as group:
                    for u in range(2):
                        load_adj(0, group, u)
                blocks(sp, head_pass, lambda ib: None)

            @block.gpsimd
            def _(pool):
                pool.sem_inc(num_free, 1)

                pool.sem_inc(adj_ready, A0)

                def add_identity(ib, group, u):
                    away = ((group >> 1) + ib * (NW - 1)) & (NW - 1)
                    away = pool.snap((away + (NW - 1)) >> LOG_NW)
                    odd = pool.snap((group & 1) * 4)
                    if not isinstance(away, int):
                        away = away.with_bounds(min_val=0, max_val=1)
                    add = ident[:, bass.ds(away, 1), :].squeeze(1)
                    pool.wait_ge(adj_in[u], ib * (GROUPS * 16) + group * 16 + 16)
                    pool.sem_inc(carried_pool, 1)
                    for m in range(LT):
                        diag = adjr[:, u, bass.ds(odd + (2 * u + m), 1), m * P:(m + 1) * P].squeeze(1)
                        nc.gpsimd.tensor_tensor(diag, diag, add, ALU.add).then_inc(diag_done, 1)

                def compare(ib, group, u):
                    pool.wait_ge(diag_done, ib * (GROUPS * 4) + group * 4 + (u + 1) * LT)
                    pool.wait_ge(t_ps, ib * (GROUPS * 4) + group * 4 + (T0 - 2 + 2 * u))
                    pool.sem_inc(carried_pool, 1)
                    nc.gpsimd.tensor_scalar(rows_mask[:, u, :, :], adjr[:, u, :, :], 0.0, None,
                                            ALU.is_gt).then_inc(adj_ready, 1)

                def head_pass(ib, h, jb, produce):
                    if produce:
                        for u in range(2):
                            add_identity(ib + 1, jb + h * NBODY, u)
                            compare(ib + 1, jb + h * NBODY, u)

                def end(ib):
                    pool.wait_ge(num_ready, ib * H + (H + 1))
                    pool.dma_start(sums_d[bass.ds(ib * WT, WT), :, :].rearrange("t p x -> p t x"),
                                   num[:, :, :, :].rearrange("p t h v -> p t (h v)")).then_inc(num_out, 16)
                    pool.wait_ge(num_out, ib * 16 + 16)
                    pool.sem_inc(num_free, 1)

                with pool.Fori(0, GROUPS) as group:
                    for u in range(2):
                        add_identity(0, group, u)
                    for u in range(2):
                        pool.wait_ge(rows_dve, group * 2 + (u + 1))
                        pool.sem_inc(adj_ready, 1)
                blocks(pool, head_pass, end)
                pool.wait_ge(num_out, 16 * NW)

            @block.scalar
            def _(act):
                act.sem_inc(sel1_ready, L0)
                act.sem_inc(fold_ps, 1)

                def copy_sums(ib, h):
                    act.wait_ge(sel_free, ib * (H * PER_PASS) + ((h + 1) * PER_PASS + F0))
                    act.wait_ge(fold_ps, ib * H + (h + 1))
                    for a in range(2):
                        nc.scalar.activation(accs[0:DVH, a, :], ps_acc[0:DVH, a, :], ACT.Copy).then_inc(acc_act, 1)

                def head_pass(ib, h, jb, produce):
                    number = body_number(ib, h, jb)
                    for k in range(STEPS):
                        act.wait_ge(sel1_ready, number * STEPS + (k + L0 - R + 1))
                        if starts(jb) and k == 0:
                            act.wait_ge(left_in[h % 2], ib * 32 + (h // 2 + 1) * 16)
                        for j in range(ST):
                            if (k, j) != (DVE_STEP, DVE_TILE):
                                op = nc.scalar.activation(side[:, k % R, j, :], left[:, h % 2, :], ACT.Sign,
                                                          bias=right[:, jb * BT + (k * ST + j), h:h + 1])
                        op.then_inc(side_act, 1)
                        if starts(jb) and h > 0 and k == 1:
                            copy_sums(ib, h - 1)

                blocks(act, head_pass, lambda ib: copy_sums(ib, H - 1))

            @block.vector
            def _(dve):
                dve.sem_inc(num_ready, 1)
                dve.sem_inc(mask_ready, M0)
                nc.vector.tensor_scalar(neg_right[:, :, :], right[:, DVE_STEP * ST + DVE_TILE::BT, :], -1.0, None,
                                        ALU.mult).then_inc(side_dve, 1)
                dve.wait_ge(side_dve, 1)
                nc.vector.tensor_copy(ident16[:, :], ident[:, 0, :]).then_inc(ident_ready, 1)
                mask32 = mask[:, :, :].bitcast(UINT32)
                side32 = side[:, :, :, :].bitcast(UINT32)
                sel32 = sel[:, :, :, :, :].bitcast(UINT32)

                def make_mask(ib, group, i):
                    tile = ib * (GROUPS * 4) + group * 4 + i
                    dve.wait_ge(t_ps, tile + (T0 + 1))
                    row = (ib & 1) * NT + group * 4 + i
                    nc.vector.tensor_scalar(mask[:, bass.ds(row, 1), :].squeeze(1), ps_t[:, i % 2, :], float(ONE), None,
                                            ALU.mult).then_inc(mask_ready, 1)

                def copy_sums(ib, h):
                    dve.wait_ge(sel_free, ib * (H * PER_PASS) + ((h + 1) * PER_PASS + F0))
                    dve.wait_ge(fold_ps, ib * H + (h + 1))
                    for a in range(2, 4):
                        nc.vector.tensor_copy(accs[0:DVH, a, :], ps_acc[0:DVH, a, :]).then_inc(acc_dve, 1)

                def sum_branches(ib, h):
                    link = Chain(dve, chain_dve, ib * (H * CHAINED) + h * CHAINED)
                    dve.wait_ge(fold_ps, ib * H + (h + 2))
                    if h == 0:
                        dve.wait_ge(num_free, ib + 1)
                    for b in range(2):
                        folded = ps_f[:, b, 0:4 * 2 * DV].rearrange("p (i g v) -> p g i v", i=4, g=2)
                        tiles = bass.ds(ib * WT + b * 4, 4)
                        out = num[:, b * 4:b * 4 + 4, h, :]
                        row = [scale01[:, tiles, g, h:h + 1].to_broadcast([P, 4, DV]) for g in range(2)]
                        link(nc.vector.tensor_tensor(half[:, :, :], folded[:, 0], row[0], ALU.mult))
                        link(nc.vector.tensor_tensor(out, folded[:, 1], row[1], ALU.mult))
                        link(nc.vector.tensor_tensor(out, out, half[:, :, :], ALU.add))
                    assert link.ops == CHAINED
                    dve.sem_inc(num_ready, 1)

                def head_pass(ib, h, jb, produce):
                    number = body_number(ib, h, jb)
                    for k in range(STEPS):
                        step = number * STEPS + k
                        if k == DVE_STEP:
                            nc.vector.tensor_scalar(side[:, k % R, DVE_TILE, :].bitcast(U8), left[:, h % 2, :],
                                                    neg_right[:, jb, h:h + 1], 255.0,
                                                    ALU.is_lt, ALU.mult).then_inc(side_dve, 1)
                            dve.wait_ge(side_dve, number + 2)
                        dve.wait_ge(side_act, step + 1)
                        dve.wait_ge(sel_free, step + (F0 - R + 1))
                        rows = mask32[:, bass.ds((ib & 1) * NT + jb * BT + k * ST, ST), :]
                        nc.vector.tensor_tensor(sel32[:, k % R, 1, :, :], side32[:, k % R, :, :], rows,
                                                ALU.bitwise_and).then_inc(sel1_ready, 1)
                        dve.wait_ge(sel1_ready, step + (L0 + 1))
                        nc.vector.tensor_tensor(sel32[:, k % R, 0, :, :], sel32[:, k % R, 1, :, :], rows,
                                                ALU.bitwise_xor).then_inc(sel0_ready, 1)
                        if starts(jb) and h > 0:
                            if k == 0:
                                copy_sums(ib, h - 1)
                            if k == 3:
                                sum_branches(ib, h - 1)
                        if produce and k in (2, 4, 6):
                            make_mask(ib + 1, jb + h * NBODY, k // 2 - 1)
                    if produce:
                        make_mask(ib + 1, jb + h * NBODY, 3)

                def end(ib):
                    copy_sums(ib, H - 1)
                    sum_branches(ib, H - 1)

                with dve.Fori(0, GROUPS) as group:
                    for u in range(2):
                        dve.wait_ge(diag_done, group * 4 + (u + 1) * LT)
                        dve.wait_ge(t_ps, group * 4 + (T0 - 2 + 2 * u))
                        nc.vector.tensor_scalar(rows_mask[:, u, :, :], adjr[:, u, :, :], 0.0, None,
                                                ALU.is_gt).then_inc(rows_dve, 1)
                    for i in range(4):
                        make_mask(0, group, i)
                dve.wait_ge(mask_ready, NT + M0)
                blocks(dve, head_pass, end)

            @block.tensor
            def _(pe):
                pe.sem_inc(sel_free, F0)
                pe.sem_inc(t_ps, T0)
                pe.sem_inc(acc_act, 1)
                pe.sem_inc(acc_dve, 1)

                def transposes(ib, group, i):
                    if i % LT == 0:
                        pe.wait_ge(adj_ready, ib * (GROUPS * 2) + group * 2 + (i // LT + A0 + 1))
                    pe.wait_ge(mask_ready, ib * (GROUPS * 4) + group * 4 + (i + M0 - 1))
                    for t in range(WT):
                        op = nc.tensor.transpose(ps_t[:, i % 2, t * P:(t + 1) * P],
                                                 rows_mask[:, i // LT, t, (i % LT) * P:(i % LT + 1) * P],
                                                 ident16[:, :])
                    op.then_inc(t_ps, 1)

                def fold_sums(ib, h):
                    pe.wait_ge(num_ready, ib * H + (h + 1))
                    for copied in (acc_act, acc_dve):
                        pe.wait_ge(copied, ib * (H * 2) + ((h + 1) * 2 + 1))
                    for t in range(WT):
                        for g in range(2):
                            at = (t % 4) * 2 * DV + g * DV
                            op = nc.tensor.matmul(ps_f[:, t // 4, at:at + DV],
                                                  accs[0:DVH, g * 2 + t // 4, (t % 4) * P:(t % 4 + 1) * P],
                                                  fold[:, :], start=True, stop=True)
                    op.then_inc(fold_ps, 1)

                def head_pass(ib, h, jb, produce):
                    number = body_number(ib, h, jb)
                    for k in range(STEPS):
                        step = number * STEPS + k
                        if produce and k % 2 == 0:
                            transposes(ib + 1, jb + h * NBODY, k // 2)
                        if k % (STEPS // 2) == 0:
                            pe.wait_ge(vals_in[k // (STEPS // 2)], number * 16 + 16)
                        for g, ready in ((1, step + (L0 + 1)), (0, step + 1)):
                            if starts(jb) and k == 0:
                                pe.wait_ge((acc_act, acc_dve)[g], ib * (H * 2) + (h * 2 + 1))
                            pe.wait_ge((sel0_ready, sel1_ready)[g], ready)
                            pe.sem_inc(carried_pe, 1)
                            for j in range(ST):
                                for a in range(2):
                                    op = nc.tensor.matmul(
                                        ps_acc[0:DVH, g * 2 + a, :],
                                        vals[:, k // (STEPS // 2), (k * ST + j) % (BT // 2), g, :],
                                        sel[:, k % R, g, j, a * HALF:(a + 1) * HALF].bitcast(F8),
                                        start=(starts(jb) and k == 0 and j == 0), stop=False, skip_group_check=True)
                        op.then_inc(sel_free, 1)
                        if starts(jb) and h > 0 and k == 1:
                            fold_sums(ib, h - 1)

                pe.wait_ge(ident_ready, 1)
                with pe.Fori(0, GROUPS) as group:
                    for i in range(4):
                        transposes(0, group, i)
                blocks(pe, head_pass, lambda ib: fold_sums(ib, H - 1))


HM = 4
PM = 64
DI = HM * PM
S = 64
TAPS = 4
SSM_EPS = 1e-5


def mamba_layer(nc, x, sums_d, bias, w_zdt, w_xbc, conv_w, conv_b, dt_bias, a_log, d_skip, norm_w, w_out_t, w_lin, b_lin, xr):
    N = x.shape[0]
    NT, NB = N // P, N // BLK
    x_tiles = x.rearrange("(t p) c -> p t c", p=P)

    keep = ExitStack()
    with keep:
        k = Scope(nc, keep, "ssm")
        ut = k.sb("ut", [C, N])
        wz = k.sb("wz", [C, DI + HM])
        wx = k.sb("wx", [C, DI + 2 * S])
        wc = k.sb("wc", [P, 2, C])
        cw = k.sb("cw", [P, 3, TAPS])
        cb = k.sb("cb", [P, 3])
        dskip = k.sb("dskip", [P, HM])
        ident = k.sb("ident", [P, P])
        upto = k.sb("upto", [P, P])
        after = k.sb("after", [P, P])
        dt = k.sb("dt", [P, NT, HM])
        da = k.sb("da", [P, NT, HM])
        decay = k.sb("decay", [P, 3, NT, HM])

        with ExitStack() as ctx:
            s = Scope(nc, ctx, "ssmprep")
            Q = 4
            TQ = NT // Q
            sums = s.sb("sums", [P, 2, TQ, H, DV])
            rec = s.sb("rec", [P, NT, H])
            att = s.sb("att", [P, 2, TQ, C])
            tanh = s.sb("tanh", [P, TQ, C])
            sq = s.sb("sq", [P, NT])
            vn = s.sb("vn", [P, NT])
            tn = s.sb("tn", [P, NT])
            arow = s.sb("arow", [P, C])
            sums_in = [s.sem(f"sums_in{u}") for u in range(2)]
            out_ready = s.sem("out_ready")
            tanh_done = s.sem("tanh_done")
            silu_ready = s.sem("silu_ready")
            square_done = s.sem("square_done")
            norm_ready = s.sem("norm_ready")
            normed = s.sem("normed")
            sums_used = s.sem("sums_used")
            xn = s.sb("xn", [P, 2, TB, C])
            stats = s.sb("stats", [P, NT, 6])
            mean = s.sb("mean", [P, NT])
            var = s.sb("var", [P, NT])
            tmp = s.sb("tmp", [P, NT])
            root = s.sb("root", [P, NT])
            rstd = s.sb("rstd", [P, NT])
            ones = s.sb("ones", [P, P])
            brow = s.sb("brow", [P, C])
            dtb = s.sb("dtb", [P, HM])
            al = s.sb("al", [P, HM])
            wot = s.sb("wot", [C, DI])
            wl = s.sb("wl", [C, C])
            nw = s.sb("nw", [P, 2])
            f = s.sb("f", [P, 6, NT, HM])
            ps_t = s.ps("t", [P, 2, BLK])
            ps_d = s.ps("d", [P, BLK])
            ps_w = s.ps("w", [P, BLK])
            ps_a = s.ps("a", [P, 3, BLK])
            x_in = s.sem("x_in")
            w_in = s.sem("w_in")
            consts = s.sem("consts")
            chain_dve = s.sem("chain_dve")
            stats_done = s.sem("stats_done")
            var_ready = s.sem("var_ready")
            rooted = s.sem("rooted")
            xn_ready = s.sem("xn_ready")
            t_ps = s.sem("t_ps")
            ut_ready = s.sem("ut_ready")
            dt_ps = s.sem("dt_ps")
            wc_ps = s.sem("wc_ps")
            abs_ready = s.sem("abs_ready")
            exps = s.sem("exps")
            one_more = s.sem("one_more")
            da_ready = s.sem("da_ready")
            sums_ps = s.sem("sums_ps")

            with nc.Block() as block:
                @block.sync
                def _(sp):
                    for qt in range(Q):
                        if qt >= 2:
                            sp.wait_ge(sums_used, qt - 1)
                        tiles = slice(qt * TQ, (qt + 1) * TQ)
                        sp.dma_start(sums[:, qt % 2, :, :, :].rearrange("p t h v -> p t (h v)"),
                                     sums_d[tiles, :, :].rearrange("t p x -> p t x")).then_inc(sums_in[qt % 2], 16)
                        if qt == 0:
                            sp.dma_start(xr[:, :, :], x_tiles).then_inc(x_in, 16)
                            sp.dma_start(arow[:, :], bias.partition_broadcast(P)).then_inc(x_in, 16)
                    sp.dma_start(wz[:, :], w_zdt).then_inc(w_in, 16)
                    sp.dma_start(wx[:, :], w_xbc).then_inc(w_in, 16)
                    sp.dma_start(cw[:, :, :], conv_w.rearrange("(g p) k -> p g k", p=P)).then_inc(w_in, 16)
                    sp.dma_start(cb[:, :], conv_b).then_inc(w_in, 16)
                    sp.dma_start(dskip[:, :], d_skip.partition_broadcast(P)).then_inc(w_in, 16)
                    sp.dma_start(brow[:, :], b_lin.partition_broadcast(P)).then_inc(w_in, 16)
                    sp.dma_start(dtb[:, :], dt_bias.partition_broadcast(P)).then_inc(w_in, 16)
                    sp.dma_start(al[:, :], a_log.partition_broadcast(P)).then_inc(w_in, 16)
                    sp.dma_start(wot[:, :], w_out_t).then_inc(w_in, 16)
                    sp.dma_start(wl[:, :], w_lin).then_inc(w_in, 16)
                    sp.dma_start(nw[:, :], norm_w).then_inc(w_in, 16)

                @block.gpsimd
                def _(pool):
                    link = Chain(pool, consts)
                    link(nc.gpsimd.memset(ident[:, :], 0.0))
                    link(nc.gpsimd.memset(ones[:, :], 1.0))
                    link(nc.gpsimd.affine_select(out=ident[:, :], in_=ident[:, :], compare_op=ALU.not_equal,
                                                 fill=1.0, base=0, pattern=[[-1, P]], channel_multiplier=1))
                    link(nc.gpsimd.affine_select(out=upto[:, :], in_=ones[:, :], compare_op=ALU.is_ge,
                                                 fill=0.0, base=0, pattern=[[1, P]], channel_multiplier=-1))
                    link(nc.gpsimd.affine_select(out=after[:, :], in_=ones[:, :], compare_op=ALU.is_gt,
                                                 fill=0.0, base=0, pattern=[[-1, P]], channel_multiplier=1))

                @block.scalar
                def _(act):
                    act.sem_inc(ut_ready, 2)
                    for qt in range(Q):
                        act.wait_ge(out_ready, qt + 1)
                        nc.scalar.activation(tanh[:, :, :], att[:, qt % 2, :, :], ACT.Tanh, scale=0.5).then_inc(tanh_done, 1)
                        act.wait_ge(silu_ready, qt + 1)
                        for i in range(TQ):
                            nc.scalar.activation(tanh[:, i, :], att[:, qt % 2, i, :], ACT.Square, scale=0.5,
                                                 accum_out=sq[:, qt * TQ + i:qt * TQ + i + 1]).then_inc(square_done, 1)
                        act.wait_ge(square_done, (qt + 1) * TQ + qt * 2)
                        nc.scalar.activation(vn[:, qt * TQ:(qt + 1) * TQ], sq[:, qt * TQ:(qt + 1) * TQ],
                                             ACT.Sqrt).then_inc(square_done, 1)
                        act.wait_ge(norm_ready, qt + 1)
                        nc.scalar.activation(tn[:, qt * TQ:(qt + 1) * TQ], vn[:, qt * TQ:(qt + 1) * TQ],
                                             ACT.Tanh).then_inc(square_done, 1)
                    act.wait_ge(var_ready, 1)
                    nc.scalar.activation(root[:, :], tmp[:, :], ACT.Sqrt).then_inc(rooted, 1)
                    with act.Fori(0, NB // 2) as pair:
                        for u in range(2):
                            b = pair * 2 + u
                            act.wait_ge(t_ps, b + 3)
                            nc.scalar.activation(ut[:, bass.ds(b * BLK, BLK)], ps_t[:, u, :],
                                                 ACT.Copy).then_inc(ut_ready, 1)
                    act.wait_ge(w_in, 16 * 11)
                    nc.scalar.activation(al[:, :], al[:, :], ACT.Exp).then_inc(exps, 1)
                    act.wait_ge(abs_ready, 1)
                    nc.scalar.activation(f[:, 2, :, :], f[:, 1, :, :], ACT.Exp, scale=-1.0).then_inc(exps, 1)
                    act.wait_ge(one_more, 1)
                    nc.scalar.activation(f[:, 4, :, :], f[:, 3, :, :], ACT.Ln).then_inc(exps, 1)
                    act.wait_ge(sums_ps, 1)
                    for i in range(3):
                        nc.scalar.activation(decay[:, i, :, :], ps_a[:, i, 0:NT * HM]
                                             .rearrange("p (t h) -> p t h", h=HM), ACT.Exp).then_inc(exps, 1)

                @block.vector
                def _(dve):
                    link = Chain(dve, chain_dve)
                    dve.wait_ge(x_in, 32)
                    for qt in range(Q):
                        tiles = slice(qt * TQ, (qt + 1) * TQ)
                        num, out = sums[:, qt % 2, :, :, :], att[:, qt % 2, :, :]
                        dve.wait_ge(sums_in[qt % 2], 16 * (qt // 2 + 1))
                        link(nc.vector.reciprocal(rec[:, tiles, :], num[:, :, :, D]))
                        link(nc.vector.tensor_tensor(out.rearrange("p t (h d) -> p t h d", h=H), num[:, :, :, 0:D],
                                                     rec[:, tiles, :].unsqueeze(3).to_broadcast([P, TQ, H, D]), ALU.mult))
                        dve.sem_inc(sums_used, 1)
                        nc.vector.tensor_tensor(out, out, arow[:, :].unsqueeze(1).to_broadcast([P, TQ, C]),
                                                ALU.add).then_inc(out_ready, 1)
                        dve.wait_ge(tanh_done, qt + 1)
                        nc.vector.scalar_tensor_tensor(out=out, in0=tanh[:, :, :], scalar=1.0, in1=out, op0=ALU.add,
                                                       op1=ALU.mult).then_inc(silu_ready, 1)
                        dve.wait_ge(square_done, (qt + 1) * TQ + qt * 2 + 1)
                        nc.vector.tensor_scalar(vn[:, tiles], vn[:, tiles], 1e-15, None, ALU.max).then_inc(norm_ready, 1)
                        dve.wait_ge(norm_ready, qt + 1)
                        link(nc.vector.reciprocal(rstd[:, tiles], vn[:, tiles]))
                        dve.wait_ge(square_done, (qt + 1) * TQ + qt * 2 + 2)
                        link(nc.vector.tensor_tensor(rstd[:, tiles], rstd[:, tiles], tn[:, tiles], ALU.mult))
                        link(nc.vector.tensor_scalar(rstd[:, tiles], rstd[:, tiles], 0.5, None, ALU.mult))
                        for i in range(TQ):
                            t = qt * TQ + i
                            op = nc.vector.scalar_tensor_tensor(out=xr[:, t, :], in0=out[:, i, :], scalar=rstd[:, t:t + 1],
                                                                in1=xr[:, t, :], op0=ALU.mult, op1=ALU.add)
                        link(op)
                    with dve.Fori(0, NT // UNROLL) as group:
                        for i in range(UNROLL):
                            nc.vector.bn_stats(stats[:, group * UNROLL + i, :],
                                               xr[:, group * UNROLL + i, :]).then_inc(stats_done, 1)
                    dve.wait_ge(stats_done, NT)
                    row_statistics(nc, link, stats, mean[:, :], var[:, :], tmp[:, :])
                    nc.vector.tensor_scalar(tmp[:, :], var[:, :], LN_EPS, None, ALU.add).then_inc(var_ready, 1)
                    dve.wait_ge(rooted, 1)
                    link(nc.vector.reciprocal(rstd[:, :], root[:, :]))
                    dve.wait_ge(w_in, 16 * 11)
                    with dve.Fori(0, NB // 2) as pair:
                        for u in range(2):
                            b = pair * 2 + u
                            dve.wait_ge(t_ps, b + 1)
                            for i in range(TB):
                                op = nc.vector.tensor_scalar(xn[:, u, i, :], xr[:, b * TB + i, :],
                                                             mean[:, bass.ds(b * TB + i, 1)],
                                                             rstd[:, bass.ds(b * TB + i, 1)],
                                                             ALU.subtract, ALU.mult)
                            op.then_inc(xn_ready, 1)
                            dve.wait_ge(xn_ready, b + 1)
                            rows = xr[:, bass.ds(b * TB, TB), :]
                            nc.vector.tensor_tensor(rows, rows, brow[:, :].unsqueeze(1).to_broadcast([P, TB, C]), ALU.add)
                    for g in range(2):
                        dve.wait_ge(wc_ps, 2)
                        link(nc.vector.tensor_scalar(wc[:, g, :], ps_w[:, g * C:(g + 1) * C], nw[:, g:g + 1], None,
                                                     ALU.mult))
                    link(nc.vector.tensor_scalar(cw[:, :, :], cw[:, :, :], 0.5, None, ALU.mult))
                    link(nc.vector.tensor_scalar(cb[:, :], cb[:, :], 0.5, None, ALU.mult))
                    v, a, e, w, lw, z = (f[:, i, :, :] for i in range(6))
                    dve.wait_ge(dt_ps, NT)
                    link(nc.vector.tensor_tensor(v, ps_d[:, 0:NT * HM].rearrange("p (t h) -> p t h", h=HM),
                                                 dtb[:, :].unsqueeze(1).to_broadcast([P, NT, HM]), ALU.add))
                    link(nc.vector.tensor_scalar(a, v, -1.0, None, ALU.mult))
                    nc.vector.tensor_tensor(a, a, v, ALU.max).then_inc(abs_ready, 1)
                    dve.wait_ge(exps, 2)
                    nc.vector.tensor_scalar(w, e, 1.0, None, ALU.add).then_inc(one_more, 1)
                    dve.wait_ge(one_more, 1)
                    link(nc.vector.tensor_scalar(a, w, -1.0, None, ALU.add))
                    link(nc.vector.tensor_scalar(z, a, 0.0, None, ALU.is_equal))
                    link(nc.vector.tensor_tensor(a, a, z, ALU.add))
                    dve.wait_ge(exps, 3)
                    link(nc.vector.tensor_tensor(lw, lw, z, ALU.add))
                    link(nc.vector.reciprocal(a, a))
                    link(nc.vector.tensor_tensor(lw, lw, a, ALU.mult))
                    link(nc.vector.tensor_tensor(lw, lw, e, ALU.mult))
                    link(nc.vector.tensor_scalar(v, v, 0.0, None, ALU.max))
                    link(nc.vector.tensor_tensor(dt[:, :, :], v, lw, ALU.add))
                    link(nc.vector.tensor_scalar(al[:, :], al[:, :], -1.0, None, ALU.mult))
                    nc.vector.tensor_tensor(da[:, :, :], dt[:, :, :], al[:, :].unsqueeze(1).to_broadcast([P, NT, HM]),
                                            ALU.mult).then_inc(da_ready, 1)

                @block.tensor
                def _(pe):
                    pe.sem_inc(t_ps, 2)
                    pe.wait_ge(consts, 5)
                    pe.wait_ge(w_in, 16 * 11)
                    for g in range(2):
                        nc.tensor.matmul(ps_w[:, g * C:(g + 1) * C], wot[:, g * P:(g + 1) * P], wl[:, :],
                                         start=True, stop=True).then_inc(wc_ps, 1)
                    with pe.Fori(0, NB // 2) as pair:
                        for u in range(2):
                            b = pair * 2 + u
                            pe.wait_ge(xn_ready, b + 1)
                            pe.wait_ge(ut_ready, b + 1)
                            for i in range(TB):
                                op = nc.tensor.transpose(ps_t[:, u, i * P:(i + 1) * P], xn[:, u, i, :], ident[:, :])
                            op.then_inc(t_ps, 1)
                    pe.wait_ge(ut_ready, NB + 2)
                    for t in range(NT):
                        nc.tensor.matmul(ps_d[:, t * HM:(t + 1) * HM], ut[:, t * P:(t + 1) * P], wz[:, DI:DI + HM],
                                         start=True, stop=True).then_inc(dt_ps, 1)
                    pe.wait_ge(da_ready, 1)
                    flat = da[:, :, :].rearrange("p t h -> p (t h)")
                    for i, sums in enumerate((upto, after, ones)):
                        op = nc.tensor.matmul(ps_a[:, i, 0:NT * HM], sums[:, :], flat, start=True, stop=True)
                    op.then_inc(sums_ps, 1)

        with ExitStack() as ctx:
            s = Scope(nc, ctx, "scan")
            ub = s.sb("ub", [C, 2, BLK])
            raw = s.sb("raw", [P, 3, TAPS - 1 + BLK])
            cv = s.sb("cv", [P, 3, BLK])
            th = s.sb("th", [P, 3, BLK])
            xs = s.sb("xs", [P, 2, 2, BLK])
            bt = s.sb("bt", [S, 2, BLK])
            ct = s.sb("ct", [S, 2, BLK])
            dal = s.sb("dal", [P, 2, HM, P])
            ex = s.sb("ex", [P, 2, HM, P])
            gm = s.sb("gm", [P, 2, P])
            mx = s.sb("mx", [P, 2, HM, P])
            xrow = s.sb("xrow", [P, 2, DI + S])
            xdt = s.sb("xdt", [P, 2, DI])
            xdec = s.sb("xdec", [P, 2, DI])
            xd = s.sb("xd", [P, 2, DI])
            hs = s.sb("hs", [S, 2, DI])
            hd = s.sb("hd", [S, DI])
            zt = s.sb("zt", [P, 2, DI])
            zs = s.sb("zs", [P, 2, DI])
            y = s.sb("y", [P, 2, DI])
            yt = s.sb("yt", [P, 2, DI])
            yo = s.sb("yo", [P, NT, C])
            ss = s.sb("ss", [P, NT])
            junk = s.sb("junk", [P, 2, DI])
            ps_e = s.ps("e", [P, BLK])
            ps_g = s.ps("g", [P, BLK])
            ps_x = s.ps("x", [P, BLK])
            ps_y = s.ps("y", [P, BLK])
            ps_s = s.ps("s", [P, BLK])
            ps_z = s.ps("z", [P, BLK])
            ps_r = s.ps("r", [P, 2, BLK])
            names = ("ub_ready raw_ps raw_ready conv_done tanh_done xs_ready seg_ps dal_ready exp_done g_ps x_ps "
                     "gm_ready mx_ready xrow_ready xdt_ready xdec_ready xd_ready yd_ps st_ps hd_ready hs_ready "
                     "z_ps zt_done zs_ready y_ready square_done yt_ps yt_ready out_ps yo_ready halo_done chain_conv "
                     "chain_y chain_end cleared rooted var_ready").split()
            sem = {n: s.sem(n) for n in names}
            YT0, YO0 = 1, 2

            def slots(engine, slot):
                slot(0, 0, 0)
                with engine.Fori(0, NB // 2 - 1) as pair:
                    for k in range(1, 2 * TB + 1):
                        slot(pair * (2 * TB) + k, k, pair * 2 + k // TB)
                for q in range(NT - 2 * TB + 1, NT):
                    slot(q, q % (2 * TB), q // TB)

            def more_chunks(q):
                return not isinstance(q, int) or q + 1 < NT

            def more_blocks(b):
                return not isinstance(b, int) or b + 1 < NB

            def heads(v):
                return v.rearrange("p (h d) -> p h d", h=HM)

            with nc.Block() as block:
                @block.gpsimd
                def _(pool):
                    def per_head(v):
                        return v.unsqueeze(2).to_broadcast([P, HM, PM])

                    def segments(i, k):
                        nc.gpsimd.tensor_tensor(dal[:, k % 2, :, :],
                                                da[:, i, :].unsqueeze(2).to_broadcast([P, HM, P]),
                                                after[:, :].unsqueeze(1).to_broadcast([P, HM, P]),
                                                ALU.mult).then_inc(sem["dal_ready"], 1)

                    def copy_block(n, u):
                        nc.gpsimd.tensor_copy(ub[:, u, :], ut[:, bass.ds(n * BLK, BLK)]).then_inc(sem["ub_ready"], 1)

                    def part_a(i, k):
                        p = k % 2
                        pool.wait_ge(sem["xrow_ready"], i + 1)
                        if k > 1:
                            pool.wait_ge(sem["yd_ps"], i - 1)
                            pool.wait_ge(sem["y_ready"], i - 1)
                        rows = heads(xrow[:, p, 0:DI])
                        nc.gpsimd.tensor_tensor(heads(xdt[:, p, :]), rows, per_head(dt[:, i, :]),
                                                ALU.mult).then_inc(sem["xdt_ready"], 1)
                        nc.gpsimd.tensor_tensor(heads(xd[:, p, :]), rows, per_head(dskip[:, :]),
                                                ALU.mult).then_inc(sem["xd_ready"], 1)
                        pool.wait_ge(sem["xdt_ready"], i + 1)
                        nc.gpsimd.tensor_tensor(heads(xdec[:, p, :]), heads(xdt[:, p, :]),
                                                per_head(decay[:, 1, i, :]), ALU.mult).then_inc(sem["xdec_ready"], 1)

                    def slot(q, k, b):
                        if k > 0:
                            pool.wait_ge(sem["hs_ready"], q)
                        nc.gpsimd.tensor_tensor(heads(hd[:, :]), heads(hs[:, k % 2, :]),
                                                decay[0:S, 2, q, :].unsqueeze(2).to_broadcast([S, HM, PM]),
                                                ALU.mult).then_inc(sem["hd_ready"], 1)
                        if more_chunks(q):
                            part_a(q + 1, k + 1)
                        if not isinstance(q, int) or q + 2 < NT:
                            pool.wait_ge(sem["seg_ps"], q + 1)
                            segments(q + 2, k + 2)
                        if k % TB == 0 and more_blocks(b):
                            if k > 0:
                                pool.wait_ge(sem["z_ps"], q)
                            copy_block(b + 1, (k // TB + 1) % 2)

                    nc.gpsimd.memset(raw[:, :, :], 0.0).then_inc(sem["cleared"], 1)
                    nc.gpsimd.memset(hs[:, :, :], 0.0).then_inc(sem["cleared"], 1)
                    pool.wait_ge(sem["cleared"], 2)
                    copy_block(0, 0)
                    segments(0, 0)
                    segments(1, 1)
                    part_a(0, 0)
                    slots(pool, slot)

                @block.scalar
                def _(act):
                    def copy_raw(n, g):
                        if g == 0 and (not isinstance(n, int) or n > 0):
                            act.wait_ge(sem["halo_done"], n)
                        act.wait_ge(sem["raw_ps"], n * 3 + (g + 1))
                        nc.scalar.activation(raw[:, g, TAPS - 1:], ps_r[:, g % 2, :],
                                             ACT.Copy).then_inc(sem["raw_ready"], 1)

                    def tanh(n, g):
                        act.wait_ge(sem["conv_done"], n * 3 + (g + 1))
                        nc.scalar.activation(th[:, g, :], cv[:, g, :], ACT.Tanh).then_inc(sem["tanh_done"], 1)

                    def part_a(i, k):
                        p = k % 2
                        act.wait_ge(sem["seg_ps"], i + 1)
                        if k > 0:
                            act.wait_ge(sem["mx_ready"], i)
                        nc.scalar.activation(ex[:, p, :, :].rearrange("p h l -> p (h l)"), ps_e[:, :],
                                             ACT.Exp).then_inc(sem["exp_done"], 1)
                        act.wait_ge(sem["x_ps"], i + 1)
                        nc.scalar.activation(xrow[:, p, :], ps_x[:, 0:DI + S],
                                             ACT.Copy).then_inc(sem["xrow_ready"], 1)
                        act.wait_ge(sem["z_ps"], i + 1)
                        nc.scalar.activation(zt[:, p, :], ps_z[:, 0:DI], ACT.Tanh,
                                             scale=0.5).then_inc(sem["zt_done"], 1)

                    def part_c(r, k):
                        p = k % 2
                        act.wait_ge(sem["y_ready"], r + 1)
                        nc.scalar.activation(junk[:, p, :], y[:, p, :], ACT.Square,
                                             accum_out=ss[:, bass.ds(r, 1)]).then_inc(sem["square_done"], 1)
                        act.wait_ge(sem["yt_ps"], r + (YT0 + 1))
                        nc.scalar.activation(yt[:, p, :], ps_g[:, P:P + DI], ACT.Copy).then_inc(sem["yt_ready"], 1)
                        act.wait_ge(sem["out_ps"], r + 1)
                        nc.scalar.activation(yo[:, r, :], ps_x[:, DI + S:DI + S + C], ACT.Copy).then_inc(sem["yo_ready"], 1)

                    def slot(q, k, b):
                        c = k % TB
                        if more_chunks(q):
                            part_a(q + 1, k + 1)
                        if c in (1, 2) and more_blocks(b):
                            tanh(b + 1, c - 1)
                        if k > 0:
                            part_c(q - 1, k + 1)
                        if more_blocks(b):
                            for g in ((0, 1), (2,), (), ())[c]:
                                copy_raw(b + 1, g)
                            if c == 2:
                                tanh(b + 1, 2)

                    act.sem_inc(sem["yo_ready"], YO0)
                    act.wait_ge(sem["cleared"], 2)
                    for g in range(3):
                        copy_raw(0, g)
                    for g in range(3):
                        tanh(0, g)
                    part_a(0, 0)
                    slots(act, slot)
                    part_c(NT - 1, NT - 1)
                    act.wait_ge(sem["var_ready"], 1)
                    nc.scalar.activation(ss[:, :], ss[:, :], ACT.Sqrt).then_inc(sem["rooted"], 1)

                @block.vector
                def _(dve):
                    conv_ops = 3 * (TAPS - 1) + 1

                    def convolve(n, g):
                        link = Chain(dve, sem["chain_conv"], n * conv_ops + g * (TAPS - 1))
                        dve.wait_ge(sem["raw_ready"], n * 3 + (g + 1))
                        link(nc.vector.tensor_scalar(cv[:, g, :], raw[:, g, 0:BLK], cw[:, g, 0:1], cb[:, g:g + 1],
                                                     ALU.mult, ALU.add))
                        for j in range(1, TAPS):
                            op = nc.vector.scalar_tensor_tensor(out=cv[:, g, :], in0=raw[:, g, j:j + BLK],
                                                                scalar=cw[:, g, j:j + 1], in1=cv[:, g, :],
                                                                op0=ALU.mult, op1=ALU.add)
                            if j < TAPS - 1:
                                link(op)
                            else:
                                op.then_inc(sem["conv_done"], 1)
                        if g == 2:
                            link(nc.vector.tensor_copy(raw[:, :, 0:TAPS - 1], raw[:, :, BLK:BLK + TAPS - 1]))
                            dve.sem_inc(sem["halo_done"], 1)

                    def silu(n, g, u):
                        dve.wait_ge(sem["tanh_done"], n * 3 + (g + 1))
                        if g < 2:
                            nc.vector.scalar_tensor_tensor(out=xs[:, u, g, :], in0=th[:, g, :], scalar=1.0,
                                                           in1=cv[:, g, :], op0=ALU.add, op1=ALU.mult)
                        else:
                            for i, to in enumerate((bt, ct)):
                                rows = slice(i * S, (i + 1) * S)
                                op = nc.vector.scalar_tensor_tensor(out=to[:, u, :], in0=th[rows, g, :], scalar=1.0,
                                                                    in1=cv[rows, g, :], op0=ALU.add, op1=ALU.mult)
                            op.then_inc(sem["xs_ready"], 1)

                    def part_a(i, k):
                        p = k % 2
                        dve.wait_ge(sem["g_ps"], i + 1)
                        nc.vector.tensor_tensor(gm[:, p, :], ps_g[:, 0:P], upto[:, :],
                                                ALU.mult).then_inc(sem["gm_ready"], 1)
                        dve.wait_ge(sem["gm_ready"], i + 1)
                        dve.wait_ge(sem["exp_done"], i + 1)
                        if k > 1:
                            dve.wait_ge(sem["yd_ps"], i - 1)
                            dve.wait_ge(sem["y_ready"], i - 1)
                        nc.vector.tensor_tensor(mx[:, p, :, :], ex[:, p, :, :],
                                                gm[:, p, :].unsqueeze(1).to_broadcast([P, HM, P]),
                                                ALU.mult).then_inc(sem["mx_ready"], 1)
                        dve.wait_ge(sem["zt_done"], i + 1)
                        nc.vector.scalar_tensor_tensor(out=zs[:, p, :], in0=zt[:, p, :], scalar=1.0,
                                                       in1=ps_z[:, 0:DI], op0=ALU.add,
                                                       op1=ALU.mult).then_inc(sem["zs_ready"], 1)

                    def part_b(q, k):
                        p = k % 2
                        link = Chain(dve, sem["chain_y"], q * 3)
                        dve.wait_ge(sem["st_ps"], q + 1)
                        dve.wait_ge(sem["hd_ready"], q + 1)
                        nc.vector.tensor_tensor(hs[:, 1 - p, :], hd[:, :], ps_s[0:S, 0:DI],
                                                ALU.add).then_inc(sem["hs_ready"], 1)
                        dve.wait_ge(sem["yd_ps"], q + 1)
                        if k > 0:
                            dve.wait_ge(sem["yt_ps"], q + (YT0 - 1))
                        yy = y[:, p, :]
                        link(nc.vector.tensor_tensor(heads(yy), heads(ps_y[:, DI:2 * DI]),
                                                     decay[:, 0, q, :].unsqueeze(2).to_broadcast([P, HM, PM]),
                                                     ALU.mult))
                        link(nc.vector.tensor_tensor(yy, yy, ps_y[:, 0:DI], ALU.add))
                        dve.wait_ge(sem["xd_ready"], q + 1)
                        link(nc.vector.tensor_tensor(yy, yy, xd[:, p, :], ALU.add))
                        dve.wait_ge(sem["zs_ready"], q + 1)
                        nc.vector.tensor_tensor(yy, yy, zs[:, p, :], ALU.mult).then_inc(sem["y_ready"], 1)

                    def slot(q, k, b):
                        c, u = k % TB, (k // TB + 1) % 2
                        if c == 2 and more_blocks(b):
                            convolve(b + 1, 2)
                        if more_chunks(q):
                            part_a(q + 1, k + 1)
                        part_b(q, k)
                        if more_blocks(b):
                            if c < 2:
                                convolve(b + 1, c)
                            if 0 < c < 3:
                                silu(b + 1, c - 1, u)
                            if c == 2:
                                silu(b + 1, 2, u)

                    dve.wait_ge(sem["cleared"], 2)
                    for g in range(3):
                        convolve(0, g)
                    for g in range(3):
                        silu(0, g, 0)
                    part_a(0, 0)
                    slots(dve, slot)

                    link = Chain(dve, sem["chain_end"])
                    dve.wait_ge(sem["square_done"], NT)
                    nc.vector.tensor_scalar(ss[:, :], ss[:, :], 0.25 / DI, SSM_EPS, ALU.mult,
                                            ALU.add).then_inc(sem["var_ready"], 1)
                    dve.wait_ge(sem["rooted"], 1)
                    link(nc.vector.reciprocal(ss[:, :], ss[:, :]))
                    link(nc.vector.tensor_scalar(ss[:, :], ss[:, :], 0.5, None, ALU.mult))
                    dve.wait_ge(sem["yo_ready"], NT + YO0)
                    with dve.Fori(0, NT // UNROLL) as group:
                        for i in range(UNROLL):
                            t = group * UNROLL + i
                            nc.vector.scalar_tensor_tensor(out=xr[:, t, :], in0=yo[:, t, :], scalar=ss[:, bass.ds(t, 1)],
                                                           in1=xr[:, t, :], op0=ALU.mult,
                                                           op1=ALU.add)

                @block.tensor
                def _(pe):
                    def project(n, g, u):
                        if g == 0:
                            pe.wait_ge(sem["ub_ready"], n + 1)
                        if not isinstance(n, int) or n * 3 + g > 1:
                            pe.wait_ge(sem["raw_ready"], n * 3 + max(g - 1, 0))
                        nc.tensor.matmul(ps_r[:, g % 2, :], wx[:, g * P:(g + 1) * P], ub[:, u, :], start=True,
                                         stop=True).then_inc(sem["raw_ps"], 1)

                    def part_a(i, k, n):
                        p, u = k % 2, (k // TB) % 2
                        cols = slice(k % TB * P, (k % TB + 1) * P)
                        if k > 0:
                            pe.wait_ge(sem["zs_ready"], i)
                        nc.tensor.matmul(ps_z[:, 0:DI], ub[:, u, cols], wz[:, 0:DI], start=True,
                                         stop=True).then_inc(sem["z_ps"], 1)
                        pe.wait_ge(sem["dal_ready"], i + 1)
                        if k > 0:
                            pe.wait_ge(sem["exp_done"], i)
                        for h in range(HM):
                            op = nc.tensor.matmul(ps_e[:, h * P:(h + 1) * P], dal[:, p, h, :], upto[:, :],
                                                  start=True, stop=True)
                        op.then_inc(sem["seg_ps"], 1)
                        if k % TB == 0:
                            pe.wait_ge(sem["xs_ready"], n + 1)
                        if k > 0:
                            pe.wait_ge(sem["gm_ready"], i)
                        nc.tensor.matmul(ps_g[:, 0:P], bt[:, u, cols], ct[:, u, cols], start=True,
                                         stop=True).then_inc(sem["g_ps"], 1)
                        if k > 0:
                            pe.wait_ge(sem["yo_ready"], i + (YO0 - 2))
                        for g in range(2):
                            nc.tensor.transpose(ps_x[:, g * P:(g + 1) * P], xs[:, u, g, cols], ident[:, :])
                        nc.tensor.transpose(ps_x[:, DI:DI + S], bt[:, u, cols],
                                            ident[0:S, 0:S]).then_inc(sem["x_ps"], 1)

                    def part_b(q, k):
                        p, u = k % 2, (k // TB) % 2
                        cols = slice(k % TB * P, (k % TB + 1) * P)
                        if k > 0:
                            pe.wait_ge(sem["y_ready"], q)
                            pe.wait_ge(sem["hs_ready"], q)
                        nc.tensor.matmul(ps_y[:, DI:2 * DI], ct[:, u, cols], hs[:, p, :], start=True, stop=True)
                        pe.wait_ge(sem["xdec_ready"], q + 1)
                        nc.tensor.matmul(ps_s[0:S, 0:DI], xrow[:, p, DI:DI + S], xdec[:, p, :], start=True,
                                         stop=True).then_inc(sem["st_ps"], 1)
                        pe.wait_ge(sem["mx_ready"], q + 1)
                        for h in range(HM):
                            op = nc.tensor.matmul(ps_y[:, h * PM:(h + 1) * PM], mx[:, p, h, :],
                                                  xdt[:, p, h * PM:(h + 1) * PM], start=True, stop=True)
                        op.then_inc(sem["yd_ps"], 1)

                    def part_c(r, k, ahead):
                        p = k % 2
                        pe.wait_ge(sem["y_ready"], r + 1)
                        pe.wait_ge(sem["gm_ready"], r + (1 + ahead))
                        for g in range(2):
                            op = nc.tensor.transpose(ps_g[:, P + g * P:P + (g + 1) * P],
                                                     y[:, p, g * P:(g + 1) * P], ident[:, :])
                        op.then_inc(sem["yt_ps"], 1)
                        pe.wait_ge(sem["yt_ready"], r + 1)
                        pe.wait_ge(sem["xrow_ready"], r + (1 + ahead))
                        for g in range(2):
                            op = nc.tensor.matmul(ps_x[:, DI + S:DI + S + C], yt[:, p, g * P:(g + 1) * P], wc[:, g, :],
                                                  start=(g == 0), stop=(g == 1))
                        op.then_inc(sem["out_ps"], 1)

                    def slot(q, k, b):
                        if more_chunks(q):
                            part_a(q + 1, k + 1, b + (k % TB + 1) // TB)
                        part_b(q, k)
                        if k > 0:
                            part_c(q - 1, k + 1, 2 if more_chunks(q) else 1)
                        if more_blocks(b):
                            for g in ((0, 1), (2,), (), ())[k % TB]:
                                project(b + 1, g, (k // TB + 1) % 2)

                    pe.sem_inc(sem["yt_ps"], YT0)
                    for g in range(3):
                        project(0, g, 0)
                    part_a(0, 0, 0)
                    slots(pe, slot)
                    part_c(NT - 1, NT - 1, 0)



E = 8
TOP = 2
HID = 341
GATE_EPS = 1e-9
HID_TILES = [(h0, min(P, HID - h0)) for h0 in range(0, HID, P)]


def propagate_layer(nc, xr, adj, w_row, router_t, w1_t, w3_t, w2_t, out):
    N = out.shape[0]
    NT, NB = N // P, N // BLK
    out_tiles = out.rearrange("(t p) c -> p t c", p=P)
    adj_rows = adj.rearrange("(t p) c -> p t c", p=P)

    keep = ExitStack()
    with keep:
        k = Scope(nc, keep, "gnn")
        hid = k.sb("hid", [P, NT, C])
        ident = k.sb("ident", [P, P])
        eye8 = k.sb("eye8", [P, E])
        rt = k.sb("rt", [C, E])
        wcol = k.sb("wcol", [C, 1])
        w1 = k.sb("w1", [C, E, HID])
        w3 = k.sb("w3", [C, E, HID])
        w2 = k.sb("w2", [P, len(HID_TILES), E, C])

        with ExitStack() as ctx:
            s = Scope(nc, ctx, "gnnprep")
            stats = s.sb("stats", [P, NT, 6])
            mean = s.sb("mean", [P, NT])
            var = s.sb("var", [P, NT])
            tmp = s.sb("tmp", [P, NT])
            root = s.sb("root", [P, NT])
            rstd = s.sb("rstd", [P, NT])
            count8 = s.sb("count8", [P, E], mybir.dt.int32)
            w_in = s.sem("w_in")
            consts = s.sem("consts")
            chain_dve = s.sem("chain_dve")
            stats_done = s.sem("stats_done")
            var_ready = s.sem("var_ready")
            rooted = s.sem("rooted")

            with nc.Block() as block:
                @block.sync
                def _(sp):
                    sp.dma_start(wcol[:, :], w_row.unsqueeze(1)).then_inc(w_in, 16)
                    sp.dma_start(rt[:, :], router_t).then_inc(w_in, 16)
                    sp.dma_start(w1[:, :, :], w1_t).then_inc(w_in, 16)
                    sp.dma_start(w3[:, :, :], w3_t).then_inc(w_in, 16)
                    for i, (h0, hn) in enumerate(HID_TILES):
                        sp.dma_start(w2[0:hn, i, :, :], w2_t[h0:h0 + hn, :, :]).then_inc(w_in, 16)
                    sp.wait_ge(w_in, 16 * (4 + len(HID_TILES)))

                @block.gpsimd
                def _(pool):
                    link = Chain(pool, consts)
                    link(nc.gpsimd.memset(ident[:, :], 0.0))
                    link(nc.gpsimd.affine_select(out=ident[:, :], in_=ident[:, :], compare_op=ALU.not_equal,
                                                 fill=1.0, base=0, pattern=[[-1, P]], channel_multiplier=1))
                    link(nc.gpsimd.iota(count8[:, :], pattern=[[1, E]], base=0, channel_multiplier=0))
                    link(nc.gpsimd.tensor_copy(eye8[:, :], count8[:, :]))

                @block.scalar
                def _(act):
                    act.wait_ge(var_ready, 1)
                    nc.scalar.activation(root[:, :], tmp[:, :], ACT.Sqrt).then_inc(rooted, 1)

                @block.vector
                def _(dve):
                    link = Chain(dve, chain_dve)
                    with dve.Fori(0, NT // UNROLL) as group:
                        for i in range(UNROLL):
                            nc.vector.bn_stats(stats[:, group * UNROLL + i, :],
                                               xr[:, group * UNROLL + i, :]).then_inc(stats_done, 1)
                    dve.wait_ge(stats_done, NT)
                    row_statistics(nc, link, stats, mean[:, :], var[:, :], tmp[:, :])
                    nc.vector.tensor_scalar(tmp[:, :], var[:, :], LN_EPS, None, ALU.add).then_inc(var_ready, 1)
                    dve.wait_ge(rooted, 1)
                    link(nc.vector.reciprocal(rstd[:, :], root[:, :]))
                    with dve.Fori(0, NT // UNROLL) as group:
                        for i in range(UNROLL):
                            t = group * UNROLL + i
                            nc.vector.tensor_scalar(hid[:, t, :], xr[:, t, :], mean[:, bass.ds(t, 1)],
                                                    rstd[:, bass.ds(t, 1)], ALU.subtract, ALU.mult)

        with ExitStack() as ctx:
            s = Scope(nc, ctx, "sweep")
            AR = 4
            T0 = AR * TB
            adjr = s.sb("adjr", [P, AR, TB, BLK])
            adjt = s.sb("adjt", [P, 2, BLK])
            acct = s.sb("acct", [C, BLK])
            xo = s.sb("xo", [P, 2, TB, C])
            xn = s.sb("xn", [P, TB, C])
            xt = s.sb("xt", [C, BLK])
            stats = s.sb("stats", [P, TB, 6])
            mv = s.sb("mv", [P, TB, 2])
            ve = s.sb("ve", [P, TB])
            rstd = s.sb("rstd", [P, TB])
            lg = s.sb("lg", [P, TB, E])
            pr = s.sb("pr", [P, TB, E])
            hot = s.sb("hot", [P, TB, E])
            gate = s.sb("gate", [P, TB, E])
            m4 = s.sb("m4", [P, TB])
            top = s.sb("top", [P, TB, 8])
            topi = s.sb("topi", [P, TB, 8], UINT32)
            topf = s.sb("topf", [P, TB, 8])
            wk = s.sb("wk", [P, TB, TOP])
            th = s.sb("th", [P, 2, BLK])
            pa = s.sb("pa", [P, 2, BLK])
            hh = s.sb("hh", [P, 2, BLK])
            ps_acc = s.ps("acc", [P, BLK])
            ps_h = s.ps("h", [P, 4, BLK])
            ps_m = s.ps("m", [P, BLK])
            ps_y = s.ps("y", [P, 2, BLK])
            adj_in = [s.sem(f"adj_in{u}") for u in range(AR)]
            names = ("t_ps mm_done acct_ready back_ps x3_ready ve_ready rooted xn_ready xt_ps xt_ready "
                     "xo_free router_ps lg_ready exp_done pa_ready h_ps th_ready hh_ready y_ps y_used carried chain_dve").split()
            sem = {n: s.sem(n) for n in names}
            x_out = [s.sem(f"x_out{u}") for u in range(2)]
            adjt_ready = [s.sem(f"adjt_ready{u}") for u in range(2)]
            NU = E * len(HID_TILES)
            NCH = NT // TB
            HH0 = 1
            AHEAD = 2

            def blocks(engine, one_block):
                with engine.Fori(0, NB // 2 - 1) as pair:
                    for v in range(2):
                        one_block(pair * 2 + v, v, True)
                for v in range(2):
                    one_block(NB - 2 + v, v, v == 0)

            with nc.Block() as block:
                @block.sync
                def _(sp):
                    with sp.Fori(0, NB // 2) as pair:
                        for v in range(2):
                            ib = pair * 2 + v
                            with sp.Fori(0, NCH // AR) as cp:
                                for u in range(AR):
                                    sp.wait_ge(sem["t_ps"], ib * NT + (cp * AR + u + 1) * TB)
                                    sp.dma_start(adjr[:, u, :, :],
                                                 adj_rows[:, bass.ds(ib * TB, TB), bass.ds((cp * AR + u) * BLK, BLK)]
                                                 ).then_inc(adj_in[u], 16)

                @block.gpsimd
                def _(pool):
                    pool.sem_inc(sem["xo_free"], 2)
                    with pool.Fori(0, NB // 2) as pair:
                        for v in range(2):
                            ib = pair * 2 + v
                            pool.wait_ge(sem["y_used"], (ib + 1) * E)
                            pool.dma_start(out_tiles[:, bass.ds(ib * TB, TB), :], xo[:, v, :, :]).then_inc(x_out[v], 16)
                            pool.wait_ge(x_out[v], pair * 16 + 16)
                            pool.sem_inc(sem["xo_free"], 1)

                @block.scalar
                def _(act):
                    def copy_tiles(ib, first, end):
                        for j in range(first + 1, end, 2):
                            act.wait_ge(sem["t_ps"], ib * NT + (j + 1 + T0))
                            nc.scalar.activation(adjt[:, 1, :], ps_h[:, 1, :], ACT.Copy).then_inc(adjt_ready[1], 1)

                    def one_block(ib, v, more):
                        copy_tiles(ib, AHEAD, NT)
                        act.wait_ge(sem["mm_done"], (ib + 1) * NT)
                        nc.scalar.activation(acct[:, :], ps_acc[:, :], ACT.Copy,
                                             scale=wcol[:, 0:1]).then_inc(sem["acct_ready"], 1)
                        if more:
                            copy_tiles(ib + 1, 0, AHEAD)
                        act.wait_ge(sem["ve_ready"], ib + 1)
                        nc.scalar.activation(ve[:, :], ve[:, :], ACT.Sqrt).then_inc(sem["rooted"], 1)
                        act.wait_ge(sem["xt_ps"], ib + 1)
                        nc.scalar.activation(xt[:, :], ps_m[:, :], ACT.Copy).then_inc(sem["xt_ready"], 1)
                        for n in range(NU):
                            h0, hn = HID_TILES[n % len(HID_TILES)]
                            act.wait_ge(sem["h_ps"], ib * NU + (n + 1))
                            nc.scalar.activation(th[0:hn, n % 2, :], ps_h[0:hn, 2 * (n % 2), :], ACT.Tanh,
                                                 scale=0.5).then_inc(sem["th_ready"], 1)
                            if n == 1:
                                act.wait_ge(sem["lg_ready"], ib + 1)
                                nc.scalar.activation(pr[:, :, :], lg[:, :, :], ACT.Exp).then_inc(sem["exp_done"], 1)

                    copy_tiles(0, 0, AHEAD)
                    blocks(act, one_block)

                @block.vector
                def _(dve):
                    per_block = 27

                    def carry():
                        dve.sem_inc(sem["carried"], 1)

                    def copy_tiles(ib, first, end):
                        for j in range(first, end, 2):
                            dve.wait_ge(sem["t_ps"], ib * NT + (j + 1 + T0))
                            nc.vector.tensor_copy(adjt[:, 0, :], ps_h[:, 0, :]).then_inc(adjt_ready[0], 1)

                    def one_block(ib, v, more):
                        link = Chain(dve, sem["chain_dve"], ib * per_block)
                        copy_tiles(ib, AHEAD + 2, NT)
                        x3 = xo[:, v, :, :]
                        dve.wait_ge(sem["xo_free"], ib + 1)
                        dve.wait_ge(sem["back_ps"], ib + 1)
                        nc.vector.tensor_tensor(x3, xr[:, bass.ds(ib * TB, TB), :],
                                                ps_m[:, :].rearrange("p (t c) -> p t c", t=TB),
                                                ALU.add).then_inc(sem["x3_ready"], 1)
                        dve.wait_ge(sem["x3_ready"], ib + 1)
                        for i in range(TB):
                            op = nc.vector.bn_stats(stats[:, i, :], x3[:, i, :])
                        link(op)
                        if more:
                            copy_tiles(ib + 1, 0, AHEAD)
                        carry()
                        for i in range(TB):
                            op = nc.vector.bn_aggr(mv[:, i, :], stats[:, i, :])
                        link(op)
                        nc.vector.tensor_scalar(ve[:, :], mv[:, :, 1], LN_EPS, None, ALU.add).then_inc(sem["ve_ready"], 1)
                        dve.wait_ge(sem["rooted"], ib + 1)
                        link(nc.vector.reciprocal(rstd[:, :], ve[:, :]))
                        for i in range(TB):
                            op = nc.vector.tensor_scalar(xn[:, i, :], x3[:, i, :], mv[:, i, 0:1], rstd[:, i:i + 1],
                                                         ALU.subtract, ALU.mult)
                        op.then_inc(sem["xn_ready"], 1)
                        def take_logits():
                            dve.wait_ge(sem["router_ps"], ib + 1)
                            link(nc.vector.tensor_scalar(lg[:, :, :], ps_m[:, 0:TB * E].rearrange("p (t e) -> p t e", e=E),
                                                         1.0, None, ALU.mult))
                            link(nc.vector.tensor_reduce(m4[:, :], lg[:, :, :], AX.X, ALU.max))
                            nc.vector.tensor_tensor(lg[:, :, :], lg[:, :, :], m4[:, :].unsqueeze(2).to_broadcast([P, TB, E]),
                                                    ALU.subtract).then_inc(sem["lg_ready"], 1)

                        def normalize():
                            dve.wait_ge(sem["exp_done"], ib + 1)
                            link(nc.vector.tensor_reduce(m4[:, :], pr[:, :, :], AX.X, ALU.add))
                            link(nc.vector.reciprocal(m4[:, :], m4[:, :]))
                            link(nc.vector.tensor_tensor(pr[:, :, :], pr[:, :, :], m4[:, :].unsqueeze(2).to_broadcast([P, TB, E]),
                                                         ALU.mult))

                        def choose():
                            for i in range(TB):
                                carry()
                                link(nc.vector.max(top[:, i, :], pr[:, i, :]))
                                carry()
                                link(nc.vector.max_index(topi[:, i, :], top[:, i, :], pr[:, i, :]))

                        def make_gates():
                            link(nc.vector.tensor_copy(topf[:, :, :], topi[:, :, :]))
                            link(nc.vector.tensor_tensor(m4[:, :], top[:, :, 0], top[:, :, 1], ALU.add))
                            link(nc.vector.tensor_scalar(m4[:, :], m4[:, :], GATE_EPS, None, ALU.add))
                            link(nc.vector.reciprocal(m4[:, :], m4[:, :]))
                            link(nc.vector.tensor_scalar(m4[:, :], m4[:, :], 0.5, None, ALU.mult))
                            link(nc.vector.tensor_tensor(wk[:, :, :], top[:, :, 0:TOP],
                                                         m4[:, :].unsqueeze(2).to_broadcast([P, TB, TOP]), ALU.mult))
                            places = eye8[:, :].unsqueeze(1).to_broadcast([P, TB, E])
                            for r, to in enumerate((gate, hot)):
                                link(nc.vector.tensor_tensor(to[:, :, :], places,
                                                             topf[:, :, r:r + 1].to_broadcast([P, TB, E]), ALU.is_equal))
                                link(nc.vector.tensor_tensor(to[:, :, :], to[:, :, :],
                                                             wk[:, :, r:r + 1].to_broadcast([P, TB, E]), ALU.mult))
                            link(nc.vector.tensor_tensor(gate[:, :, :], gate[:, :, :], hot[:, :, :], ALU.add))

                        def add_expert(e):
                            dve.wait_ge(sem["y_ps"], ib * E + (e + 1))
                            if e > 0:
                                dve.wait_ge(sem["y_used"], ib * E + e)
                            for i in range(TB):
                                op = nc.vector.scalar_tensor_tensor(
                                    out=x3[:, i, :], in0=ps_y[:, e % 2, i * C:(i + 1) * C],
                                    scalar=gate[:, i, e:e + 1], in1=x3[:, i, :], op0=ALU.mult, op1=ALU.add)
                            op.then_inc(sem["y_used"], 1)

                        for n in range(NU):
                            h0, hn = HID_TILES[n % len(HID_TILES)]
                            dve.wait_ge(sem["th_ready"], ib * NU + (n + 1))
                            dve.wait_ge(sem["hh_ready"], ib * NU + (n + HH0))
                            nc.vector.scalar_tensor_tensor(out=pa[0:hn, n % 2, :], in0=th[0:hn, n % 2, :], scalar=1.0,
                                                           in1=ps_h[0:hn, 2 * (n % 2), :], op0=ALU.add,
                                                           op1=ALU.mult).then_inc(sem["pa_ready"], 1)
                            dve.wait_ge(sem["pa_ready"], ib * NU + (n + 1))
                            nc.vector.tensor_tensor(hh[0:hn, n % 2, :], pa[0:hn, n % 2, :],
                                                    ps_h[0:hn, 2 * (n % 2) + 1, :], ALU.mult).then_inc(sem["hh_ready"], 1)
                            if 1 <= n <= 4:
                                (take_logits, normalize, choose, make_gates)[n - 1]()
                            if n == 5:
                                add_expert(0)
                            if n >= 7 and (n - 4) % 3 == 0:
                                add_expert((n - 4) // 3)
                        if more:
                            copy_tiles(ib + 1, AHEAD, AHEAD + 1)
                        add_expert(E - 1)
                        assert link.ops == per_block, link.ops

                    dve.sem_inc(sem["hh_ready"], HH0)
                    copy_tiles(0, 0, AHEAD + 1)
                    blocks(dve, one_block)

                @block.tensor
                def _(pe):
                    pe.sem_inc(sem["t_ps"], T0)
                    def transposes(ib, j):
                        u = (j // TB) % AR
                        if j % TB == 0:
                            pe.wait_ge(adj_in[u], ib * (NCH // AR * 16) + 16 * (j // (AR * TB) + 1))
                        if j >= 2:
                            pe.wait_ge(adjt_ready[j % 2], ib * (NT // 2) + j // 2)
                        for i in range(TB):
                            op = nc.tensor.transpose(ps_h[:, j % 2, i * P:(i + 1) * P],
                                                     adjr[:, u, i, (j % TB) * P:(j % TB + 1) * P], ident[:, :])
                        op.then_inc(sem["t_ps"], 1)

                    def sweep(ib, first, end):
                        if first == 0:
                            transposes(ib, first)
                        for j in range(first, end):
                            if j + 1 < end:
                                transposes(ib, j + 1)
                            pe.wait_ge(adjt_ready[j % 2], ib * (NT // 2) + (j // 2 + 1))
                            nc.tensor.matmul(ps_acc[:, :], hid[:, j, :], adjt[:, j % 2, :], start=(j == 0),
                                             stop=(j == NT - 1)).then_inc(sem["mm_done"], 1)

                    def one_block(ib, v, more):

                        sweep(ib, AHEAD, NT)
                        pe.wait_ge(sem["acct_ready"], ib + 1)
                        for i in range(TB):
                            op = nc.tensor.transpose(ps_m[:, i * C:(i + 1) * C], acct[:, i * P:(i + 1) * P], ident[:, :])
                        op.then_inc(sem["back_ps"], 1)
                        if more:
                            sweep(ib + 1, 0, AHEAD)
                        pe.wait_ge(sem["xn_ready"], ib + 1)
                        for i in range(TB):
                            op = nc.tensor.transpose(ps_m[:, i * P:(i + 1) * P], xn[:, i, :], ident[:, :])
                        op.then_inc(sem["xt_ps"], 1)
                        pe.wait_ge(sem["xt_ready"], ib + 1)
                        for i in range(TB):
                            op = nc.tensor.matmul(ps_m[:, i * E:(i + 1) * E], xt[:, i * P:(i + 1) * P], rt[:, :],
                                                  start=True, stop=True)
                        op.then_inc(sem["router_ps"], 1)

                        def hidden(n):
                            e, (h0, hn) = n // len(HID_TILES), HID_TILES[n % len(HID_TILES)]
                            if n >= 2:
                                pe.wait_ge(sem["hh_ready"], ib * NU + (n - 1 + HH0))
                            nc.tensor.matmul(ps_h[0:hn, 2 * (n % 2), :], w1[:, e, h0:h0 + hn], xt[:, :],
                                             start=True, stop=True)
                            nc.tensor.matmul(ps_h[0:hn, 2 * (n % 2) + 1, :], w3[:, e, h0:h0 + hn], xt[:, :],
                                             start=True, stop=True).then_inc(sem["h_ps"], 1)

                        hidden(0)
                        for n in range(NU):
                            if n + 1 < NU:
                                hidden(n + 1)
                            elif more:
                                transposes(ib + 1, AHEAD)
                            e, t = n // len(HID_TILES), n % len(HID_TILES)
                            hn = HID_TILES[t][1]
                            if t == 0 and e >= 2:
                                pe.wait_ge(sem["y_used"], ib * E + (e - 1))
                            pe.wait_ge(sem["hh_ready"], ib * NU + (n + 1 + HH0))
                            for i in range(TB):
                                op = nc.tensor.matmul(ps_y[:, e % 2, i * C:(i + 1) * C],
                                                      hh[0:hn, n % 2, i * P:(i + 1) * P], w2[0:hn, t, e, :],
                                                      start=(t == 0 and i == 0), stop=(t == len(HID_TILES) - 1),
                                                      skip_group_check=True)
                            if t == len(HID_TILES) - 1:
                                op.then_inc(sem["y_ps"], 1)

                    sweep(0, 0, AHEAD)
                    transposes(0, AHEAD)
                    blocks(pe, one_block)


def build(nc, ins, out):
    N = ins["x"].shape[0]
    left_t = nc.dram_tensor("left_t", (H, N), FP32).ap()
    values_d = nc.dram_tensor("values_d", (H, P, N // P, 2 * 3 * DV), BF16).ap()
    sums_d = nc.dram_tensor("sums_d", (N // P, P, H * DV), FP32).ap()
    attention_layer(nc, ins["x"], ins["adj"], ins["W"], ins["W_T"], ins["a_l"], ins["a_r"], left_t, values_d, sums_d)
    with ExitStack() as ctx:
        xr = Scope(nc, ctx, "rows").sb("xr", [P, N // P, C])
        mamba_layer(nc, ins["x"], sums_d, ins["bias"], ins["w_zdt"], ins["w_xbc"], ins["conv_w"], ins["conv_b"],
                    ins["dt_bias"], ins["a_log"], ins["d_skip"], ins["norm_w"], ins["w_out_t"], ins["w_lin"],
                    ins["b_lin"], xr)
        propagate_layer(nc, xr, ins["adj"], ins["w_row"], ins["router_t"], ins["w1_t"], ins["w3_t"], ins["w2_t"],
                        out)


def kernel(**inputs):
    import numpy as _np
    import concourse.bacc as _bacc
    from concourse import mybir as _mybir
    from concourse.bass_utils import run_bass_kernel_spmd as _run

    nc = _bacc.Bacc("TRN2", target_bir_lowering=False, num_devices=1)
    w_in = _np.asarray(inputs["L0_ffn_W_in"])
    inner, conv_dim = DI, DI + 2 * S
    laid = {
        "x": inputs["x"], "adj": inputs["adj"], "W": inputs["L0_gnn_W"], "W_T": _np.asarray(inputs["L0_gnn_W"]).T,
        "a_l": inputs["L0_gnn_a_l"], "a_r": inputs["L0_gnn_a_r"], "bias": inputs["L0_gnn_bias"],
        "w_zdt": _np.concatenate([w_in[:, :inner], w_in[:, inner + conv_dim:]], axis=1),
        "w_xbc": w_in[:, inner:inner + conv_dim],
        "conv_w": inputs["L0_ffn_conv_w"], "conv_b": _np.asarray(inputs["L0_ffn_conv_b"]).reshape(-1, P).T, "dt_bias": inputs["L0_ffn_dt_bias"],
        "a_log": inputs["L0_ffn_A_log"], "d_skip": inputs["L0_ffn_D"], "norm_w": _np.asarray(inputs["L0_ffn_norm_w"]).reshape(-1, P).T,
        "w_out_t": _np.asarray(inputs["L0_ffn_W_out"]).T, "w_lin": inputs["L0_ffn_W_lin"],
        "b_lin": inputs["L0_ffn_b_lin"], "w_row": inputs["L1_gnn_W"],
        "router_t": _np.asarray(inputs["L1_ffn_router_w"]).T,
        "w1_t": _np.asarray(inputs["L1_ffn_w1"]).transpose(2, 0, 1),
        "w3_t": _np.asarray(inputs["L1_ffn_w3"]).transpose(2, 0, 1),
        "w2_t": _np.asarray(inputs["L1_ffn_w2"]).transpose(2, 0, 1),
    }
    arrays, ins = {}, {}
    for name, value in laid.items():
        a = _np.ascontiguousarray(value)
        arrays[f"in_{name}_dram"] = a
        ins[name] = nc.dram_tensor(f"in_{name}_dram", a.shape, _mybir.dt.from_np(a.dtype), kind="ExternalInput").ap()
    out = nc.dram_tensor("out_0_dram", laid["x"].shape, FP32, kind="ExternalOutput").ap()
    build(nc, ins, out)
    r = _run(nc, [arrays], core_ids=[0])
    return r.results[0]["out_0_dram"]
```
